# Optimizing a Trainium2 kernel written in Bass

```python
import numpy as np
import jax
import jax.numpy as jnp

def _softmax(x, axis=-1):
    return jax.nn.softmax(x, axis=axis)

def _gelu(x):
    return jax.nn.gelu(x, approximate=True)

def _silu(x):
    return jax.nn.silu(x)

def _sigmoid(x):
    return jax.nn.sigmoid(x)

def _layernorm(x, axis=-1, eps=1e-05):
    m = jnp.mean(x, axis=axis, keepdims=True)
    v = jnp.var(x, axis=axis, keepdims=True)
    return (x - m) / jnp.sqrt(v + eps)

def _scatter_add(tgt, idx, src, axis=0):
    return tgt.at[idx].add(src)

def _segment_sum(src, seg, n):
    return jax.ops.segment_sum(src, seg, n)
kernel_name = 'mk_xattn_ffn_d2_seqx_r8_5d9e6b'

def setup_inputs(seed: int=0):
    np.random.seed(seed)
    _w = jnp.asarray

    def _rec_inputs():
        import jax
        import jax.numpy as jnp
        _rk = jax.random.key(seed)
        x = -0.0003929 + 0.9999 * jax.random.normal(jax.random.fold_in(_rk, 1), (2, 256, 256), jnp.float32)
        _lenS = 256 - jax.random.randint(jax.random.fold_in(_rk, 7), (2,), 0, max(1, 256 // 4) + 1, jnp.int32)
        _lenS2 = 512 - jax.random.randint(jax.random.fold_in(_rk, 8), (2,), 0, max(1, 512 // 4) + 1, jnp.int32)
        _ctx_2048P = jax.random.normal(jax.random.fold_in(_rk, 11), (2, 16, 256), jnp.float32)
        _ctx_2048c = jax.random.dirichlet(jax.random.fold_in(_rk, 511), 0.3 * jnp.ones((16,), jnp.float32), (2, 512))
        _ctx_2048t = jnp.einsum('bsk,bkd->bsd', _ctx_2048c, _ctx_2048P)
        _ctx_2048t = _ctx_2048t * jax.lax.rsqrt(jnp.mean(jnp.square(_ctx_2048t)) + 1e-12) * 0.953939
        ctx_2048 = -1.39393e-06 + 0.999914 * (_ctx_2048t + 0.3 * jax.random.normal(jax.random.fold_in(_rk, 611), (2, 512, 256), jnp.float32))
        itok_BxS_0_1023 = jax.random.randint(jax.random.fold_in(_rk, 12), (2, 256), 0, 128, jnp.int32)
        return (x, ctx_2048, itok_BxS_0_1023)
    x, ctx_2048, itok_BxS_0_1023 = _rec_inputs()

    def _L0_xattn_setup():
        import jax, jax.numpy as jnp
        import numpy as np
        B, Lq, Lk = (2, 512, 128)
        Q_DIM, KV_DIM = (256, 256)
        H, HD = (16, 128)
        KVC, QC, R = (64, 96, 64)
        LOOKBACK = 8
        NEG = -1e+30

        def _rope(x, L):
            half = x.shape[-1] // 2
            inv_freq = 1.0 / 10000.0 ** (jnp.arange(half, dtype=jnp.float32) / half)
            ang = jnp.arange(L, dtype=jnp.float32)[:, None] * inv_freq
            cos, sin = (jnp.cos(ang), jnp.sin(ang))
            x1, x2 = (x[..., :half], x[..., half:])
            return jnp.concatenate([x1 * cos - x2 * sin, x1 * sin + x2 * cos], axis=-1)
        key = jax.random.key(seed)
        ks = jax.random.split(key, 11)

        def w(k, shape, fan_in):
            return jax.random.normal(k, shape, jnp.float32) / np.sqrt(fan_in).astype(np.float32)
        return {'q': jax.random.normal(ks[0], (B, Lq, Q_DIM), jnp.float32), 'kv': jax.random.normal(ks[1], (B, Lk, KV_DIM), jnp.float32), 'seg_id': jnp.sort(jax.random.randint(ks[2], (B, Lq), 0, Lk), axis=-1), 'W_kvc': w(ks[3], (KV_DIM, KVC), KV_DIM), 'W_dq': w(ks[4], (Q_DIM, QC), Q_DIM), 'W_uq': w(ks[5], (QC, H * HD), QC), 'W_qr': w(ks[6], (QC, H * R), QC), 'W_uk': w(ks[7], (KVC, H * HD), KVC), 'W_kr': w(ks[8], (KVC, R), KVC), 'W_uv': w(ks[9], (KVC, H * HD), KVC), 'W_o': w(ks[10], (H * HD, Q_DIM), H * HD)}
    _L0_xattn_all = _L0_xattn_setup()
    _L0_xattn_in = {k: v for k, v in _L0_xattn_all.items() if k in ('W_kvc', 'W_dq', 'W_uq', 'W_qr', 'W_uk', 'W_kr', 'W_uv', 'W_o')}
    del _L0_xattn_all

    def _L0_ffn_setup():
        import jax, jax.numpy as jnp
        import numpy as np
        BLOCK_SIZE = 32
        HIDDEN_SIZE = 256
        MLP_DIM = 2048
        NVFP4_LUT = jnp.array([0.0, 0.5, 1.0, 1.5, 2.0, 3.0, 4.0, 6.0, 0.0, -0.5, -1.0, -1.5, -2.0, -3.0, -4.0, -6.0], dtype=jnp.float32)

        def dequant_nvfp4(W_packed, scales, block=BLOCK_SIZE):
            N = W_packed.shape[0]
            low = W_packed & 15
            high = W_packed >> 4 & 15
            idx = jnp.stack([low, high], axis=-1).reshape(N, -1)
            vals = NVFP4_LUT[idx]
            K = vals.shape[1]
            vals = vals.reshape(N, K // block, block) * scales[:, :, None]
            return vals.reshape(N, K)
        key = jax.random.key(seed)
        ks = jax.random.split(key, 7)
        x = jax.random.normal(ks[0], (4, 32, HIDDEN_SIZE), dtype=jnp.float32)
        gate_W_packed = jax.random.randint(ks[1], (MLP_DIM, HIDDEN_SIZE // 2), 0, 32, dtype=jnp.int32)
        gate_scales = jax.random.uniform(ks[2], (MLP_DIM, HIDDEN_SIZE // BLOCK_SIZE), dtype=jnp.float32) * 0.1 + 0.001
        up_W_packed = jax.random.randint(ks[3], (MLP_DIM, HIDDEN_SIZE // 2), 0, 32, dtype=jnp.int32)
        up_scales = jax.random.uniform(ks[4], (MLP_DIM, HIDDEN_SIZE // BLOCK_SIZE), dtype=jnp.float32) * 0.1 + 0.001
        down_W_packed = jax.random.randint(ks[5], (HIDDEN_SIZE, MLP_DIM // 2), 0, 32, dtype=jnp.int32)
        down_scales = jax.random.uniform(ks[6], (HIDDEN_SIZE, MLP_DIM // BLOCK_SIZE), dtype=jnp.float32) * 0.1 + 0.001
        return {'x': x, 'gate_W_packed': gate_W_packed, 'gate_scales': gate_scales, 'up_W_packed': up_W_packed, 'up_scales': up_scales, 'down_W_packed': down_W_packed, 'down_scales': down_scales}
    _L0_ffn_all = _L0_ffn_setup()
    _L0_ffn_in = {k: v for k, v in _L0_ffn_all.items() if k in ('gate_W_packed', 'gate_scales', 'up_W_packed', 'up_scales', 'down_W_packed', 'down_scales')}
    del _L0_ffn_all

    def _L1_xattn_setup():
        import jax, jax.numpy as jnp
        import numpy as np
        DIM = 256
        H = 16
        D = 128
        INNER = H * D
        N_IMG = 257
        EPS = 1e-06

        def rms_norm(x, scale, eps=EPS):
            ms = jnp.mean(jnp.square(x), axis=-1, keepdims=True)
            return x * jax.lax.rsqrt(ms + eps) * scale

        def sdpa(q, k, v):
            scale = 1.0 / jnp.sqrt(jnp.asarray(D, q.dtype))
            scores = jnp.einsum('bshd,blhd->bhsl', q, k) * scale
            attn = jax.nn.softmax(scores, axis=-1)
            return jnp.einsum('bhsl,blhd->bshd', attn, v)
        key = jax.random.key(seed)
        ks = jax.random.split(key, 16)
        std = 1.0 / np.sqrt(DIM)
        inp = {'x': jax.random.normal(ks[0], (2, 512, DIM), jnp.float32), 'context': jax.random.normal(ks[1], (2, 769, DIM), jnp.float32), 'q_w': jax.random.normal(ks[2], (DIM, INNER), jnp.float32) * std, 'q_b': jnp.zeros((INNER,), jnp.float32), 'k_w': jax.random.normal(ks[3], (DIM, INNER), jnp.float32) * std, 'k_b': jnp.zeros((INNER,), jnp.float32), 'v_w': jax.random.normal(ks[4], (DIM, INNER), jnp.float32) * std, 'v_b': jnp.zeros((INNER,), jnp.float32), 'ki_w': jax.random.normal(ks[5], (DIM, INNER), jnp.float32) * std, 'ki_b': jnp.zeros((INNER,), jnp.float32), 'vi_w': jax.random.normal(ks[6], (DIM, INNER), jnp.float32) * std, 'vi_b': jnp.zeros((INNER,), jnp.float32), 'o_w': jax.random.normal(ks[7], (INNER, DIM), jnp.float32) * std, 'o_b': jnp.zeros((DIM,), jnp.float32), 'nq_s': jnp.ones((INNER,), jnp.float32), 'nkt_s': jnp.ones((INNER,), jnp.float32), 'nki_s': jnp.ones((INNER,), jnp.float32)}
        return inp
    _L1_xattn_all = _L1_xattn_setup()
    _L1_xattn_in = {k: v for k, v in _L1_xattn_all.items() if k in ('q_w', 'q_b', 'k_w', 'k_b', 'v_w', 'v_b', 'ki_w', 'ki_b', 'vi_w', 'vi_b', 'o_w', 'o_b', 'nq_s', 'nkt_s', 'nki_s')}
    del _L1_xattn_all

    def _L1_ffn_setup():
        import jax, jax.numpy as jnp
        import numpy as np
        B, S, H = (2, 256, 256)
        E, K = (16, 4)
        I_MOE, I_SH = (176, 704)
        key = jax.random.key(seed)
        ks = jax.random.split(key, 9)

        def w(k, shape, fan_in):
            return jax.random.normal(k, shape, jnp.float32) * fan_in ** (-0.5)
        return {'hidden_states': jax.random.normal(ks[0], (B, S, H), jnp.float32), 'router_w': w(ks[1], (E, H), H), 'w_gate': w(ks[2], (E, H, I_MOE), H), 'w_up': w(ks[3], (E, H, I_MOE), H), 'w_down': w(ks[4], (E, I_MOE, H), I_MOE), 'sh_gate': w(ks[5], (H, I_SH), H), 'sh_up': w(ks[6], (H, I_SH), H), 'sh_down': w(ks[7], (I_SH, H), I_SH), 'sh_gate_w': w(ks[8], (H, 1), H)}
    _L1_ffn_all = _L1_ffn_setup()
    _L1_ffn_in = {k: v for k, v in _L1_ffn_all.items() if k in ('router_w', 'w_gate', 'w_up', 'w_down', 'sh_gate', 'sh_up', 'sh_down', 'sh_gate_w')}
    del _L1_ffn_all
    return {'x': x, 'ctx_2048': ctx_2048, 'itok_BxS_0_1023': itok_BxS_0_1023, 'L0_xattn_W_kvc': _L0_xattn_in['W_kvc'], 'L0_xattn_W_dq': _L0_xattn_in['W_dq'], 'L0_xattn_W_uq': _L0_xattn_in['W_uq'], 'L0_xattn_W_qr': _L0_xattn_in['W_qr'], 'L0_xattn_W_uk': _L0_xattn_in['W_uk'], 'L0_xattn_W_kr': _L0_xattn_in['W_kr'], 'L0_xattn_W_uv': _L0_xattn_in['W_uv'], 'L0_xattn_W_o': _L0_xattn_in['W_o'], 'L0_ffn_gate_W_packed': _L0_ffn_in['gate_W_packed'], 'L0_ffn_gate_scales': _L0_ffn_in['gate_scales'], 'L0_ffn_up_W_packed': _L0_ffn_in['up_W_packed'], 'L0_ffn_up_scales': _L0_ffn_in['up_scales'], 'L0_ffn_down_W_packed': _L0_ffn_in['down_W_packed'], 'L0_ffn_down_scales': _L0_ffn_in['down_scales'], 'L1_xattn_q_w': _L1_xattn_in['q_w'], 'L1_xattn_q_b': _L1_xattn_in['q_b'], 'L1_xattn_k_w': _L1_xattn_in['k_w'], 'L1_xattn_k_b': _L1_xattn_in['k_b'], 'L1_xattn_v_w': _L1_xattn_in['v_w'], 'L1_xattn_v_b': _L1_xattn_in['v_b'], 'L1_xattn_ki_w': _L1_xattn_in['ki_w'], 'L1_xattn_ki_b': _L1_xattn_in['ki_b'], 'L1_xattn_vi_w': _L1_xattn_in['vi_w'], 'L1_xattn_vi_b': _L1_xattn_in['vi_b'], 'L1_xattn_o_w': _L1_xattn_in['o_w'], 'L1_xattn_o_b': _L1_xattn_in['o_b'], 'L1_xattn_nq_s': _L1_xattn_in['nq_s'], 'L1_xattn_nkt_s': _L1_xattn_in['nkt_s'], 'L1_xattn_nki_s': _L1_xattn_in['nki_s'], 'L1_ffn_router_w': _L1_ffn_in['router_w'], 'L1_ffn_w_gate': _L1_ffn_in['w_gate'], 'L1_ffn_w_up': _L1_ffn_in['w_up'], 'L1_ffn_w_down': _L1_ffn_in['w_down'], 'L1_ffn_sh_gate': _L1_ffn_in['sh_gate'], 'L1_ffn_sh_up': _L1_ffn_in['sh_up'], 'L1_ffn_sh_down': _L1_ffn_in['sh_down'], 'L1_ffn_sh_gate_w': _L1_ffn_in['sh_gate_w']}

def reference(x, ctx_2048, itok_BxS_0_1023, L0_xattn_W_kvc, L0_xattn_W_dq, L0_xattn_W_uq, L0_xattn_W_qr, L0_xattn_W_uk, L0_xattn_W_kr, L0_xattn_W_uv, L0_xattn_W_o, L0_ffn_gate_W_packed, L0_ffn_gate_scales, L0_ffn_up_W_packed, L0_ffn_up_scales, L0_ffn_down_W_packed, L0_ffn_down_scales, L1_xattn_q_w, L1_xattn_q_b, L1_xattn_k_w, L1_xattn_k_b, L1_xattn_v_w, L1_xattn_v_b, L1_xattn_ki_w, L1_xattn_ki_b, L1_xattn_vi_w, L1_xattn_vi_b, L1_xattn_o_w, L1_xattn_o_b, L1_xattn_nq_s, L1_xattn_nkt_s, L1_xattn_nki_s, L1_ffn_router_w, L1_ffn_w_gate, L1_ffn_w_up, L1_ffn_w_down, L1_ffn_sh_gate, L1_ffn_sh_up, L1_ffn_sh_down, L1_ffn_sh_gate_w):
    import jax
    import jax.numpy as jnp

    def _L0_xattn_ref(q, kv, seg_id, W_kvc, W_dq, W_uq, W_qr, W_uk, W_kr, W_uv, W_o):
        import jax, jax.numpy as jnp
        import numpy as np
        B, Lq, Lk = (2, 512, 128)
        Q_DIM, KV_DIM = (256, 256)
        H, HD = (16, 128)
        KVC, QC, R = (64, 96, 64)
        LOOKBACK = 8
        NEG = -1e+30

        def _rope(x, L):
            half = x.shape[-1] // 2
            inv_freq = 1.0 / 10000.0 ** (jnp.arange(half, dtype=jnp.float32) / half)
            ang = jnp.arange(L, dtype=jnp.float32)[:, None] * inv_freq
            cos, sin = (jnp.cos(ang), jnp.sin(ang))
            x1, x2 = (x[..., :half], x[..., half:])
            return jnp.concatenate([x1 * cos - x2 * sin, x1 * sin + x2 * cos], axis=-1)
        b, lq, _ = q.shape
        lk = kv.shape[1]
        kv_c = kv @ W_kvc
        q_c = q @ W_dq
        q_nope = (q_c @ W_uq).reshape(b, lq, H, HD).transpose(0, 2, 1, 3)
        q_rope = (q_c @ W_qr).reshape(b, lq, H, R).transpose(0, 2, 1, 3)
        k_nope = (kv_c @ W_uk).reshape(b, lk, H, HD)
        v = (kv_c @ W_uv).reshape(b, lk, H, HD)
        k_rope = kv_c @ W_kr
        q_rope = _rope(q_rope, lq)
        k_rope = _rope(k_rope, lk)
        scale = 1.0 / np.sqrt(HD + R).astype(np.float32)
        scores = (jnp.einsum('bhqd,bkhd->bhqk', q_nope, k_nope) + jnp.einsum('bhqr,bkr->bhqk', q_rope, k_rope)) * scale
        k_ids = jnp.arange(lk)[None, None, :]
        qs = seg_id[:, :, None]
        good = (k_ids <= qs) & (k_ids >= qs - LOOKBACK)
        scores = jnp.where(good[:, None, :, :], scores, NEG)
        attn = jax.nn.softmax(scores, axis=-1)
        out = jnp.einsum('bhqk,bkhd->bqhd', attn, v).reshape(b, lq, H * HD)
        return out @ W_o

    def _L0_ffn_ref(x, gate_W_packed, gate_scales, up_W_packed, up_scales, down_W_packed, down_scales):
        import jax, jax.numpy as jnp
        import numpy as np
        BLOCK_SIZE = 32
        HIDDEN_SIZE = 256
        MLP_DIM = 2048
        NVFP4_LUT = jnp.array([0.0, 0.5, 1.0, 1.5, 2.0, 3.0, 4.0, 6.0, 0.0, -0.5, -1.0, -1.5, -2.0, -3.0, -4.0, -6.0], dtype=jnp.float32)

        def dequant_nvfp4(W_packed, scales, block=BLOCK_SIZE):
            N = W_packed.shape[0]
            low = W_packed & 15
            high = W_packed >> 4 & 15
            idx = jnp.stack([low, high], axis=-1).reshape(N, -1)
            vals = NVFP4_LUT[idx]
            K = vals.shape[1]
            vals = vals.reshape(N, K // block, block) * scales[:, :, None]
            return vals.reshape(N, K)
        B, S, H = x.shape
        xt = x.reshape(B * S, H)
        Wg = dequant_nvfp4(gate_W_packed, gate_scales)
        Wu = dequant_nvfp4(up_W_packed, up_scales)
        Wd = dequant_nvfp4(down_W_packed, down_scales)
        gate = jnp.einsum('th,nh->tn', xt, Wg)
        up = jnp.einsum('th,nh->tn', xt, Wu)
        gelu = jnp.tanh(0.7978845608028654 * (gate + 0.044715 * gate ** 3)) * gate * 0.5 + gate * 0.5
        inter = gelu * up
        out = jnp.einsum('tn,hn->th', inter, Wd)
        return out.reshape(B, S, H)

    def _L1_xattn_ref(x, context, q_w, q_b, k_w, k_b, v_w, v_b, ki_w, ki_b, vi_w, vi_b, o_w, o_b, nq_s, nkt_s, nki_s):
        import jax, jax.numpy as jnp
        import numpy as np
        DIM = 256
        H = 16
        D = 128
        INNER = H * D
        N_IMG = 257
        EPS = 1e-06

        def rms_norm(x, scale, eps=EPS):
            ms = jnp.mean(jnp.square(x), axis=-1, keepdims=True)
            return x * jax.lax.rsqrt(ms + eps) * scale

        def sdpa(q, k, v):
            scale = 1.0 / jnp.sqrt(jnp.asarray(D, q.dtype))
            scores = jnp.einsum('bshd,blhd->bhsl', q, k) * scale
            attn = jax.nn.softmax(scores, axis=-1)
            return jnp.einsum('bhsl,blhd->bshd', attn, v)
        B, S, _ = x.shape
        img_ctx = context[:, :N_IMG]
        txt_ctx = context[:, N_IMG:]
        q = rms_norm(x @ q_w + q_b, nq_s).reshape(B, S, H, D)
        k_txt = rms_norm(txt_ctx @ k_w + k_b, nkt_s).reshape(B, -1, H, D)
        v_txt = (txt_ctx @ v_w + v_b).reshape(B, -1, H, D)
        out_txt = sdpa(q, k_txt, v_txt)
        k_img = rms_norm(img_ctx @ ki_w + ki_b, nki_s).reshape(B, -1, H, D)
        v_img = (img_ctx @ vi_w + vi_b).reshape(B, -1, H, D)
        out_img = sdpa(q, k_img, v_img)
        out = (out_txt + out_img).reshape(B, S, INNER)
        return out @ o_w + o_b

    def _L1_ffn_ref(hidden_states, router_w, w_gate, w_up, w_down, sh_gate, sh_up, sh_down, sh_gate_w):
        import jax, jax.numpy as jnp
        import numpy as np
        B, S, H = (2, 256, 256)
        E, K = (16, 4)
        I_MOE, I_SH = (176, 704)
        orig = hidden_states.shape
        h = hidden_states.reshape(-1, orig[-1])
        N = h.shape[0]
        logits = h @ router_w.T
        probs = jax.nn.softmax(logits.astype(jnp.float32), axis=-1)
        top_vals, top_idx = jax.lax.top_k(probs, K)
        top_vals = top_vals / jnp.maximum(top_vals.sum(-1, keepdims=True), 1e-09)
        top_vals = top_vals.astype(h.dtype)
        comb = jnp.zeros((N, E), h.dtype).at[jnp.arange(N)[:, None], top_idx].add(top_vals)
        g = jnp.einsum('nh,ehi->eni', h, w_gate)
        u = jnp.einsum('nh,ehi->eni', h, w_up)
        y = jnp.einsum('eni,eih->enh', jax.nn.silu(g) * u, w_down)
        routed = jnp.einsum('enh,ne->nh', y, comb)
        shared = jax.nn.silu(h @ sh_gate) * (h @ sh_up) @ sh_down
        sg = jax.nn.sigmoid(h @ sh_gate_w)
        return (routed + sg * shared).reshape(orig)
    x = x + _L0_xattn_ref(_layernorm(x, axis=-1), ctx_2048, itok_BxS_0_1023, L0_xattn_W_kvc, L0_xattn_W_dq, L0_xattn_W_uq, L0_xattn_W_qr, L0_xattn_W_uk, L0_xattn_W_kr, L0_xattn_W_uv, L0_xattn_W_o)
    x = x + _L0_ffn_ref(_layernorm(x, axis=-1), L0_ffn_gate_W_packed, L0_ffn_gate_scales, L0_ffn_up_W_packed, L0_ffn_up_scales, L0_ffn_down_W_packed, L0_ffn_down_scales)
    x = x + _L1_xattn_ref(_layernorm(x, axis=-1), ctx_2048, L1_xattn_q_w, L1_xattn_q_b, L1_xattn_k_w, L1_xattn_k_b, L1_xattn_v_w, L1_xattn_v_b, L1_xattn_ki_w, L1_xattn_ki_b, L1_xattn_vi_w, L1_xattn_vi_b, L1_xattn_o_w, L1_xattn_o_b, L1_xattn_nq_s, L1_xattn_nkt_s, L1_xattn_nki_s)
    x = x + _L1_ffn_ref(_layernorm(x, axis=-1), L1_ffn_router_w, L1_ffn_w_gate, L1_ffn_w_up, L1_ffn_w_down, L1_ffn_sh_gate, L1_ffn_sh_up, L1_ffn_sh_down, L1_ffn_sh_gate_w)
    return x

_drawn_inputs = setup_inputs


def setup_inputs(seed=0):
    import zlib

    import numpy as np

    out = dict(_drawn_inputs(seed))
    spreads = {'L1_xattn_q_b': (0.0, 0.8),
     'L1_xattn_k_b': (0.0, 0.8),
     'L1_xattn_v_b': (0.0, 0.422),
     'L1_xattn_ki_b': (0.0, 0.8),
     'L1_xattn_vi_b': (0.0, 0.434),
     'L1_xattn_o_b': (0.0, 0.8),
     'L1_xattn_nq_s': (1.0, 0.6),
     'L1_xattn_nkt_s': (1.0, 0.6),
     'L1_xattn_nki_s': (1.0, 0.6)}
    factors = {'L1_ffn_router_w': 2.966,
     'L1_ffn_w_gate': 2.781,
     'L1_ffn_sh_gate': 3.173,
     'L1_ffn_sh_up': 3.017,
     'L1_ffn_sh_down': 3.009,
     'L1_ffn_sh_gate_w': 6.734}
    for name, (base, spread) in spreads.items():
        noise = np.random.default_rng([zlib.crc32(name.encode()), seed]).standard_normal(out[name].shape)
        drawn = base * np.exp(spread * noise) if base else spread * noise
        out[name] = jnp.asarray(drawn.astype(out[name].dtype))
    for name, factor in factors.items():
        out[name] = (out[name] * factor).astype(out[name].dtype)
    return out
```

```python
from contextlib import ExitStack

import numpy as np

import concourse.bass as bass
from concourse import mybir

ALU = mybir.AluOpType
ACT = mybir.ActivationFunctionType
AX = mybir.AxisListType.X
F32 = mybir.dt.float32
F16 = mybir.dt.float16
F8 = mybir.dt.float8e4
I32 = mybir.dt.int32

P = 128
D = 256
KT = D // P
NB = 2
SQ = 256
SK = 512
TOK = NB * SQ
TT = TOK // P
KC = SK // P
H = 16
HD = 128
NEG = -1e30
LOWEST = -3.0e38

KVC, QC, R = 64, 96, 64
LOOKBACK = 8
SCALE0 = float(1.0 / np.sqrt(HD + R).astype(np.float32))

FT = 2048 // P
PK = 3 * P
BLK = 24

NIMG = 257
NTXT = SK - NIMG
SEG = ((0, NIMG), (NIMG, NTXT))
INNER = H * HD
SCALE1 = float(HD) ** -0.5

E, TOPK, IM, ISH = 16, 4, 176, 704
EG = E + 1
MROWS = E * IM + ISH
MT = (MROWS + P - 1) // P
MLAST = MROWS - (MT - 1) * P

PASSES = ((0, 0), (0, 1), (1, 0))


def build(nc, a):
    top = ExitStack()
    with top:
        sems = {}

        def sem(name):
            if name not in sems:
                sems[name] = top.enter_context(nc.semaphore(name))
            return sems[name]

        def tensors(stack, part="all"):
            return lambda name, shape, dt=F32: stack.enter_context(
                nc.sbuf_tensor(f"{part}_{name}", shape, dt))

        sb = tensors(top)
        bank = [top.enter_context(nc.psum_tensor(f"bank{i}", [P, 512], F32)) for i in range(8)]

        ident = sb("ident", [P, P])
        x = sb("x", [P, TT, D])
        xT = sb("xT", [P, 2, KT, TOK], F16)
        ctxT = sb("ctxT", [P, 2, KT, NB * SK], F16)
        ctxM = sb("ctxM", [P, 2, KT, NB, 2, P], F16)
        ln_st = sb("ln_st", [P, TT, 6])
        ln_mv = sb("ln_mv", [P, TT, 2])
        ln_ve = sb("ln_ve", [P, TT])
        ln_rs = sb("ln_rs", [P, TT])
        ln_x = sb("ln_x", [P, TT, D])
        mhalf = sb("mhalf", [P, 16])
        pk = top.enter_context(ExitStack())
        packed = tensors(pk)("packed", [P, FT, PK], I32)
        pscale = tensors(pk)("pscale", [P, FT + 1, BLK])

        def ln_vector(dve, n):
            for t in range(TT):
                dve.bn_stats(ln_st[:, t, :], x[:, t, :]).then_inc(sem("ln_stats"), 1)
            for t in range(TT):
                dve.wait_ge(sem("ln_stats"), TT * n + t + 1)
                dve.bn_aggr(ln_mv[:, t, :], ln_st[:, t, :]).then_inc(sem("ln_aggr"), 1)
            dve.wait_ge(sem("ln_aggr"), TT * n + TT)
            dve.tensor_scalar(ln_ve[:], ln_mv[:, :, 1], 1e-5, None, ALU.add).then_inc(sem("ln_var"), 1)
            dve.wait_ge(sem("ln_rstd"), n + 1)
            for t in range(TT):
                dve.tensor_scalar(ln_x[:, t, :], x[:, t, :], ln_mv[:, t, 0:1], ln_rs[:, t:t + 1],
                                  ALU.subtract, ALU.mult).then_inc(sem("ln_x"), 1)

        def ln_pool(pool, n):
            pool.wait_ge(sem("ln_var"), n + 1)
            pool.tensor_tensor(ln_rs[:], ln_ve[:], mhalf[:, 0:TT], ALU.pow).then_inc(sem("ln_rstd"), 1)

        def ln_tensor(pe, n, banks):
            for t in range(TT):
                pe.wait_ge(sem("ln_x"), TT * n + t + 1)
                for k in range(KT):
                    last = pe.transpose(banks[k][:, t * P:(t + 1) * P], ln_x[:, t, k * P:(k + 1) * P], ident[:])
            last.then_inc(sem("ln_T"), 1)

        def ln_scalar(act, n, banks):
            act.wait_ge(sem("ln_T"), n + 1)
            for k in range(KT):
                act.activation(xT[:, 0, k, :], banks[k][:], ACT.Copy).then_inc(sem("ln_hi"), 1)

        def ln_vector_low(dve, n, banks):
            for k in range(KT):
                dve.wait_ge(sem("ln_hi"), KT * n + k + 1)
                dve.tensor_tensor(xT[:, 1, k, :], banks[k][:], xT[:, 0, k, :], ALU.subtract)\
                   .then_inc(sem("ln_lo"), 1)

        with ExitStack() as ph:
            sp = tensors(ph, "l0")
            Aq = sp("Aq", [QC, 2, H, P], F16)
            As = sp("As", [QC, 2, H, P], F16)
            qcT = sp("qcT", [QC, 2, TOK], F16)
            kF = sp("kF", [P, 2, NB * SK], F16)
            kv = sp("kv", [P, 2, NB * KC, KVC], F16)
            M = sp("M", [P, 2, H // 2, D], F16)
            mask = sp("mask", [P, TT, SK])
            cosT = sp("cosT", [P, SK])
            sinT = sp("sinT", [P, SK])

            def q_table(tab):
                return tab[:, 0:SQ].rearrange("p (b q) -> p b q", b=1).to_broadcast([P, NB, SQ])

            def by_batch(ap):
                return ap.rearrange("p (b q) -> p b q", b=NB)

            with ExitStack() as su:
                ss = tensors(su, "setup")
                ctx = ss("ctx", [P, NB * KC, D])
                wkvc = ss("wkvc", [P, KT, KVC])
                wdq = ss("wdq", [P, KT, QC])
                wkvcS = ss("wkvcS", [P, 2, KT, KVC], F16)
                wdqS = ss("wdqS", [P, 2, KT, QC], F16)
                wkr = ss("wkr", [KVC, 2, P])
                wuq = ss("wuq", [QC, H * HD])
                wqr = ss("wqr", [QC, H, R])
                wuk = ss("wuk", [KVC, H * HD])
                wuv = ss("wuv", [KVC, H * HD])
                wo = ss("wo", [P, H, D])
                uqT = ss("uqT", [P, H, QC])
                ukT = ss("ukT", [P, H, KVC])
                uvT = ss("uvT", [P, H, KVC])
                kvcT = ss("kvcT", [KVC, NB, SK])
                kidx = ss("kidx", [P, SK])
                segi = ss("segi", [P, TT], I32)
                segf = ss("segf", [P, TT])
                mtmp = ss("mtmp", [P, SK])
                rc = ss("rc", [P, 2, SK])
                rs = ss("rs", [P, 2, SK])
                rk = ss("rk", [P, 2, SK])

                J_CTX, J_UQ, J_UK, J_UV, J_KVT, J_KV, J_A, J_M, J_K, J_X, J_QC, J_END = \
                    0, 4, 8, 10, 12, 14, 15, 17, 21, 25, 27, 28

                def fill(pe, j):
                    if j >= 8:
                        pe.wait_ge(sem("su_read"), j - 7)
                    return bank[j % 8]

                with nc.Block() as block:
                    @block.sync
                    def _(sync):
                        def load(name, dst, src):
                            sync.dma_start(dst, src).then_inc(sem("in_" + name), 16)
                        load("ident", ident[:], a["ident"])
                        load("x", x[:], a["x"].rearrange("b (t p) d -> p (b t) d", p=P))
                        load("ctx", ctx[:], a["ctx_2048"].rearrange("b (t p) d -> p (b t) d", p=P))
                        load("wuq", wuq[:], a["L0_xattn_W_uq"])
                        load("wuk", wuk[:], a["L0_xattn_W_uk"])
                        load("wuv", wuv[:], a["L0_xattn_W_uv"])
                        load("proj", wkvc[:], a["L0_xattn_W_kvc"].rearrange("(k p) n -> p k n", p=P))
                        load("proj", wdq[:], a["L0_xattn_W_dq"].rearrange("(k p) n -> p k n", p=P))
                        load("wqr", wqr[:], a["L0_xattn_W_qr"].rearrange("c (h r) -> c h r", r=R))
                        sync.dma_start(segi[:], a["itok_BxS_0_1023"].rearrange("b (t p) -> p (b t)", p=P),
                                       allow_slow_non_contiguous=True).then_inc(sem("in_tables"), 16)
                        load("tables", kidx[:], a["kidx"])
                        load("wkr", wkr[:, 0, 0:KVC], a["ident"][0:KVC, 0:KVC])
                        load("wkr", wkr[:, 0, KVC:P], a["L0_xattn_W_kr"])
                        load("wkr", wkr[:, 1, KVC:KVC + R // 2], a["L0_xattn_W_kr"][:, R // 2:R])
                        load("wkr", wkr[:, 1, KVC + R // 2:P], a["L0_xattn_W_kr"][:, 0:R // 2])
                        load("tables", cosT[:], a["cos"])
                        load("tables", sinT[:], a["sin"])
                        load("wo", wo[:], a["L0_xattn_W_o"].rearrange("(h p) n -> p h n", p=P))
                        for n, w in enumerate(("gate", "up")):
                            load("packed", packed[:, :, n * P:(n + 1) * P],
                                 a[f"L0_ffn_{w}_W_packed"].rearrange("(t p) k -> p t k", p=P))
                            load("packed", pscale[:, 0:FT, n * 8:n * 8 + 8],
                                 a[f"L0_ffn_{w}_scales"].rearrange("(t p) k -> p t k", p=P))
                        for m in range(KT):
                            load("packed", packed[:, :, 2 * P + m * 64:2 * P + m * 64 + 64],
                                 a["L0_ffn_down_W_packed"][m * P:(m + 1) * P, :]
                                 .rearrange("p (t k) -> p t k", t=FT))
                            load("packed", pscale[:, 0:FT, 16 + 4 * m:20 + 4 * m],
                                 a["L0_ffn_down_scales"][m * P:(m + 1) * P, :]
                                 .rearrange("p (t k) -> p t k", t=FT))

                    @block.gpsimd
                    def _(pool):
                        pool.memset(mhalf[:], -0.5).then_inc(sem("half"), 1)
                        pool.memset(pscale[:, FT, :], 0.0).then_inc(sem("half"), 1)
                        pool.memset(As[:, :, :, 0:KVC], 0.0).then_inc(sem("half"), 1)
                        pool.memset(wkr[:, 1, 0:KVC], 0.0).then_inc(sem("wkr_zero"), 1)
                        pool.memset(ctxM[:], 0.0).then_inc(sem("ctxM_zero"), 1)
                        pool.wait_ge(sem("half"), 3)
                        ln_pool(pool, 0)
                        pool.wait_ge(sem("in_proj"), 32)
                        pool.tensor_copy(wkvcS[:, 0], wkvc[:]).then_inc(sem("wsplit"), 1)
                        pool.tensor_copy(wdqS[:, 0], wdq[:]).then_inc(sem("wsplit"), 1)
                        pool.wait_ge(sem("wsplit"), 2)
                        pool.tensor_tensor(wkvcS[:, 1], wkvc[:], wkvcS[:, 0], ALU.subtract)\
                            .then_inc(sem("wsplit"), 1)
                        pool.tensor_tensor(wdqS[:, 1], wdq[:], wdqS[:, 0], ALU.subtract)\
                            .then_inc(sem("wsplit"), 1)
                        pool.wait_ge(sem("in_wqr"), 16)
                        hR = R // 2
                        pool.tensor_copy(Aq[:, 0, :, KVC:P], wqr[:]).then_inc(sem("rope_hi"), 1)
                        pool.wait_ge(sem("rope_hi"), 1)
                        pool.tensor_tensor(Aq[:, 1, :, KVC:P], wqr[:], Aq[:, 0, :, KVC:P], ALU.subtract)\
                            .then_inc(sem("rope_hi"), 1)
                        pool.wait_ge(sem("rope_hi"), 2)
                        for part in range(2):
                            pool.tensor_copy(As[:, part, :, KVC:KVC + hR], Aq[:, part, :, KVC + hR:P])\
                                .then_inc(sem("rope_swap"), 1)
                            pool.tensor_copy(As[:, part, :, KVC + hR:P], Aq[:, part, :, KVC:KVC + hR])\
                                .then_inc(sem("rope_swap"), 1)
                        pool.wait_ge(sem("ctxM_zero"), 1)
                        pool.wait_ge(sem("su_read"), J_CTX + 4)
                        for k in range(KT):
                            c = ctxT[:, :, k, :].rearrange("p s (b j) -> p s b j", b=NB)
                            c0 = NIMG - 1
                            for part in range(2):
                                pool.tensor_copy(ctxM[:, part, k, :, 0, 0:1], c[:, part, :, c0:c0 + 1])\
                                    .then_inc(sem("ctxM"), 1)
                                pool.tensor_copy(ctxM[:, part, k, :, 1, 1:P], c[:, part, :, c0 + 1:c0 + P])\
                                    .then_inc(sem("ctxM"), 1)

                    @block.tensor
                    def _(pe):
                        pe.wait_ge(sem("in_ident"), 16)
                        pe.wait_ge(sem("in_ctx"), 16)
                        for k in range(KT):
                            for b in range(NB):
                                out = fill(pe, J_CTX + 2 * k + b)
                                for c in range(KC):
                                    last = pe.transpose(out[:, c * P:(c + 1) * P],
                                                        ctx[:, b * KC + c, k * P:(k + 1) * P], ident[:])
                                last.then_inc(sem("su_full"), 1)
                        pe.wait_ge(sem("in_wuq"), 16)
                        for g in range(4):
                            out = fill(pe, J_UQ + g)
                            for i in range(4):
                                h = 4 * g + i
                                last = pe.transpose(out[:, i * QC:(i + 1) * QC],
                                                    wuq[:, h * HD:(h + 1) * HD], ident[0:QC, 0:QC])
                            last.then_inc(sem("su_full"), 1)
                        for j, w, ready in ((J_UK, wuk, "in_wuk"), (J_UV, wuv, "in_wuv")):
                            pe.wait_ge(sem(ready), 16)
                            for g in range(2):
                                out = fill(pe, j + g)
                                for i in range(8):
                                    h = 8 * g + i
                                    last = pe.transpose(out[:, i * KVC:(i + 1) * KVC],
                                                        w[:, h * HD:(h + 1) * HD], ident[0:KVC, 0:KVC])
                                last.then_inc(sem("su_full"), 1)
                        pe.wait_ge(sem("wsplit"), 4)
                        for b in range(NB):
                            out = fill(pe, J_KVT + b)
                            if b == 0:
                                pe.wait_ge(sem("su_read"), J_CTX + 4)
                            n = 0
                            for k in range(KT):
                                for l, r in PASSES:
                                    last = pe.matmul(out[0:KVC, :], wkvcS[:, l, k, :],
                                                     ctxT[:, r, k, b * SK:(b + 1) * SK],
                                                     start=(n == 0), stop=(n == 5))
                                    n += 1
                            last.then_inc(sem("su_full"), 1)
                        out = fill(pe, J_KV)
                        for c in range(NB * KC):
                            n = 0
                            for k in range(KT):
                                for l, r in PASSES:
                                    last = pe.matmul(out[:, c * KVC:(c + 1) * KVC],
                                                     ctxT[:, l, k, c * P:(c + 1) * P], wkvcS[:, r, k, :],
                                                     start=(n == 0), stop=(n == 5))
                                    n += 1
                        last.then_inc(sem("su_full"), 1)
                        pe.wait_ge(sem("su_read"), J_UK + 2)
                        for g in range(2):
                            out = fill(pe, J_A + g)
                            for i in range(8):
                                h = 8 * g + i
                                last = pe.matmul(out[0:QC, i * KVC:(i + 1) * KVC], uqT[:, h, :], ukT[:, h, :],
                                                 start=True, stop=True)
                            last.then_inc(sem("su_full"), 1)
                        pe.wait_ge(sem("in_wo"), 16)
                        pe.wait_ge(sem("su_read"), J_UV + 2)
                        for g in range(4):
                            out = fill(pe, J_M + g)
                            for i in range(4):
                                h = 4 * g + i
                                lo = (h % 2) * KVC
                                last = pe.matmul(out[lo:lo + KVC, (i // 2) * D:(i // 2 + 1) * D],
                                                 uvT[:, h, :], wo[:, h, :], start=True, stop=True)
                            last.then_inc(sem("su_full"), 1)
                        pe.wait_ge(sem("in_wkr"), 64)
                        pe.wait_ge(sem("wkr_zero"), 1)
                        pe.wait_ge(sem("su_read"), J_KVT + 2)
                        for b in range(NB):
                            for s in range(2):
                                out = fill(pe, J_K + 2 * b + s)
                                pe.matmul(out[:, :], wkr[:, s, :], kvcT[:, b, :], start=True, stop=True)\
                                  .then_inc(sem("su_full"), 1)
                        fill(pe, J_X)
                        ln_banks = [bank[(J_X + k) % 8] for k in range(KT)]
                        fill(pe, J_X + 1)
                        ln_tensor(pe, 0, ln_banks)
                        out = fill(pe, J_QC)
                        pe.wait_ge(sem("ln_lo"), KT)
                        n = 0
                        for k in range(KT):
                            for l, r in PASSES:
                                last = pe.matmul(out[0:QC, :], wdqS[:, l, k, :], xT[:, r, k, :],
                                                 start=(n == 0), stop=(n == 5))
                                n += 1
                        last.then_inc(sem("su_full2"), 1)

                    @block.scalar
                    def _(act):
                        def high(j, dst, src):
                            act.wait_ge(sem("su_full"), j + 1)
                            act.activation(dst, src, ACT.Copy).then_inc(sem("su_high"), 1)
                        for k in range(KT):
                            for b in range(NB):
                                high(J_CTX + 2 * k + b, ctxT[:, 0, k, b * SK:(b + 1) * SK],
                                     bank[(J_CTX + 2 * k + b) % 8][:])
                        high(J_KV, kv[:, 0].rearrange("p c n -> p (c n)"), bank[J_KV % 8][:])
                        for g in range(2):
                            high(J_A + g, Aq[:, 0, 8 * g:8 * g + 8, 0:KVC],
                                 bank[(J_A + g) % 8][0:QC, :].rearrange("p (h n) -> p h n", n=KVC))
                        for g in range(4):
                            high(J_M + g, M[:, 0, 2 * g:2 * g + 2, :],
                                 bank[(J_M + g) % 8][:].rearrange("p (h n) -> p h n", n=D))
                        for b in range(NB):
                            act.wait_ge(sem("k_roped"), b + 1)
                            act.activation(kF[:, 0, b * SK:(b + 1) * SK], rk[:, b, :], ACT.Copy)\
                               .then_inc(sem("k_high"), 1)
                        ln_scalar(act, 0, [bank[(J_X + k) % 8] for k in range(KT)])
                        act.wait_ge(sem("su_full2"), 1)
                        act.activation(qcT[:, 0, :], bank[J_QC % 8][0:QC, :], ACT.Copy)\
                           .then_inc(sem("qc_high"), 1)

                    @block.vector
                    def _(dve):
                        n_high = [0]

                        def low(dst, src, high):
                            n_high[0] += 1
                            dve.wait_ge(sem("su_high"), n_high[0])
                            dve.tensor_tensor(dst, src, high, ALU.subtract).then_inc(sem("su_read"), 1)

                        def plain(j, dst, src):
                            dve.wait_ge(sem("su_full"), j + 1)
                            dve.tensor_copy(dst, src).then_inc(sem("su_read"), 1)

                        dve.wait_ge(sem("in_x"), 16)
                        ln_vector(dve, 0)
                        for k in range(KT):
                            for b in range(NB):
                                s = slice(b * SK, (b + 1) * SK)
                                low(ctxT[:, 1, k, s], bank[(J_CTX + 2 * k + b) % 8][:], ctxT[:, 0, k, s])
                        for g in range(4):
                            plain(J_UQ + g, uqT[:, 4 * g:4 * g + 4, :],
                                  bank[(J_UQ + g) % 8][:, 0:4 * QC].rearrange("p (h n) -> p h n", n=QC))
                        for g in range(2):
                            plain(J_UK + g, ukT[:, 8 * g:8 * g + 8, :],
                                  bank[(J_UK + g) % 8][:].rearrange("p (h n) -> p h n", n=KVC))
                        for g in range(2):
                            plain(J_UV + g, uvT[:, 8 * g:8 * g + 8, :],
                                  bank[(J_UV + g) % 8][:].rearrange("p (h n) -> p h n", n=KVC))
                        for b in range(NB):
                            plain(J_KVT + b, kvcT[:, b, :], bank[(J_KVT + b) % 8][0:KVC, :])
                        low(kv[:, 1].rearrange("p c n -> p (c n)"), bank[J_KV % 8][:],
                            kv[:, 0].rearrange("p c n -> p (c n)"))
                        for g in range(2):
                            low(Aq[:, 1, 8 * g:8 * g + 8, 0:KVC],
                                bank[(J_A + g) % 8][0:QC, :].rearrange("p (h n) -> p h n", n=KVC),
                                Aq[:, 0, 8 * g:8 * g + 8, 0:KVC])
                        for g in range(4):
                            low(M[:, 1, 2 * g:2 * g + 2, :],
                                bank[(J_M + g) % 8][:].rearrange("p (h n) -> p h n", n=D),
                                M[:, 0, 2 * g:2 * g + 2, :])
                        dve.wait_ge(sem("in_tables"), 64)
                        for b in range(NB):
                            j = J_K + 2 * b
                            dve.wait_ge(sem("su_full"), j + 2)
                            dve.tensor_tensor(rc[:, b, :], bank[j % 8][:], cosT[:], ALU.mult)\
                               .then_inc(sem("su_read"), 1)
                            dve.tensor_tensor(rs[:, b, :], bank[(j + 1) % 8][:], sinT[:], ALU.mult)\
                               .then_inc(sem("su_read"), 1)
                            dve.wait_ge(sem("su_read"), j + 2)
                            dve.tensor_tensor(rk[:, b, :], rc[:, b, :], rs[:, b, :], ALU.add)\
                               .then_inc(sem("k_roped"), 1)
                        for b in range(NB):
                            s = slice(b * SK, (b + 1) * SK)
                            dve.wait_ge(sem("k_high"), b + 1)
                            dve.tensor_tensor(kF[:, 1, s], rk[:, b, :], kF[:, 0, s], ALU.subtract)\
                               .then_inc(sem("k_low"), 1)
                        dve.tensor_scalar(segf[:], segi[:], -1.0, LOOKBACK / 2, ALU.mult, ALU.add)\
                           .then_inc(sem("segf"), 1)
                        dve.wait_ge(sem("segf"), 1)
                        for t in range(TT):
                            if t:
                                dve.wait_ge(sem("mask"), t)
                            dve.tensor_scalar(mask[:, t, :], kidx[:], segf[:, t:t + 1], None, ALU.add)\
                               .then_inc(sem("mask_dist"), 1)
                            dve.wait_ge(sem("mask_dist"), 2 * t + 1)
                            dve.scalar_tensor_tensor(out=mtmp[:], in0=mask[:, t, :], scalar=-1.0,
                                                     in1=mask[:, t, :], op0=ALU.mult, op1=ALU.max)\
                               .then_inc(sem("mask_dist"), 1)
                            dve.wait_ge(sem("mask_dist"), 2 * t + 2)
                            dve.tensor_scalar(mask[:, t, :], mtmp[:], LOOKBACK / 2, NEG, ALU.is_gt, ALU.mult)\
                               .then_inc(sem("mask"), 1)
                        ln_vector_low(dve, 0, [bank[(J_X + k) % 8] for k in range(KT)])
                        dve.wait_ge(sem("qc_high"), 1)
                        dve.tensor_tensor(qcT[:, 1, :], bank[J_QC % 8][0:QC, :], qcT[:, 0, :], ALU.subtract)\
                           .then_inc(sem("qc_low"), 1)

            with ExitStack() as at:
                s_ = tensors(at, "l0head")
                tc = s_("tc", [P, 2, TOK])
                ts_ = s_("ts", [P, 2, TOK])
                tq = s_("tq", [P, 2, TOK])
                Q = s_("Q", [P, 2, 2, TOK], F16)
                X = s_("X", [P, TT, SK])
                PT = s_("PT", [P, 2, 2, SK], F16)
                mx = s_("mx", [P, TT])
                nm = s_("nm", [P, TT])
                den = s_("den", [P, 2 * TT])
                rden = s_("rden", [P, 2 * TT])
                O = s_("O", [P, TT, H * KVC])
                OT = s_("OT", [P, 2, 2, TOK], F16)
                SB, TB, QA, QS, OB = bank[0:2], bank[2:4], bank[4], bank[5], bank[6:8]
                ACC = bank[4:6]

                with nc.Block() as block:
                    @block.tensor
                    def _(pe):
                        def project(h):
                            pe.wait_ge(sem("a_qread"), 2 * h)
                            for out, w in ((QA, Aq), (QS, As)):
                                for n, (l, r) in enumerate(PASSES):
                                    last = pe.matmul(out[:], w[:, l, bass.ds(h, 1), :], qcT[:, r, :],
                                                     start=(n == 0), stop=(n == 2))
                            last.then_inc(sem("a_qfull"), 1)

                        def scores(h, t, par):
                            if t == 0:
                                pe.wait_ge(sem("a_qlow"), h + 1)
                            n = 4 * h + t
                            pe.wait_ge(sem("a_max"), n + 1)
                            b = t // 2
                            for i, (l, r) in enumerate(PASSES):
                                last = pe.matmul(SB[t % 2][:], Q[:, par, l, t * P:(t + 1) * P],
                                                 kF[:, r, b * SK:(b + 1) * SK], start=(i == 0), stop=(i == 2))
                            last.then_inc(sem("a_sfull"), 1)

                        def turn(h, t):
                            n = 4 * h + t
                            pe.wait_ge(sem("a_exp"), n + 1)
                            pe.wait_ge(sem("a_ptlow"), n + 1)
                            for c in range(KC):
                                last = pe.transpose(TB[t % 2][:, c * P:(c + 1) * P],
                                                    X[:, t, c * P:(c + 1) * P], ident[:])
                            last.then_inc(sem("a_tfull"), 1)

                        def attend(h, t):
                            n = 4 * h + t
                            pe.wait_ge(sem("a_ptlow"), n + 3)
                            pe.wait_ge(sem("a_oread"), n + 1)
                            b = t // 2
                            i = 0
                            for c in range(KC):
                                for l, r in PASSES:
                                    last = pe.matmul(OB[t % 2][:, 0:KVC], PT[:, t % 2, l, c * P:(c + 1) * P],
                                                     kv[:, r, b * KC + c, :], start=(i == 0),
                                                     stop=(i == 3 * KC - 1))
                                    i += 1
                            last.then_inc(sem("a_ofull"), 1)

                        def step(h, par, first=False, last=False, late=False):
                            for t in range(TT):
                                turn(h, t)
                                if not last:
                                    scores(h + 1, t, 1 - par)
                                if t:
                                    attend(h, t - 1)
                                elif not first:
                                    attend(h - 1, TT - 1)
                                if t == 1 and not late:
                                    project(h + 2)

                        project(0)
                        for t in range(TT):
                            scores(0, t, 0)
                        project(1)
                        step(0, 0, first=True)
                        step(1, 1)
                        with pe.Fori(1, H // 2 - 1) as g:
                            step(2 * g, 0)
                            step(2 * g + 1, 1)
                        step(H - 2, 0, late=True)
                        step(H - 1, 1, last=True, late=True)
                        attend(H - 1, TT - 1)

                        def turn_o(j):
                            if j >= 2:
                                pe.wait_ge(sem("a_otlow"), j - 1)
                            for t in range(TT):
                                last = pe.transpose(TB[j % 2][:, t * P:(t + 1) * P],
                                                    O[:, t, j * P:(j + 1) * P], ident[:])
                            last.then_inc(sem("a_otfull"), 1)
                        pe.wait_ge(sem("a_oread"), 4 * H + 2)
                        turn_o(0)
                        for j in range(H // 2):
                            if j + 1 < H // 2:
                                turn_o(j + 1)
                            pe.wait_ge(sem("a_otlow"), j + 1)
                            for t in range(TT):
                                for n, (l, r) in enumerate(PASSES):
                                    last = pe.matmul(ACC[t // 2][:, (t % 2) * D:(t % 2 + 1) * D],
                                                     OT[:, j % 2, l, t * P:(t + 1) * P], M[:, r, j, :],
                                                     start=(j == 0 and n == 0 and t % 2 == 0),
                                                     stop=(j == H // 2 - 1 and n == 2),
                                                     skip_group_check=True)
                            last.then_inc(sem("a_omm"), 1)

                    @block.scalar
                    def _(act):
                        def q_high(h, par):
                            act.wait_ge(sem("a_qsum"), h + 1)
                            act.activation(Q[:, par, 0, :], tq[:, par, :], ACT.Copy).then_inc(sem("a_qhigh"), 1)

                        def exp(h, t, par):
                            n = 4 * h + t
                            act.wait_ge(sem("a_nm"), n + 1)
                            act.activation(X[:, t, :], X[:, t, :], ACT.Exp, bias=nm[:, t:t + 1], scale=SCALE0,
                                           accum_out=den[:, par * TT + t:par * TT + t + 1])\
                               .then_inc(sem("a_exp"), 1)

                        def pt_high(h, t):
                            n = 4 * h + t
                            act.wait_ge(sem("a_tfull"), n + 1)
                            act.wait_ge(sem("a_ofull"), n + 1)
                            act.activation(PT[:, t % 2, 0, :], TB[t % 2][:], ACT.Copy)\
                               .then_inc(sem("a_pthigh"), 1)

                        def step(h, par, last=False, late=False):
                            for t in range(TT):
                                pt_high(h, t)
                                if t == 0:
                                    exp(h, 3, par)
                                elif not last:
                                    exp(h + 1, t - 1, 1 - par)
                                if t == 2 and not late:
                                    q_high(h + 2, par)

                        act.nop().then_inc(sem("a_ofull"), 2)
                        q_high(0, 0)
                        for t in range(3):
                            exp(0, t, 0)
                        q_high(1, 1)
                        step(0, 0)
                        step(1, 1)
                        with act.Fori(1, H // 2 - 1) as g:
                            step(2 * g, 0)
                            step(2 * g + 1, 1)
                        step(H - 2, 0, late=True)
                        step(H - 1, 1, last=True, late=True)
                        for j in range(H // 2):
                            act.wait_ge(sem("a_otfull"), j + 1)
                            if j >= 2:
                                act.wait_ge(sem("a_omm"), j - 1)
                            act.activation(OT[:, j % 2, 0, :], TB[j % 2][:], ACT.Copy)\
                               .then_inc(sem("a_othigh"), 1)

                    @block.gpsimd
                    def _(pool):
                        def q_sum(h, par):
                            pool.wait_ge(sem("a_qread"), 2 * h + 2)
                            pool.tensor_tensor(tq[:, par, :], tc[:, par, :], ts_[:, par, :], ALU.add)\
                                .then_inc(sem("a_qsum"), 1)
                            pool.wait_ge(sem("a_qhigh"), h + 1)
                            pool.tensor_tensor(Q[:, par, 1, :], tq[:, par, :], Q[:, par, 0, :], ALU.subtract)\
                                .then_inc(sem("a_qlow"), 1)
                        with pool.Fori(0, H // 2) as g:
                            q_sum(2 * g, 0)
                            q_sum(2 * g + 1, 1)

                    @block.vector
                    def _(dve):
                        def q_rope(h, par):
                            dve.wait_ge(sem("a_qfull"), h + 1)
                            dve.tensor_tensor(by_batch(tc[:, par, :]), by_batch(QA[:]), q_table(cosT),
                                              ALU.mult).then_inc(sem("a_qread"), 1)
                            dve.tensor_tensor(by_batch(ts_[:, par, :]), by_batch(QS[:]), q_table(sinT),
                                              ALU.mult).then_inc(sem("a_qread"), 1)

                        def top_score(h, t):
                            n = 4 * h + t
                            dve.tensor_tensor_reduce(X[:, t, :], SB[t % 2][:], mask[:, t, :], 1.0, LOWEST,
                                                     ALU.add, ALU.max, mx[:, t:t + 1])\
                               .then_inc(sem("a_max"), 1)
                            dve.wait_ge(sem("a_max"), n + 3)
                            dve.tensor_scalar(nm[:, t:t + 1], mx[:, t:t + 1], -SCALE0, None, ALU.mult)\
                               .then_inc(sem("a_nm"), 1)

                        def pt_low(h, t):
                            n = 4 * h + t
                            dve.wait_ge(sem("a_pthigh"), n + 1)
                            dve.tensor_tensor(PT[:, t % 2, 1, :], TB[t % 2][:], PT[:, t % 2, 0, :],
                                              ALU.subtract).then_inc(sem("a_ptlow"), 1)

                        def o_den(par, t):
                            i = par * TT + t
                            dve.reciprocal(rden[:, i:i + 1], den[:, i:i + 1]).then_inc(sem("a_rden"), 1)

                        def o_out(h, t, par):
                            n = 4 * h + t
                            i = par * TT + t
                            dve.wait_ge(sem("a_ofull"), n + 3)
                            dve.wait_ge(sem("a_rden"), n + 1)
                            dve.tensor_scalar(O[:, t, bass.ds(h * KVC, KVC)], OB[t % 2][:, 0:KVC],
                                              rden[:, i:i + 1], None, ALU.mult).then_inc(sem("a_oread"), 1)

                        def step(h, par, first=False, last=False, late=False):
                            for t in range(TT):
                                if not last:
                                    dve.wait_ge(sem("a_sfull"), 4 * (h + 1) + t + 1)
                                if t:
                                    o_den(par, t - 1)
                                elif not first:
                                    o_den(1 - par, TT - 1)
                                if not last:
                                    top_score(h + 1, t)
                                pt_low(h, t)
                                if t:
                                    o_out(h, t - 1, par)
                                elif not first:
                                    o_out(h - 1, TT - 1, 1 - par)
                                if t == 1 and not late:
                                    q_rope(h + 2, par)

                        for credit in ("a_max", "a_ptlow", "a_oread"):
                            dve.nop().then_inc(sem(credit), 2)
                        q_rope(0, 0)
                        for t in range(TT):
                            dve.wait_ge(sem("a_sfull"), t + 1)
                            top_score(0, t)
                        q_rope(1, 1)
                        step(0, 0, first=True)
                        step(1, 1)
                        with dve.Fori(1, H // 2 - 1) as g:
                            step(2 * g, 0)
                            step(2 * g + 1, 1)
                        step(H - 2, 0, late=True)
                        step(H - 1, 1, last=True, late=True)
                        o_den(1, TT - 1)
                        o_out(H - 1, TT - 1, 1)
                        for j in range(H // 2):
                            dve.wait_ge(sem("a_othigh"), j + 1)
                            dve.tensor_tensor(OT[:, j % 2, 1, :], TB[j % 2][:], OT[:, j % 2, 0, :],
                                              ALU.subtract).then_inc(sem("a_otlow"), 1)
                        dve.wait_ge(sem("a_omm"), H // 2)
                        for i in range(2):
                            xs = x[:, 2 * i:2 * i + 2, :].rearrange("p t d -> p (t d)")
                            dve.tensor_tensor(xs, ACC[i][:], xs, ALU.add).then_inc(sem("residual"), 1)

        with ExitStack() as ph:
            s_ = tensors(ph, "ffn")
            y1 = s_("y1", [P, PK], I32)
            y2 = s_("y2", [P, PK], I32)
            y3 = s_("y3", [P, PK], I32)
            codes = s_("codes", [P, 2, PK], I32)
            sc = s_("sc", [P, 2, BLK])
            W = s_("W", [P, 2, 2 * PK])
            WG = s_("WG", [P, 2, 2, 4, P], F16)
            WD = s_("WD", [P, 4, 2, D], F16)
            gl = s_("gl", [P, 2, TOK])
            it = s_("it", [P, 2, TOK])
            IN = s_("IN", [P, 4, 2, TOK], F16)
            zero = s_("zero", [P, P], F16)
            WB, WB2, ACC = bank[0], bank[1], bank[6:8]
            GB, UB = (bank[2], bank[4]), (bank[3], bank[5])
            LAST = FT - 1

            def over_blocks(ap):
                return ap.rearrange("p (b k f) -> p b k f", b=BLK, f=2)

            with nc.Block() as block:
                @block.gpsimd
                def _(pool):
                    def fetch_scales(i, u):
                        pool.tensor_copy(sc[:, u % 2, :], pscale[:, bass.ds(i, 1), :]
                                         .rearrange("p o b -> p (o b)")).then_inc(sem("f_sc"), 1)

                    def scaled(i, u):
                        pool.wait_ge(sem("f_w"), i + 2)
                        pool.wait_ge(sem("f_codes"), i + 1)
                        pool.wait_ge(sem("f_tr"), i + 1)
                        pool.wait_ge(sem("f_sc"), i + 1)
                        fetch_scales(i + 1, u + 1)
                        value = codes[:, u % 2, :].bitcast(F8)\
                            .rearrange("p (b k f) -> p b k f", b=BLK, f=4)[:, :, :, 0:2]
                        scale = sc[:, u % 2, :].rearrange("p (b o q) -> p b o q", o=1, q=1)\
                            .to_broadcast([P, BLK, 16, 2])
                        pool.tensor_tensor(over_blocks(W[:, u % 2, :]), value, scale, ALU.mult)\
                            .then_inc(sem("f_w"), 1)

                    def in_low(i, u):
                        pool.wait_ge(sem("f_ihigh"), i + 1)
                        pool.tensor_tensor(IN[:, u % 4, 1, :], it[:, u % 2, :], IN[:, u % 4, 0, :],
                                           ALU.subtract).then_inc(sem("f_ilow"), 1)

                    pool.memset(zero[:], 0.0).then_inc(sem("f_zero"), 1)
                    pool.nop().then_inc(sem("f_w"), 2)
                    pool.nop().then_inc(sem("f_ilow"), 2)
                    pool.wait_ge(sem("f_scale64"), 1)
                    fetch_scales(0, 0)
                    scaled(0, 0)
                    ln_pool(pool, 1)
                    scaled(1, 1)
                    scaled(2, 2)
                    in_low(0, 0)
                    scaled(3, 3)
                    in_low(1, 1)
                    with pool.Fori(0, 3) as g:
                        for u in range(1, 5):
                            scaled(4 * g + u + 3, u + 3)
                            in_low(4 * g + u + 1, u + 1)
                    for i in range(13, LAST):
                        in_low(i + 1, i + 1)

                @block.tensor
                def _(pe):
                    def turn(i, u):
                        pe.wait_ge(sem("f_w"), i + 3)
                        pe.wait_ge(sem("f_wlow"), 2 * i + 2)
                        for m in range(6):
                            out = WB[:, m * P:(m + 1) * P] if m < 4 else WB2[:, (m - 4) * P:(m - 3) * P]
                            last = pe.transpose(out, W[:, u % 2, m * P:(m + 1) * P], ident[:])
                        last.then_inc(sem("f_tr"), 1)

                    def gate_up(i, u):
                        pe.wait_ge(sem("f_wlow"), 2 * i + 4)
                        pe.wait_ge(sem("f_uread"), i + 1)
                        for m, out in enumerate((GB[u % 2], UB[u % 2])):
                            n = 0
                            for k in range(KT):
                                for l, r in PASSES:
                                    last = pe.matmul(out[:], WG[:, u % 2, l, 2 * m + k, :], xT[:, r, k, :],
                                                     start=(n == 0), stop=(n == 5))
                                    n += 1
                        last.then_inc(sem("f_gu"), 1)

                    def down(i, u):
                        pe.wait_ge(sem("f_ilow"), i + 3)
                        for t in range(TT):
                            for l, r in PASSES:
                                last = pe.matmul(ACC[t // 2][:, (t % 2) * D:(t % 2 + 1) * D],
                                                 IN[:, u % 4, l, t * P:(t + 1) * P], WD[:, u % 4, r, :],
                                                 start=False, stop=False, skip_group_check=True)
                        last.then_inc(sem("f_dn"), 1)

                    pe.wait_ge(sem("f_zero"), 1)
                    for acc in ACC:
                        pe.matmul(acc[:], zero[:], xT[:, 0, 0, :], start=True, stop=False,
                                  skip_group_check=True)
                    turn(0, 0)
                    turn(1, 1)
                    ln_tensor(pe, 1, bank[2:4])
                    pe.wait_ge(sem("ln_lo"), 2 * KT)
                    gate_up(0, 0)
                    turn(2, 2)
                    gate_up(1, 1)
                    with pe.Fori(0, 3) as g:
                        for u in range(1, 5):
                            turn(4 * g + u + 2, u + 2)
                            gate_up(4 * g + u + 1, u + 1)
                            down(4 * g + u - 1, u - 1)
                    for i in range(13, FT + 1):
                        if i + 2 < FT:
                            turn(i + 2, i + 2)
                        if i + 1 < FT:
                            gate_up(i + 1, i + 1)
                        down(i - 1, i - 1)

                @block.scalar
                def _(act):
                    def w_high(i, u):
                        act.wait_ge(sem("f_tr"), i + 3)
                        act.activation(WG[:, u % 2, 0].rearrange("p m n -> p (m n)"), WB[:], ACT.Copy)\
                           .then_inc(sem("f_whigh"), 1)
                        act.activation(WD[:, u % 4, 0, :], WB2[:, 0:D], ACT.Copy)\
                           .then_inc(sem("f_whigh"), 1)

                    def gelu(i, u):
                        act.wait_ge(sem("f_gu"), i + 1)
                        act.activation(gl[:, u % 2, :], GB[u % 2][:], ACT.Gelu_apprx_tanh)\
                           .then_inc(sem("f_gelu"), 1)

                    def in_high(i, u):
                        act.wait_ge(sem("f_uread"), i + 3)
                        act.activation(IN[:, u % 4, 0, :], it[:, u % 2, :], ACT.Copy)\
                           .then_inc(sem("f_ihigh"), 1)

                    act.nop().then_inc(sem("f_tr"), 2)
                    w_high(0, 0)
                    w_high(1, 1)
                    ln_scalar(act, 1, bank[2:4])
                    gelu(0, 0)
                    in_high(0, 0)
                    w_high(2, 2)
                    gelu(1, 1)
                    in_high(1, 1)
                    with act.Fori(0, 3) as g:
                        for u in range(1, 5):
                            w_high(4 * g + u + 2, u + 2)
                            gelu(4 * g + u + 1, u + 1)
                            in_high(4 * g + u + 1, u + 1)
                    for i in range(13, LAST):
                        if i + 2 < FT:
                            w_high(i + 2, i + 2)
                        gelu(i + 1, i + 1)
                        in_high(i + 1, i + 1)

                @block.vector
                def _(dve):
                    shl, band, bor = ALU.logical_shift_left, ALU.bitwise_and, ALU.bitwise_or

                    def decode(i, u):
                        src = packed[:, bass.ds(i, 1), :].rearrange("p o k -> p (o k)")
                        dve.wait_ge(sem("f_dec"), 5 * i + 1)
                        dve.tensor_scalar(y1[:], src, 4, 0xF00, shl, band).then_inc(sem("f_dec"), 1)
                        dve.tensor_scalar(y2[:], src, 0xF, None, band).then_inc(sem("f_dec"), 1)
                        dve.wait_ge(sem("f_dec"), 5 * i + 3)
                        dve.tensor_tensor(y3[:], y1[:], y2[:], bor).then_inc(sem("f_dec"), 1)
                        dve.wait_ge(sem("f_dec"), 5 * i + 4)
                        dve.tensor_scalar(y1[:], y3[:], 4, 0x8080, shl, band).then_inc(sem("f_dec"), 1)
                        dve.tensor_scalar(y2[:], y3[:], 2, 0x1C1C, shl, band).then_inc(sem("f_dec"), 1)
                        dve.wait_ge(sem("f_dec"), 5 * i + 6)
                        dve.wait_ge(sem("f_w"), i + 1)
                        dve.tensor_tensor(codes[:, u % 2, :], y1[:], y2[:], bor)\
                           .then_inc(sem("f_codes"), 1)
                        dve.wait_ge(sem("f_codes"), i + 1)

                    def w_low(i, u):
                        dve.wait_ge(sem("f_whigh"), 2 * i + 2)
                        wg = WG[:, u % 2, 0].rearrange("p m n -> p (m n)")
                        dve.tensor_tensor(WG[:, u % 2, 1].rearrange("p m n -> p (m n)"), WB[:], wg,
                                          ALU.subtract).then_inc(sem("f_wlow"), 1)
                        dve.tensor_tensor(WD[:, u % 4, 1, :], WB2[:, 0:D], WD[:, u % 4, 0, :],
                                          ALU.subtract).then_inc(sem("f_wlow"), 1)

                    def gated(i, u):
                        dve.wait_ge(sem("f_gelu"), i + 1)
                        dve.wait_ge(sem("f_ilow"), i + 1)
                        dve.tensor_tensor(it[:, u % 2, :], UB[u % 2][:], gl[:, u % 2, :], ALU.mult)\
                           .then_inc(sem("f_uread"), 1)

                    dve.nop().then_inc(sem("f_wlow"), 2)
                    dve.nop().then_inc(sem("f_uread"), 2)
                    dve.nop().then_inc(sem("f_dec"), 1)
                    dve.wait_ge(sem("in_packed"), 128)
                    sall = pscale[:].rearrange("p t b -> p (t b)")
                    dve.tensor_scalar(sall, sall, 64.0, None, ALU.mult).then_inc(sem("f_scale64"), 1)
                    decode(0, 0)
                    ln_vector(dve, 1)
                    decode(1, 1)
                    w_low(0, 0)
                    w_low(1, 1)
                    ln_vector_low(dve, 1, bank[2:4])
                    decode(2, 2)
                    gated(0, 0)
                    w_low(2, 2)
                    decode(3, 3)
                    gated(1, 1)
                    with dve.Fori(0, 3) as g:
                        for u in range(1, 5):
                            w_low(4 * g + u + 2, u + 2)
                            decode(4 * g + u + 3, u + 3)
                            gated(4 * g + u + 1, u + 1)
                    for i in range(13, LAST):
                        if i + 2 < FT:
                            w_low(i + 2, i + 2)
                        gated(i + 1, i + 1)
                    dve.wait_ge(sem("f_dn"), FT)
                    for i in range(2):
                        xs = x[:, 2 * i:2 * i + 2, :].rearrange("p t d -> p (t d)")
                        dve.tensor_tensor(xs, ACC[i][:], xs, ALU.add).then_inc(sem("residual"), 1)

        pk.close()

        with ExitStack() as ph:
            s_ = tensors(ph, "l1")
            KS = s_("KS", [P, 2, H, NB * SK], F16)
            QS_ = s_("QS_", [P, 2, H, TOK], F16)
            VW = s_("VW", [P, 2, 2, KT, INNER], F16)
            vec = s_("vec", [P, 8, H])
            vb = s_("vb", [P, H])
            ones = s_("ones", [P, P])
            obr = s_("obr", [1, 2 * D])
            rr = s_("rr", [P, NB * KC + TT])
            rq = s_("rq", [P, TT])
            nrq = s_("nrq", [P, TT])
            rK = s_("rK", [P, NB, SK])
            V_QB, V_KB, V_KIB, V_NQ, V_NKT, V_NKI, V_VB, V_VIB = range(8)

            with ExitStack() as pr:
                t_ = tensors(pr, "l1proj")
                NST = 6
                stage = t_("stage", [P, NST, KT, 2 * HD])
                WS = t_("WS", [P, 2, 2, 2, KT, 2 * HD], F16)
                raw = t_("raw", [P, 2, SK])
                sq = t_("sq", [P, 2, SK])
                ssq = t_("ssq", [P, NB + 1, SK])
                vrow = t_("vrow", [P, P])
                dg = t_("dg", [P, 2, P])
                ms = t_("ms", [P, NB * KC + TT])
                HP = H // 2
                pieces = [(w, p) for p in range(HP) for w in ("k_w", "ki_w")]
                pieces += [("q_w", p) for p in range(HP)]
                pieces += [(w, p) for p in range(HP) for w in ("v_w", "vi_w")]
                KB = (bank[0:2], bank[2:4])

                with nc.Block() as block:
                    @block.sync
                    def _(sync):
                        for n, name in enumerate(("q_b", "k_b", "ki_b", "nq_s", "nkt_s", "nki_s", "v_b",
                                                  "vi_b")):
                            sync.dma_start(vrow[n * H:(n + 1) * H, :],
                                           a["L1_xattn_" + name].rearrange("(h p) -> h p", p=P))\
                                .then_inc(sem("in_vec"), 16)
                        for i in range(2):
                            sync.dma_start(obr[:, i * D:(i + 1) * D],
                                           a["L1_xattn_o_b"].rearrange("(o n) -> o n", o=1))\
                                .then_inc(sem("in_vec"), 16)
                        for n, (w, p) in enumerate(pieces):
                            if n >= NST:
                                sync.wait_ge(sem("p_split"), n - NST + 1)
                            sync.dma_start(stage[:, n % NST], a["L1_xattn_" + w]
                                           .rearrange("(k p) n -> p k n", p=P)[:, :, p * 256:p * 256 + 256])\
                                .then_inc(sem(f"in_stage{n % NST}"), 16)

                    @block.gpsimd
                    def _(pool):
                        def split(n):
                            w, p = pieces[n]
                            if w in ("k_w", "ki_w"):
                                hi, lo = (WS[:, p % 2, s, int(w == "ki_w")] for s in range(2))
                                if p >= 2:
                                    pool.wait_ge(sem("p_kmm"), 4 * (p - 1))
                            elif w == "q_w":
                                hi, lo = (WS[:, p % 2, s, 0] for s in range(2))
                                pool.wait_ge(sem("p_kmm"), 4 * HP)
                                if p >= 2:
                                    pool.wait_ge(sem("p_qmm"), 2 * (p - 1))
                            else:
                                hi, lo = (VW[:, s, int(w == "vi_w"), :, p * 256:p * 256 + 256]
                                          for s in range(2))
                            pool.wait_ge(sem(f"in_stage{n % NST}"), 16 * (n // NST + 1))
                            pool.tensor_copy(hi, stage[:, n % NST]).then_inc(sem("p_hi"), 1)
                            pool.wait_ge(sem("p_hi"), n + 1)
                            pool.tensor_tensor(lo, stage[:, n % NST], hi, ALU.subtract)\
                                .then_inc(sem("p_split"), 1)

                        def square_sum(u, part):
                            pool.wait_ge(sem("p_sq"), u + 1)
                            if u:
                                pool.wait_ge(sem("p_ssq"), u + 2)
                            pool.tensor_tensor(ssq[:, part, :], ssq[:, part, :], sq[:, u % 2, :], ALU.add)\
                                .then_inc(sem("p_ssq"), 1)

                        pool.memset(ones[:], 1.0).then_inc(sem("p_ones"), 1)
                        pool.memset(ssq[:], 0.0).then_inc(sem("p_ones"), 1)
                        for n in range(4):
                            split(n)
                        ln_pool(pool, 2)
                        pool.wait_ge(sem("p_ones"), 2)
                        n = 4
                        for h in range(H):
                            for b in range(NB):
                                square_sum(2 * h + b, b)
                            if h % 2 == 1 and n < 2 * HP + 2:
                                split(n)
                                n += 1
                                if n < 2 * HP:
                                    split(n)
                                    n += 1
                        while n < 2 * HP + 2:
                            split(n)
                            n += 1
                        for h in range(H):
                            square_sum(2 * H + h, NB)
                            if h % 2 == 1 and n < 3 * HP:
                                split(n)
                                n += 1
                        pool.wait_ge(sem("p_ms"), 1)
                        pool.tensor_tensor(rr[:], ms[:], mhalf[:, 0:NB * KC + TT], ALU.pow)\
                            .then_inc(sem("p_rr"), 1)
                        while n < len(pieces):
                            split(n)
                            n += 1

                    @block.tensor
                    def _(pe):
                        pe.wait_ge(sem("in_vec"), 160)
                        pe.transpose(bank[4][:, 0:P], vrow[:], ident[:]).then_inc(sem("p_vec"), 1)

                        def keys(h, u):
                            for b in range(NB):
                                pe.wait_ge(sem("p_raw"), 2 * h + b + 1)
                                for seg, (c0, w) in enumerate(SEG):
                                    n = 0
                                    for k in range(KT):
                                        for l, r in PASSES:
                                            last = pe.matmul(
                                                KB[u % 2][b][:, c0:c0 + w],
                                                WS[:, (u // 2) % 2, l, 1 - seg, k, (u % 2) * HD:(u % 2 + 1) * HD],
                                                ctxT[:, r, k, b * SK + c0:b * SK + c0 + w],
                                                start=(n == 0), stop=(n == 5))
                                            n += 1
                                last.then_inc(sem("p_kmm"), 1)

                        def queries(h, u):
                            pe.wait_ge(sem("p_raw"), 2 * H + h + 1)
                            n = 0
                            for k in range(KT):
                                for l, r in PASSES:
                                    last = pe.matmul(KB[(u // 2) % 2][u % 2][:],
                                                     WS[:, (u // 2) % 2, l, 0, k, (u % 2) * HD:(u % 2 + 1) * HD],
                                                     xT[:, r, k, :], start=(n == 0), stop=(n == 5))
                                    n += 1
                            last.then_inc(sem("p_qmm"), 1)

                        pe.wait_ge(sem("p_split"), 2)
                        for u in range(2):
                            keys(u, u)
                        pe.wait_ge(sem("p_split"), 4)
                        for u in range(2, 4):
                            keys(u, u)
                        ln_tensor(pe, 2, bank[6:8])
                        with pe.Fori(1, H // 4) as g:
                            for u in range(4):
                                if u % 2 == 0:
                                    pe.wait_ge(sem("p_split"), 4 * g + u + 2)
                                keys(4 * g + u, u)
                        pe.wait_ge(sem("ln_lo"), 3 * KT)
                        with pe.Fori(0, H // 4) as g:
                            for u in range(4):
                                if u % 2 == 0:
                                    pe.wait_ge(sem("p_split"), 2 * HP + 2 * g + u // 2 + 1)
                                queries(4 * g + u, u)
                        pe.wait_ge(sem("p_ssq"), 3 * H + 2)
                        for c in range(NB * KC + TT):
                            last = pe.matmul(bank[4][:, c:c + 1],
                                             ssq[:, c // KC, (c % KC) * P:(c % KC + 1) * P],
                                             ones[:, 0:1], start=True, stop=True)
                        last.then_inc(sem("p_sum"), 1)
                        for c in range(NB * KC):
                            pe.wait_ge(sem("p_dg"), c + 1)
                            pe.matmul(bank[6 + c // KC][:, (c % KC) * P:(c % KC + 1) * P], ones[:],
                                      dg[:, c % 2, :], start=True, stop=True).then_inc(sem("p_rK"), 1)

                    @block.scalar
                    def _(act):
                        def square(n, u):
                            act.wait_ge(sem("p_raw"), n + 5)
                            act.wait_ge(sem("p_ssq"), n + 1)
                            act.activation(sq[:, u % 2, :], raw[:, u % 2, :], ACT.Square)\
                               .then_inc(sem("p_sq"), 1)

                        def raw_rows(bankv, n_mm, mm_sem, u, segs, n, first=False):
                            act.wait_ge(sem(mm_sem), n_mm)
                            act.wait_ge(sem("p_low"), n + 1)
                            if not first:
                                square(n - 1, u - 1)
                            for c0, w, bias in segs:
                                last = act.activation(raw[:, u % 2, c0:c0 + w], bankv[:, c0:c0 + w],
                                                      ACT.Identity, bias=bias)
                            last.then_inc(sem("p_raw"), 1)

                        def head_of(v, h):
                            return vec[:, v, bass.ds(h, 1)]

                        act.nop().then_inc(sem("p_raw"), 4)
                        act.wait_ge(sem("p_vec"), 1)
                        act.activation(vec[:].rearrange("p v h -> p (v h)"), bank[4][:, 0:P], ACT.Copy)\
                           .then_inc(sem("p_vec"), 1)
                        act.wait_ge(sem("p_vec"), 2)

                        def keys(h, u, fresh=False):
                            for b in range(NB):
                                raw_rows(KB[u % 2][b], 2 * h + b + 1, "p_kmm", b,
                                         ((0, NIMG, head_of(V_KIB, h)), (NIMG, NTXT, head_of(V_KB, h))),
                                         2 * h + b, first=(u == 0 and b == 0 and fresh))
                        for u in range(4):
                            keys(u, u, fresh=True)
                        ln_scalar(act, 2, bank[6:8])
                        with act.Fori(1, H // 4) as g:
                            for u in range(4):
                                keys(4 * g + u, u)
                        with act.Fori(0, H // 4) as g:
                            for u in range(4):
                                h = 4 * g + u
                                raw_rows(KB[(u // 2) % 2][u % 2], h + 1, "p_qmm", u,
                                         ((0, TOK, head_of(V_QB, h)),), 2 * H + h)
                        square(3 * H - 1, 1)
                        act.wait_ge(sem("p_rK"), NB * KC)
                        for b in range(NB):
                            act.activation(rK[:, b, :], bank[6 + b][:], ACT.Copy).then_inc(sem("p_end"), 1)

                    @block.vector
                    def _(dve):
                        def halves(dst, h, u, ahead, segs):
                            dve.wait_ge(sem("p_raw"), ahead + 5)
                            for c0, w, v in segs:
                                dve.tensor_scalar(dst(0, c0, w), raw[:, u % 2, c0:c0 + w],
                                                  vec[:, v, bass.ds(h, 1)], None, ALU.mult)\
                                   .then_inc(sem(f"p_high{len(segs)}"), 1)
                            for i, (c0, w, v) in enumerate(segs):
                                dve.wait_ge(sem(f"p_high{len(segs)}"),
                                            (2 * ahead if len(segs) == 2 else h) + i + 1)
                                last = dve.scalar_tensor_tensor(
                                    out=dst(1, c0, w), in0=raw[:, u % 2, c0:c0 + w],
                                    scalar=vec[:, v, bass.ds(h, 1)], in1=dst(0, c0, w),
                                    op0=ALU.mult, op1=ALU.subtract)
                            last.then_inc(sem("p_low"), 1)

                        def one(ap):
                            return ap.rearrange("p o n -> p (o n)")

                        def keys(h):
                            for b in range(NB):
                                halves(lambda s, c0, w, b=b: one(KS[:, s, bass.ds(h, 1),
                                                                   b * SK + c0:b * SK + c0 + w]),
                                       h, b, 2 * h + b, ((0, NIMG, V_NKI), (NIMG, NTXT, V_NKT)))

                        dve.nop().then_inc(sem("p_low"), 2)
                        dve.nop().then_inc(sem("p_ssq"), 2)
                        ln_vector(dve, 2)
                        dve.wait_ge(sem("p_vec"), 2)
                        dve.tensor_tensor(vb[:], vec[:, V_VB, :], vec[:, V_VIB, :], ALU.add)\
                           .then_inc(sem("p_end"), 1)
                        for h in range(4):
                            keys(h)
                        ln_vector_low(dve, 2, bank[6:8])
                        with dve.Fori(1, H // 4) as g:
                            for u in range(4):
                                keys(4 * g + u)
                        with dve.Fori(0, H // 4) as g:
                            for u in range(4):
                                h = 4 * g + u
                                halves(lambda s, c0, w: one(QS_[:, s, bass.ds(h, 1), c0:c0 + w]),
                                       h, u, 2 * H + h, ((0, TOK, V_NQ),))
                        dve.wait_ge(sem("p_sum"), 1)
                        dve.tensor_scalar(ms[:], bank[4][:, 0:NB * KC + TT], 1.0 / INNER, 1e-6, ALU.mult,
                                          ALU.add).then_inc(sem("p_ms"), 1)
                        dve.wait_ge(sem("p_rr"), 1)
                        qr = rr[:, NB * KC:NB * KC + TT]
                        dve.tensor_scalar(rq[:], qr, SCALE1, None, ALU.mult).then_inc(sem("p_end"), 1)
                        dve.tensor_scalar(nrq[:], qr, -SCALE1, None, ALU.mult).then_inc(sem("p_end"), 1)
                        for c in range(NB * KC):
                            if c >= 2:
                                dve.wait_ge(sem("p_rK"), c - 1)
                            dve.tensor_scalar(dg[:, c % 2, :], ident[:], rr[:, c:c + 1], None, ALU.mult)\
                               .then_inc(sem("p_dg"), 1)

            with ExitStack() as at:
                t_ = tensors(at, "l1head")
                OW = t_("OW", [P, 2, H, D], F16)
                ostage = t_("ostage", [P, 2, 2, D])
                V = t_("V", [P, 2, 2, NB * KC, HD], F16)
                X = t_("X", [P, TT, SK])
                PT = t_("PT", [P, 2, 2, SK], F16)
                mx = t_("mx", [P, TT, 2])
                nm = t_("nm", [P, TT, 2])
                den = t_("den", [P, TT, 2])
                rden = t_("rden", [P, TT, 2])
                OT = t_("OT", [P, 2, 2, TOK], F16)
                SB, TB, OB, VB, ACC = bank[0:2], bank[2:4], bank[4], bank[5], bank[6:8]

                with nc.Block() as block:
                    @block.sync
                    def _(sync):
                        for g in range(H // 2):
                            if g >= 2:
                                sync.wait_ge(sem("o_split"), g - 1)
                            sync.dma_start(ostage[:, g % 2], a["L1_xattn_o_w"].rearrange(
                                "(h p) n -> p h n", p=P)[:, 2 * g:2 * g + 2, :])\
                                .then_inc(sem(f"in_ow{g % 2}"), 16)

                    @block.gpsimd
                    def _(pool):
                        for g in range(H // 2):
                            hi, lo = (OW[:, s, 2 * g:2 * g + 2, :] for s in range(2))
                            pool.wait_ge(sem(f"in_ow{g % 2}"), 16 * (g // 2 + 1))
                            pool.tensor_copy(hi, ostage[:, g % 2]).then_inc(sem("o_hi"), 1)
                            pool.wait_ge(sem("o_hi"), g + 1)
                            pool.tensor_tensor(lo, ostage[:, g % 2], hi, ALU.subtract)\
                                .then_inc(sem("o_split"), 1)

                    @block.tensor
                    def _(pe):
                        def values(h, par, b, half):
                            if half == 0:
                                pe.wait_ge(sem("b_vlow"), 2 * h + b + 1)
                            for c in (2 * half, 2 * half + 1):
                                if c == NIMG // P:
                                    terms = [(ctxM[:, l, k, b, v, :], l, r, k, 1 - v)
                                             for v in range(2) for k in range(KT) for l, r in PASSES]
                                else:
                                    terms = [(ctxT[:, l, k, b * SK + c * P:b * SK + (c + 1) * P], l, r, k,
                                              int(c < NIMG // P)) for k in range(KT) for l, r in PASSES]
                                for n, (rows, l, r, k, w) in enumerate(terms):
                                    last = pe.matmul(VB[:, c * HD:(c + 1) * HD], rows,
                                                     VW[:, r, w, k, bass.ds(h * HD, HD)],
                                                     start=(n == 0), stop=(n == len(terms) - 1))
                            if half:
                                last.then_inc(sem("b_vfull"), 1)

                        def scores(h, t):
                            n = 4 * h + t
                            pe.wait_ge(sem("b_max"), 2 * n + 2)
                            b = t // 2
                            for i, (l, r) in enumerate(PASSES):
                                last = pe.matmul(SB[t % 2][:], QS_[:, l, bass.ds(h, 1), t * P:(t + 1) * P],
                                                 KS[:, r, bass.ds(h, 1), b * SK:(b + 1) * SK],
                                                 start=(i == 0), stop=(i == 2))
                            last.then_inc(sem("b_sfull"), 1)

                        def turn(h, t):
                            n = 4 * h + t
                            pe.wait_ge(sem("b_norm"), n + 1)
                            pe.wait_ge(sem("b_ptlow"), n + 1)
                            for c in range(KC):
                                last = pe.transpose(TB[t % 2][:, c * P:(c + 1) * P],
                                                    X[:, t, c * P:(c + 1) * P], ident[:])
                            last.then_inc(sem("b_tfull"), 1)

                        def attend(h, t, par):
                            n = 4 * h + t
                            b = t // 2
                            pe.wait_ge(sem("b_ptlow"), n + 3)
                            if t == 0:
                                pe.wait_ge(sem("b_vlow"), 2 * h + 3)
                                pe.wait_ge(sem("b_olow"), h + 1)
                            i = 0
                            for c in range(KC):
                                for l, r in PASSES:
                                    last = pe.matmul(OB[:, t * P:(t + 1) * P], V[:, par, l, b * KC + c, :],
                                                     PT[:, t % 2, r, c * P:(c + 1) * P], start=(i == 0),
                                                     stop=(i == 3 * KC - 1))
                                    i += 1
                            last.then_inc(sem("b_ofull"), 1)

                        def output(h, par):
                            pe.wait_ge(sem("b_olow"), h + 2)
                            for t in range(TT):
                                for l, r in PASSES:
                                    last = pe.matmul(ACC[t // 2][:, (t % 2) * D:(t % 2 + 1) * D],
                                                     OT[:, par, l, t * P:(t + 1) * P],
                                                     OW[:, r, bass.ds(h, 1), :], start=False, stop=False,
                                                     skip_group_check=True)
                            last.then_inc(sem("b_omm"), 1)

                        def step(h, par, first=False, last=False):
                            for t in range(TT):
                                turn(h, t)
                                if not last:
                                    scores(h + 1, t)
                                    values(h + 1, 1 - par, t // 2, t % 2)
                                if t:
                                    attend(h, t - 1, par)
                                elif not first:
                                    attend(h - 1, TT - 1, 1 - par)
                                if t == 2 and not first:
                                    output(h - 1, 1 - par)

                        for acc in ACC:
                            pe.matmul(acc[:], ones[0:1, :], obr[:], start=True, stop=False,
                                      skip_group_check=True)
                        for t in range(TT):
                            scores(0, t)
                        for b in range(NB):
                            for half in range(2):
                                values(0, 0, b, half)
                        step(0, 0, first=True)
                        pe.wait_ge(sem("o_split"), H // 2)
                        step(1, 1)
                        with pe.Fori(1, H // 2 - 1) as g:
                            step(2 * g, 0)
                            step(2 * g + 1, 1)
                        step(H - 2, 0)
                        step(H - 1, 1, last=True)
                        attend(H - 1, TT - 1, 1)
                        output(H - 1, 1)

                    @block.scalar
                    def _(act):
                        def v_high(h, par, b):
                            act.wait_ge(sem("b_vfull"), 2 * h + b + 1)
                            act.wait_ge(sem("b_ofull"), 4 * h + 1)
                            act.activation(V[:, par, 0, b * KC:(b + 1) * KC, :].rearrange("p c n -> p (c n)"),
                                           VB[:], ACT.Copy).then_inc(sem("b_vhigh"), 1)

                        def exp(h, t):
                            n = 4 * h + t
                            act.wait_ge(sem("b_nm"), n + 1)
                            for s, (c0, w) in enumerate(SEG):
                                act.activation(X[:, t, c0:c0 + w], X[:, t, c0:c0 + w], ACT.Exp,
                                               bias=nm[:, t, s:s + 1], scale=rq[:, t:t + 1],
                                               accum_out=den[:, t, s:s + 1]).then_inc(sem("b_exp"), 1)

                        def pt_high(h, t):
                            n = 4 * h + t
                            act.wait_ge(sem("b_tfull"), n + 1)
                            act.wait_ge(sem("b_ofull"), n + 7)
                            act.activation(PT[:, t % 2, 0, :], TB[t % 2][:], ACT.Copy)\
                               .then_inc(sem("b_pthigh"), 1)

                        def o_ready(h):
                            act.wait_ge(sem("b_ofull"), 4 * h + 12)
                            act.wait_ge(sem("b_omm"), h + 1)

                        def o_high(h, par):
                            act.activation(OT[:, par, 0, :], OB[:], ACT.Identity,
                                           bias=vb[:, bass.ds(h, 1)]).then_inc(sem("b_ohigh"), 1)

                        def step(h, par, first=False, last=False):
                            for t in range(TT):
                                out = t == 1 and not first
                                if out:
                                    o_ready(h - 1)
                                pt_high(h, t)
                                if out:
                                    o_high(h - 1, 1 - par)
                                if t == 0:
                                    exp(h, 3)
                                elif not last:
                                    exp(h + 1, t - 1)
                                if t % 2 and not last:
                                    v_high(h + 1, 1 - par, t // 2)

                        act.nop().then_inc(sem("b_ofull"), 8)
                        act.nop().then_inc(sem("b_omm"), 2)
                        for t in range(3):
                            exp(0, t)
                        for b in range(NB):
                            v_high(0, 0, b)
                        step(0, 0, first=True)
                        step(1, 1)
                        with act.Fori(1, H // 2 - 1) as g:
                            step(2 * g, 0)
                            step(2 * g + 1, 1)
                        step(H - 2, 0)
                        step(H - 1, 1, last=True)
                        o_ready(H - 1)
                        o_high(H - 1, 1)

                    @block.vector
                    def _(dve):
                        def top_score(h, t):
                            n = 4 * h + t
                            for s, (c0, w) in enumerate(SEG):
                                dve.tensor_tensor_reduce(X[:, t, c0:c0 + w], SB[t % 2][:, c0:c0 + w],
                                                         rK[:, t // 2, c0:c0 + w], 1.0, LOWEST, ALU.mult,
                                                         ALU.max, mx[:, t, s:s + 1])\
                                   .then_inc(sem("b_max"), 1)
                            dve.wait_ge(sem("b_max"), 2 * n + 6)
                            dve.tensor_scalar(nm[:, t, :], mx[:, t, :], nrq[:, t:t + 1], None, ALU.mult)\
                               .then_inc(sem("b_nm"), 1)

                        def inverse(t):
                            dve.reciprocal(rden[:, t, :], den[:, t, :]).then_inc(sem("b_rden"), 1)

                        def normalise(h, t):
                            n = 4 * h + t
                            t = t % TT
                            dve.wait_ge(sem("b_rden"), n + 1)
                            for s, (c0, w) in enumerate(SEG):
                                last = dve.tensor_scalar(X[:, t, c0:c0 + w], X[:, t, c0:c0 + w],
                                                         rden[:, t, s:s + 1], None, ALU.mult)
                            last.then_inc(sem("b_norm"), 1)

                        def pt_low(h, t):
                            n = 4 * h + t
                            dve.wait_ge(sem("b_pthigh"), n + 1)
                            dve.tensor_tensor(PT[:, t % 2, 1, :], TB[t % 2][:], PT[:, t % 2, 0, :],
                                              ALU.subtract).then_inc(sem("b_ptlow"), 1)

                        def v_low(h, par, b):
                            dve.wait_ge(sem("b_vhigh"), 2 * h + b + 1)
                            hi, lo = (V[:, par, s, b * KC:(b + 1) * KC, :].rearrange("p c n -> p (c n)")
                                      for s in range(2))
                            dve.tensor_tensor(lo, VB[:], hi, ALU.subtract).then_inc(sem("b_vlow"), 1)

                        def o_low(h, par):
                            dve.wait_ge(sem("b_ohigh"), h + 1)
                            dve.scalar_tensor_tensor(out=OT[:, par, 1, :], in0=OB[:],
                                                     scalar=vb[:, bass.ds(h, 1)], in1=OT[:, par, 0, :],
                                                     op0=ALU.add, op1=ALU.subtract)\
                               .then_inc(sem("b_olow"), 1)

                        def step(h, par, first=False, last=False):
                            for t in range(TT):
                                if not last:
                                    dve.wait_ge(sem("b_sfull"), 4 * (h + 1) + t + 1)
                                pt_low(h, t)
                                if not last:
                                    top_score(h + 1, t)
                                if not (last and t):
                                    dve.wait_ge(sem("b_exp"), 2 * (4 * h + t + 3) + 2)
                                    inverse((t + 3) % 4)
                                    normalise(h, t + 3)
                                if t == 1 and not first:
                                    o_low(h - 1, 1 - par)
                                if t % 2 and not last:
                                    v_low(h + 1, 1 - par, t // 2)

                        dve.nop().then_inc(sem("b_max"), 4)
                        for credit, n in (("b_ptlow", 2), ("b_vlow", 1), ("b_olow", 1)):
                            dve.nop().then_inc(sem(credit), n)
                        for t in range(TT):
                            dve.wait_ge(sem("b_sfull"), t + 1)
                            top_score(0, t)
                        for t in range(3):
                            dve.wait_ge(sem("b_exp"), 2 * t + 2)
                            inverse(t)
                            normalise(0, t)
                        for b in range(NB):
                            v_low(0, 0, b)
                        step(0, 0, first=True)
                        step(1, 1)
                        with dve.Fori(1, H // 2 - 1) as g:
                            step(2 * g, 0)
                            step(2 * g + 1, 1)
                        step(H - 2, 0)
                        step(H - 1, 1, last=True)
                        o_low(H - 1, 1)
                        dve.wait_ge(sem("b_omm"), H + 2)
                        for i in range(2):
                            xs = x[:, 2 * i:2 * i + 2, :].rearrange("p t d -> p (t d)")
                            dve.tensor_tensor(xs, ACC[i][:], xs, ALU.add).then_inc(sem("residual"), 1)


        with ExitStack() as ph:
            s_ = tensors(ph, "moe")
            mG = s_("mG", [P, KT, MT * P])
            mU = s_("mU", [P, KT, MT * P])
            mD = s_("mD", [P, MT, D])
            WG = s_("WG", [P, 2, 2, 2, KT, P], F16)
            WD = s_("WD", [P, 4, 2, D], F16)
            si = s_("si", [P, 2, TOK])
            su_ = s_("su", [P, 2, TOK])
            it = s_("it", [P, 2, TOK])
            IN = s_("IN", [P, 4, 2, TOK], F16)
            zero = s_("zero", [P, P], F16)
            rrow = s_("rrow", [E, D])
            rT = s_("rT", [P, KT, EG])
            rTS = s_("rTS", [P, 2, KT, EG], F16)
            before = s_("before", [P, E * E])
            owner = s_("owner", [EG, MT * P], F16)
            lg = s_("lg", [P, TT, EG])
            ex = s_("ex", [P, TT, EG])
            pr_ = s_("pr", [P, TT, E])
            g1 = s_("g1", [P, TT, E * E])
            g2 = s_("g2", [P, TT, E * E])
            rank = s_("rank", [P, TT, E])
            comb = s_("comb", [P, TT, EG])
            v1 = s_("v1", [P, TT])
            v2 = s_("v2", [P, TT])
            combT = s_("combT", [EG, 2, TOK], F16)
            GB, UB, CB, ACC = (bank[0], bank[2]), (bank[1], bank[3]), bank[4:6], bank[6:8]
            RT, LB, CT, LNB = bank[4], bank[5], bank[4], bank[0:2]
            EPG = 4
            GCOL = EPG * IM
            NGRP = E // EPG + 1
            group_of = [min((j * P + P - 1) // GCOL, NGRP - 1) for j in range(MT)]

            with nc.Block() as block:
                @block.sync
                def _(sync):
                    sync.dma_start(rrow[:], a["L1_ffn_router_w"]).then_inc(sem("in_router"), 16)
                    for k in range(KT):
                        sync.dma_start(rT[:, k, E:EG], a["L1_ffn_sh_gate_w"][k * P:(k + 1) * P, :],
                                       allow_slow_non_contiguous=True).then_inc(sem("in_router"), 16)
                    sync.dma_start(before[:], a["before"]).then_inc(sem("in_before"), 16)
                    sync.dma_start(owner[:], a["owner"]).then_inc(sem("in_owner"), 16)
                    for g in range(NGRP):
                        arrived = sem(f"in_moe{g}")
                        for k in range(KT):
                            for dst, w in ((mG, "gate"), (mU, "up")):
                                rows = slice(k * P, (k + 1) * P)
                                if g < E // EPG:
                                    sync.dma_start(
                                        dst[:, k, g * GCOL:(g + 1) * GCOL].rearrange("p (e i) -> p e i", i=IM),
                                        a[f"L1_ffn_w_{w}"][g * EPG:(g + 1) * EPG, rows, :]
                                        .rearrange("e p i -> p e i")).then_inc(arrived, 16)
                                else:
                                    sync.dma_start(dst[:, k, E * IM:MROWS], a[f"L1_ffn_sh_{w}"][rows, :])\
                                        .then_inc(arrived, 16)
                        tiles = [j for j in range(MT) if group_of[j] == g]
                        j0, j1 = tiles[0], tiles[-1] + 1
                        if g < E // EPG:
                            sync.dma_start(mD[:, j0:j1, :], a["L1_ffn_w_down"].rearrange(
                                "e i d -> (e i) d").rearrange("(t p) d -> p t d", p=P)[:, j0:j1, :])\
                                .then_inc(arrived, 16)
                        else:
                            sync.dma_start(mD[:, j0:j1 - 1, :], a["L1_ffn_sh_down"][0:(j1 - 1 - j0) * P, :]
                                           .rearrange("(t p) d -> p t d", p=P)).then_inc(arrived, 16)
                            sync.dma_start(mD[0:MLAST, j1 - 1, :],
                                           a["L1_ffn_sh_down"][(j1 - 1 - j0) * P:ISH, :]).then_inc(arrived, 16)
                    sync.wait_ge(sem("residual"), 8)
                    sync.dma_start(a["out"].rearrange("b (t p) d -> p (b t) d", p=P), x[:])\
                        .then_inc(sem("out"), 16)
                    sync.wait_ge(sem("out"), 16)

                @block.gpsimd
                def _(pool):
                    pool.memset(zero[:], 0.0).then_inc(sem("m_zero"), 1)
                    for w in (mG, mU):
                        pool.memset(w[:, :, MROWS:MT * P], 0.0).then_inc(sem("m_zero"), 1)
                    pool.wait_ge(sem("m_zero"), 3)
                    pool.memset(mD[MLAST:P, MT - 1, :], 0.0).then_inc(sem("m_zero"), 1)
                    pool.nop().then_inc(sem("m_ilow"), 2)
                    pool.wait_ge(sem("m_zero"), 4)

                    def split(j):
                        if j == 0 or group_of[j] != group_of[j - 1]:
                            g = group_of[j]
                            pool.wait_ge(sem(f"in_moe{g}"), 16 * (5 if g < E // EPG else 6))
                        if j >= 2:
                            pool.wait_ge(sem("m_gu"), j - 1)
                        if j >= 4:
                            pool.wait_ge(sem("m_dn"), j - 3)
                        cols = slice(j * P, (j + 1) * P)
                        srcs = [(WG[:, j % 2, :, m], w[:, :, cols]) for m, w in enumerate((mG, mU))]
                        for m, (dst, src) in enumerate(srcs):
                            pool.tensor_copy(dst[:, 0], src).then_inc(sem("m_whi"), 1)
                        pool.tensor_copy(WD[:, j % 4, 0, :], mD[:, j, :]).then_inc(sem("m_whi"), 1)
                        for m, (dst, src) in enumerate(srcs):
                            pool.wait_ge(sem("m_whi"), 3 * j + m + 1)
                            pool.tensor_tensor(dst[:, 1], src, dst[:, 0], ALU.subtract)\
                                .then_inc(sem("m_wlo"), 1)
                        pool.wait_ge(sem("m_whi"), 3 * j + 3)
                        pool.tensor_tensor(WD[:, j % 4, 1, :], mD[:, j, :], WD[:, j % 4, 0, :],
                                           ALU.subtract).then_inc(sem("m_wlo"), 1)

                    def in_low(j):
                        pool.wait_ge(sem("m_ihigh"), j + 1)
                        pool.tensor_tensor(IN[:, j % 4, 1, :], it[:, j % 2, :], IN[:, j % 4, 0, :],
                                           ALU.subtract).then_inc(sem("m_ilow"), 1)

                    ln_pool(pool, 3)
                    pool.wait_ge(sem("m_rT"), 1)
                    pool.wait_ge(sem("in_router"), 48)
                    pool.tensor_copy(rTS[:, 0], rT[:]).then_inc(sem("m_router"), 1)
                    pool.wait_ge(sem("m_router"), 1)
                    pool.tensor_tensor(rTS[:, 1], rT[:], rTS[:, 0], ALU.subtract).then_inc(sem("m_router"), 1)
                    split(0)
                    split(1)
                    split(2)
                    for j in range(MT):
                        in_low(j)
                        if j + 3 < MT:
                            split(j + 3)

                @block.tensor
                def _(pe):
                    pe.wait_ge(sem("m_zero"), 1)
                    for acc in ACC:
                        pe.matmul(acc[:], zero[:], xT[:, 0, 0, :], start=True, stop=False,
                                  skip_group_check=True)
                    pe.wait_ge(sem("in_router"), 48)
                    for k in range(KT):
                        last = pe.transpose(RT[:, k * E:(k + 1) * E], rrow[:, k * P:(k + 1) * P],
                                            ident[0:E, 0:E])
                    last.then_inc(sem("m_rt"), 1)
                    ln_tensor(pe, 3, LNB)
                    pe.wait_ge(sem("m_router"), 2)
                    pe.wait_ge(sem("ln_lo"), 4 * KT)
                    for t in range(TT):
                        n = 0
                        for k in range(KT):
                            for l, r in PASSES:
                                last = pe.matmul(LB[:, t * EG:(t + 1) * EG], xT[:, l, k, t * P:(t + 1) * P],
                                                 rTS[:, r, k, :], start=(n == 0), stop=(n == 5))
                                n += 1
                    last.then_inc(sem("m_logits"), 1)

                    def gate_up(j, u):
                        pe.wait_ge(sem("m_wlo"), 3 * j + 3)
                        pe.wait_ge(sem("m_uread"), j + 1)
                        for m, out in enumerate((GB[u % 2], UB[u % 2])):
                            n = 0
                            for k in range(KT):
                                for l, r in PASSES:
                                    last = pe.matmul(out[:], WG[:, u % 2, l, m, k, :], xT[:, r, k, :],
                                                     start=(n == 0), stop=(n == 5))
                                    n += 1
                        last.then_inc(sem("m_gu"), 1)

                    def spread(j, u):
                        pe.wait_ge(sem("m_cread"), j + 1)
                        for r in range(2):
                            last = pe.matmul(CB[u % 2][:], owner[:, bass.ds(j * P, P)], combT[:, r, :],
                                             start=(r == 0), stop=(r == 1))
                        last.then_inc(sem("m_c"), 1)

                    def down(j, u):
                        pe.wait_ge(sem("m_ilow"), j + 3)
                        for t in range(TT):
                            for l, r in PASSES:
                                last = pe.matmul(ACC[t // 2][:, (t % 2) * D:(t % 2 + 1) * D],
                                                 IN[:, u % 4, l, t * P:(t + 1) * P], WD[:, u % 4, r, :],
                                                 start=False, stop=False, skip_group_check=True)
                        last.then_inc(sem("m_dn"), 1)

                    gate_up(0, 0)
                    gate_up(1, 1)
                    pe.wait_ge(sem("in_owner"), 16)
                    pe.wait_ge(sem("m_comb"), 1)
                    for t in range(TT):
                        last = pe.transpose(CT[0:EG, t * P:(t + 1) * P], comb[:, t, :], ident[:])
                    last.then_inc(sem("m_combT"), 1)
                    pe.wait_ge(sem("m_comblo"), 1)
                    spread(0, 0)
                    spread(1, 1)
                    with pe.Fori(0, 6) as g:
                        for u in range(1, 5):
                            gate_up(4 * g + u + 1, u + 1)
                            spread(4 * g + u + 1, u + 1)
                            down(4 * g + u - 1, u - 1)
                    for i in range(25, MT + 1):
                        if i + 1 < MT:
                            gate_up(i + 1, i + 1)
                            spread(i + 1, i + 1)
                        down(i - 1, i - 1)

                @block.scalar
                def _(act):
                    ln_scalar(act, 3, LNB)
                    act.wait_ge(sem("m_z"), 2)
                    act.activation(ex[:], lg[:], ACT.Exp).then_inc(sem("m_exp"), 1)
                    act.wait_ge(sem("m_combT"), 1)
                    act.activation(combT[:, 0, :], CT[0:EG, :], ACT.Copy).then_inc(sem("m_combhi"), 1)

                    def silu(j, u):
                        act.wait_ge(sem("m_gu"), j + 1)
                        act.activation(si[:, u % 2, :], GB[u % 2][:], ACT.Silu).then_inc(sem("m_silu"), 1)

                    def in_high(j, u):
                        act.wait_ge(sem("m_cread"), j + 3)
                        act.activation(IN[:, u % 4, 0, :], it[:, u % 2, :], ACT.Copy)\
                           .then_inc(sem("m_ihigh"), 1)

                    silu(0, 0)
                    in_high(0, 0)
                    silu(1, 1)
                    in_high(1, 1)
                    with act.Fori(0, 6) as g:
                        for u in range(1, 5):
                            silu(4 * g + u + 1, u + 1)
                            in_high(4 * g + u + 1, u + 1)
                    for i in range(25, MT - 1):
                        silu(i + 1, i + 1)
                        in_high(i + 1, i + 1)

                @block.vector
                def _(dve):
                    dve.nop().then_inc(sem("m_uread"), 2)
                    dve.nop().then_inc(sem("m_cread"), 2)
                    ln_vector(dve, 3)
                    dve.wait_ge(sem("m_rt"), 1)
                    dve.tensor_copy(rT[:, :, 0:E], RT[:, 0:KT * E].rearrange("p (k e) -> p k e", e=E))\
                       .then_inc(sem("m_rT"), 1)
                    ln_vector_low(dve, 3, LNB)

                    links = [0]

                    def link(ins):
                        links[0] += 1
                        ins.then_inc(sem("m_link"), 1)
                        dve.wait_ge(sem("m_link"), links[0])

                    def of_row(ap, n):
                        return ap.rearrange("p (t o) -> p t o", o=1).to_broadcast([P, TT, n])

                    dve.wait_ge(sem("m_logits"), 1)
                    logits = LB[:, 0:TT * EG].rearrange("p (t e) -> p t e", e=EG)
                    link(dve.tensor_reduce(v1[:], logits[:, :, 0:E], AX, ALU.max))
                    dve.tensor_tensor(lg[:, :, 0:E], logits[:, :, 0:E], of_row(v1[:], E), ALU.subtract)\
                       .then_inc(sem("m_z"), 1)
                    dve.tensor_scalar(lg[:, :, E:EG], logits[:, :, E:EG], -1.0, None, ALU.mult)\
                       .then_inc(sem("m_z"), 1)
                    dve.wait_ge(sem("m_exp"), 1)
                    link(dve.tensor_reduce(v2[:], ex[:, :, 0:E], AX, ALU.add))
                    link(dve.reciprocal(v1[:], v2[:]))
                    link(dve.tensor_tensor(pr_[:], ex[:, :, 0:E], of_row(v1[:], E), ALU.mult))
                    shape = [P, E, E]
                    dve.wait_ge(sem("in_before"), 16)
                    for t in range(TT):
                        others = pr_[:, t, :].rearrange("p (o j) -> p o j", o=1).to_broadcast(shape)
                        own = pr_[:, t, :].rearrange("p (e o) -> p e o", o=1).to_broadcast(shape)
                        grid = [x_[:, t, :].rearrange("p (e j) -> p e j", j=E) for x_ in (g1, g2)]
                        dve.tensor_tensor(grid[0], others, own, ALU.is_gt).then_inc(sem("m_grid"), 1)
                        dve.tensor_tensor(grid[1], others, own, ALU.is_equal).then_inc(sem("m_grid"), 1)
                    for t in range(TT):
                        dve.wait_ge(sem("m_grid"), 2 * t + 2)
                        dve.tensor_tensor(g2[:, t, :], g2[:, t, :], before[:], ALU.mult)\
                           .then_inc(sem("m_tie"), 1)
                    dve.wait_ge(sem("m_tie"), TT)
                    link(dve.tensor_tensor(g1[:], g1[:], g2[:], ALU.add))
                    link(dve.tensor_reduce(rank[:], g1[:].rearrange("p t (e j) -> p (t e) j", j=E), AX,
                                           ALU.add))
                    link(dve.scalar_tensor_tensor(out=pr_[:], in0=rank[:], scalar=float(TOPK), in1=pr_[:],
                                                  op0=ALU.is_lt, op1=ALU.mult))
                    link(dve.tensor_reduce(v2[:], pr_[:], AX, ALU.add))
                    link(dve.tensor_scalar(v2[:], v2[:], 1e-9, None, ALU.max))
                    link(dve.reciprocal(v1[:], v2[:]))
                    link(dve.tensor_scalar(ex[:, :, E:EG], ex[:, :, E:EG], 1.0, None, ALU.add))
                    link(dve.reciprocal(comb[:, :, E:EG], ex[:, :, E:EG]))
                    dve.tensor_tensor(comb[:, :, 0:E], pr_[:], of_row(v1[:], E), ALU.mult)\
                       .then_inc(sem("m_comb"), 1)
                    dve.wait_ge(sem("m_combhi"), 1)
                    dve.tensor_tensor(combT[:, 1, :], CT[0:EG, :], combT[:, 0, :], ALU.subtract)\
                       .then_inc(sem("m_comblo"), 1)

                    def gated(j, u):
                        dve.wait_ge(sem("m_silu"), j + 1)
                        dve.tensor_tensor(su_[:, u % 2, :], UB[u % 2][:], si[:, u % 2, :], ALU.mult)\
                           .then_inc(sem("m_uread"), 1)
                        dve.wait_ge(sem("m_uread"), j + 3)
                        dve.wait_ge(sem("m_c"), j + 1)
                        dve.wait_ge(sem("m_ilow"), j + 1)
                        dve.tensor_tensor(it[:, u % 2, :], CB[u % 2][:], su_[:, u % 2, :], ALU.mult)\
                           .then_inc(sem("m_cread"), 1)

                    gated(0, 0)
                    gated(1, 1)
                    with dve.Fori(0, 6) as g:
                        for u in range(1, 5):
                            gated(4 * g + u + 1, u + 1)
                    for i in range(25, MT - 1):
                        gated(i + 1, i + 1)
                    dve.wait_ge(sem("m_dn"), MT)
                    for i in range(2):
                        xs = x[:, 2 * i:2 * i + 2, :].rearrange("p t d -> p (t d)")
                        dve.tensor_tensor(xs, ACC[i][:], xs, ALU.add).then_inc(sem("residual"), 1)



def constants():
    half = R // 2
    inv = (np.float32(1.0) / np.power(np.float32(10000.0),
                                      np.arange(half, dtype=np.float32) / np.float32(half))).astype(np.float32)
    ang = (np.arange(SK, dtype=np.float32)[:, None] * inv).astype(np.float32).T
    cos = np.ones((P, SK), np.float32)
    sin = np.zeros((P, SK), np.float32)
    cos[KVC:KVC + half] = cos[KVC + half:] = np.cos(ang)
    sin[KVC:KVC + half] = -np.sin(ang)
    sin[KVC + half:] = np.sin(ang)
    rows = np.minimum(np.arange(MT * P) // IM, E)
    return {
        "ident": np.eye(P, dtype=np.float32),
        "kidx": np.broadcast_to(np.arange(SK, dtype=np.float32), (P, SK)).copy(),
        "cos": cos, "sin": sin,
        "owner": (np.arange(EG)[:, None] == rows[None, :]).astype(np.float16),
        "before": np.broadcast_to((np.arange(E)[None, :] < np.arange(E)[:, None]).astype(np.float32)
                                  .reshape(1, E * E), (P, E * E)).copy(),
    }


def kernel(**inputs):
    import concourse.bacc as _bacc
    from concourse.bass_utils import run_bass_kernel_spmd as _run

    nc = _bacc.Bacc("TRN2", target_bir_lowering=False, num_devices=1)
    arrays, aps = {}, {}
    for name, v in [*inputs.items(), *constants().items()]:
        v = np.ascontiguousarray(v)
        arrays[f"in_{name}"] = v
        aps[name] = nc.dram_tensor(f"in_{name}", v.shape, mybir.dt.from_np(v.dtype), kind="ExternalInput").ap()
    aps["out"] = nc.dram_tensor("out_0", (NB, SQ, D), F32, kind="ExternalOutput").ap()
    build(nc, aps)
    r = _run(nc, [arrays], core_ids=[0])
    return r.results[0]["out_0"]
```

```python
from contextlib import ExitStack

import numpy as np

import concourse.bass as bass
from concourse import mybir

ALU = mybir.AluOpType
ACT = mybir.ActivationFunctionType
AX = mybir.AxisListType.X
F32 = mybir.dt.float32
F16 = mybir.dt.float16
F8 = mybir.dt.float8e4
I32 = mybir.dt.int32

P = 128
D = 256
KT = D // P
NB = 2
SQ = 256
SK = 512
TOK = NB * SQ
TT = TOK // P
KC = SK // P
H = 16
HD = 128
NEG = -1e30
LOWEST = -3.0e38

KVC, QC, R = 64, 96, 64
LOOKBACK = 8
SCALE0 = float(1.0 / np.sqrt(HD + R).astype(np.float32))

FT = 2048 // P
PK = 3 * P
BLK = 24

NIMG = 257
NTXT = SK - NIMG
SEG = ((0, NIMG), (NIMG, NTXT))
INNER = H * HD
SCALE1 = float(HD) ** -0.5

E, TOPK, IM, ISH = 16, 4, 176, 704
EG = E + 1
MROWS = E * IM + ISH
MT = (MROWS + P - 1) // P
MLAST = MROWS - (MT - 1) * P

PASSES = ((0, 0), (0, 1), (1, 0))


def build(nc, a):
    top = ExitStack()
    with top:
        sems = {}

        def sem(name):
            if name not in sems:
                sems[name] = top.enter_context(nc.semaphore(name))
            return sems[name]

        def tensors(stack, part="all"):
            return lambda name, shape, dt=F32: stack.enter_context(
                nc.sbuf_tensor(f"{part}_{name}", shape, dt))

        sb = tensors(top)
        bank = [top.enter_context(nc.psum_tensor(f"bank{i}", [P, 512], F32)) for i in range(8)]

        ident = sb("ident", [P, P])
        x = sb("x", [P, TT, D])
        xT = sb("xT", [P, 2, KT, TOK], F16)
        ctxT = sb("ctxT", [P, 2, KT, NB * SK], F16)
        ctxM = sb("ctxM", [P, 2, KT, NB, 2, P], F16)
        ln_st = sb("ln_st", [P, TT, 6])
        ln_mv = sb("ln_mv", [P, TT, 2])
        ln_ve = sb("ln_ve", [P, TT])
        ln_rs = sb("ln_rs", [P, TT])
        ln_x = sb("ln_x", [P, TT, D])
        mhalf = sb("mhalf", [P, 16])
        pk = top.enter_context(ExitStack())
        packed = tensors(pk)("packed", [P, FT, PK], I32)
        pscale = tensors(pk)("pscale", [P, FT + 1, BLK])

        def ln_vector(dve, n):
            for t in range(TT):
                dve.bn_stats(ln_st[:, t, :], x[:, t, :]).then_inc(sem("ln_stats"), 1)
            for t in range(TT):
                dve.wait_ge(sem("ln_stats"), TT * n + t + 1)
                dve.bn_aggr(ln_mv[:, t, :], ln_st[:, t, :]).then_inc(sem("ln_aggr"), 1)
            dve.wait_ge(sem("ln_aggr"), TT * n + TT)
            dve.tensor_scalar(ln_ve[:], ln_mv[:, :, 1], 1e-5, None, ALU.add).then_inc(sem("ln_var"), 1)
            dve.wait_ge(sem("ln_rstd"), n + 1)
            for t in range(TT):
                dve.tensor_scalar(ln_x[:, t, :], x[:, t, :], ln_mv[:, t, 0:1], ln_rs[:, t:t + 1],
                                  ALU.subtract, ALU.mult).then_inc(sem("ln_x"), 1)

        def ln_pool(pool, n):
            pool.wait_ge(sem("ln_var"), n + 1)
            pool.tensor_tensor(ln_rs[:], ln_ve[:], mhalf[:, 0:TT], ALU.pow).then_inc(sem("ln_rstd"), 1)

        def ln_tensor(pe, n, banks):
            for t in range(TT):
                pe.wait_ge(sem("ln_x"), TT * n + t + 1)
                for k in range(KT):
                    last = pe.transpose(banks[k][:, t * P:(t + 1) * P], ln_x[:, t, k * P:(k + 1) * P], ident[:])
            last.then_inc(sem("ln_T"), 1)

        def ln_scalar(act, n, banks):
            act.wait_ge(sem("ln_T"), n + 1)
            for k in range(KT):
                act.activation(xT[:, 0, k, :], banks[k][:], ACT.Copy).then_inc(sem("ln_hi"), 1)

        def ln_vector_low(dve, n, banks):
            for k in range(KT):
                dve.wait_ge(sem("ln_hi"), KT * n + k + 1)
                dve.tensor_tensor(xT[:, 1, k, :], banks[k][:], xT[:, 0, k, :], ALU.subtract)\
                   .then_inc(sem("ln_lo"), 1)

        with ExitStack() as ph:
            sp = tensors(ph, "l0")
            Aq = sp("Aq", [QC, 2, H, P], F16)
            As = sp("As", [QC, 2, H, P], F16)
            qcT = sp("qcT", [QC, 2, TOK], F16)
            kF = sp("kF", [P, 2, NB * SK], F16)
            kv = sp("kv", [P, 2, NB * KC, KVC], F16)
            M = sp("M", [P, 2, H // 2, D], F16)
            mask = sp("mask", [P, TT, SK])
            cosT = sp("cosT", [P, SK])
            sinT = sp("sinT", [P, SK])

            def q_table(tab):
                return tab[:, 0:SQ].rearrange("p (b q) -> p b q", b=1).to_broadcast([P, NB, SQ])

            def by_batch(ap):
                return ap.rearrange("p (b q) -> p b q", b=NB)

            with ExitStack() as su:
                ss = tensors(su, "setup")
                ctx = ss("ctx", [P, NB * KC, D])
                wkvc = ss("wkvc", [P, KT, KVC])
                wdq = ss("wdq", [P, KT, QC])
                wkvcS = ss("wkvcS", [P, 2, KT, KVC], F16)
                wdqS = ss("wdqS", [P, 2, KT, QC], F16)
                wkr = ss("wkr", [KVC, 2, P])
                wuq = ss("wuq", [QC, H * HD])
                wqr = ss("wqr", [QC, H, R])
                wuk = ss("wuk", [KVC, H * HD])
                wuv = ss("wuv", [KVC, H * HD])
                wo = ss("wo", [P, H, D])
                uqT = ss("uqT", [P, H, QC])
                ukT = ss("ukT", [P, H, KVC])
                uvT = ss("uvT", [P, H, KVC])
                kvcT = ss("kvcT", [KVC, NB, SK])
                kidx = ss("kidx", [P, SK])
                segi = ss("segi", [P, TT], I32)
                segf = ss("segf", [P, TT])
                mtmp = ss("mtmp", [P, SK])
                rc = ss("rc", [P, 2, SK])
                rs = ss("rs", [P, 2, SK])
                rk = ss("rk", [P, 2, SK])

                J_CTX, J_UQ, J_UK, J_UV, J_KVT, J_KV, J_A, J_M, J_K, J_X, J_QC, J_END = \
                    0, 4, 8, 10, 12, 14, 15, 17, 21, 25, 27, 28

                def fill(pe, j):
                    if j >= 8:
                        pe.wait_ge(sem("su_read"), j - 7)
                    return bank[j % 8]

                with nc.Block() as block:
                    @block.sync
                    def _(sync):
                        def load(name, dst, src):
                            sync.dma_start(dst, src).then_inc(sem("in_" + name), 16)
                        load("ident", ident[:], a["ident"])
                        load("x", x[:], a["x"].rearrange("b (t p) d -> p (b t) d", p=P))
                        load("ctx", ctx[:], a["ctx_2048"].rearrange("b (t p) d -> p (b t) d", p=P))
                        load("wuq", wuq[:], a["L0_xattn_W_uq"])
                        load("wuk", wuk[:], a["L0_xattn_W_uk"])
                        load("wuv", wuv[:], a["L0_xattn_W_uv"])
                        load("proj", wkvc[:], a["L0_xattn_W_kvc"].rearrange("(k p) n -> p k n", p=P))
                        load("proj", wdq[:], a["L0_xattn_W_dq"].rearrange("(k p) n -> p k n", p=P))
                        load("wqr", wqr[:], a["L0_xattn_W_qr"].rearrange("c (h r) -> c h r", r=R))
                        sync.dma_start(segi[:], a["itok_BxS_0_1023"].rearrange("b (t p) -> p (b t)", p=P),
                                       allow_slow_non_contiguous=True).then_inc(sem("in_tables"), 16)
                        load("tables", kidx[:], a["kidx"])
                        load("wkr", wkr[:, 0, 0:KVC], a["ident"][0:KVC, 0:KVC])
                        load("wkr", wkr[:, 0, KVC:P], a["L0_xattn_W_kr"])
                        load("wkr", wkr[:, 1, KVC:KVC + R // 2], a["L0_xattn_W_kr"][:, R // 2:R])
                        load("wkr", wkr[:, 1, KVC + R // 2:P], a["L0_xattn_W_kr"][:, 0:R // 2])
                        load("tables", cosT[:], a["cos"])
                        load("tables", sinT[:], a["sin"])
                        load("wo", wo[:], a["L0_xattn_W_o"].rearrange("(h p) n -> p h n", p=P))
                        for n, w in enumerate(("gate", "up")):
                            load("packed", packed[:, :, n * P:(n + 1) * P],
                                 a[f"L0_ffn_{w}_W_packed"].rearrange("(t p) k -> p t k", p=P))
                            load("packed", pscale[:, 0:FT, n * 8:n * 8 + 8],
                                 a[f"L0_ffn_{w}_scales"].rearrange("(t p) k -> p t k", p=P))
                        for m in range(KT):
                            load("packed", packed[:, :, 2 * P + m * 64:2 * P + m * 64 + 64],
                                 a["L0_ffn_down_W_packed"][m * P:(m + 1) * P, :]
                                 .rearrange("p (t k) -> p t k", t=FT))
                            load("packed", pscale[:, 0:FT, 16 + 4 * m:20 + 4 * m],
                                 a["L0_ffn_down_scales"][m * P:(m + 1) * P, :]
                                 .rearrange("p (t k) -> p t k", t=FT))

                    @block.gpsimd
                    def _(pool):
                        pool.memset(mhalf[:], -0.5).then_inc(sem("half"), 1)
                        pool.memset(pscale[:, FT, :], 0.0).then_inc(sem("half"), 1)
                        pool.memset(As[:, :, :, 0:KVC], 0.0).then_inc(sem("half"), 1)
                        pool.memset(wkr[:, 1, 0:KVC], 0.0).then_inc(sem("wkr_zero"), 1)
                        pool.memset(ctxM[:], 0.0).then_inc(sem("ctxM_zero"), 1)
                        pool.wait_ge(sem("half"), 3)
                        ln_pool(pool, 0)
                        pool.wait_ge(sem("in_proj"), 32)
                        pool.tensor_copy(wkvcS[:, 0], wkvc[:]).then_inc(sem("wsplit"), 1)
                        pool.tensor_copy(wdqS[:, 0], wdq[:]).then_inc(sem("wsplit"), 1)
                        pool.wait_ge(sem("wsplit"), 2)
                        pool.tensor_tensor(wkvcS[:, 1], wkvc[:], wkvcS[:, 0], ALU.subtract)\
                            .then_inc(sem("wsplit"), 1)
                        pool.tensor_tensor(wdqS[:, 1], wdq[:], wdqS[:, 0], ALU.subtract)\
                            .then_inc(sem("wsplit"), 1)
                        pool.wait_ge(sem("in_wqr"), 16)
                        hR = R // 2
                        pool.tensor_copy(Aq[:, 0, :, KVC:P], wqr[:]).then_inc(sem("rope_hi"), 1)
                        pool.wait_ge(sem("rope_hi"), 1)
                        pool.tensor_tensor(Aq[:, 1, :, KVC:P], wqr[:], Aq[:, 0, :, KVC:P], ALU.subtract)\
                            .then_inc(sem("rope_hi"), 1)
                        pool.wait_ge(sem("rope_hi"), 2)
                        for part in range(2):
                            pool.tensor_copy(As[:, part, :, KVC:KVC + hR], Aq[:, part, :, KVC + hR:P])\
                                .then_inc(sem("rope_swap"), 1)
                            pool.tensor_copy(As[:, part, :, KVC + hR:P], Aq[:, part, :, KVC:KVC + hR])\
                                .then_inc(sem("rope_swap"), 1)
                        pool.wait_ge(sem("ctxM_zero"), 1)
                        pool.wait_ge(sem("su_read"), J_CTX + 4)
                        for k in range(KT):
                            c = ctxT[:, :, k, :].rearrange("p s (b j) -> p s b j", b=NB)
                            c0 = NIMG - 1
                            for part in range(2):
                                pool.tensor_copy(ctxM[:, part, k, :, 0, 0:1], c[:, part, :, c0:c0 + 1])\
                                    .then_inc(sem("ctxM"), 1)
                                pool.tensor_copy(ctxM[:, part, k, :, 1, 1:P], c[:, part, :, c0 + 1:c0 + P])\
                                    .then_inc(sem("ctxM"), 1)

                    @block.tensor
                    def _(pe):
                        pe.wait_ge(sem("in_ident"), 16)
                        pe.wait_ge(sem("in_ctx"), 16)
                        for k in range(KT):
                            for b in range(NB):
                                out = fill(pe, J_CTX + 2 * k + b)
                                for c in range(KC):
                                    last = pe.transpose(out[:, c * P:(c + 1) * P],
                                                        ctx[:, b * KC + c, k * P:(k + 1) * P], ident[:])
                                last.then_inc(sem("su_full"), 1)
                        pe.wait_ge(sem("in_wuq"), 16)
                        for g in range(4):
                            out = fill(pe, J_UQ + g)
                            for i in range(4):
                                h = 4 * g + i
                                last = pe.transpose(out[:, i * QC:(i + 1) * QC],
                                                    wuq[:, h * HD:(h + 1) * HD], ident[0:QC, 0:QC])
                            last.then_inc(sem("su_full"), 1)
                        for j, w, ready in ((J_UK, wuk, "in_wuk"), (J_UV, wuv, "in_wuv")):
                            pe.wait_ge(sem(ready), 16)
                            for g in range(2):
                                out = fill(pe, j + g)
                                for i in range(8):
                                    h = 8 * g + i
                                    last = pe.transpose(out[:, i * KVC:(i + 1) * KVC],
                                                        w[:, h * HD:(h + 1) * HD], ident[0:KVC, 0:KVC])
                                last.then_inc(sem("su_full"), 1)
                        pe.wait_ge(sem("wsplit"), 4)
                        for b in range(NB):
                            out = fill(pe, J_KVT + b)
                            if b == 0:
                                pe.wait_ge(sem("su_read"), J_CTX + 4)
                            n = 0
                            for k in range(KT):
                                for l, r in PASSES:
                                    last = pe.matmul(out[0:KVC, :], wkvcS[:, l, k, :],
                                                     ctxT[:, r, k, b * SK:(b + 1) * SK],
                                                     start=(n == 0), stop=(n == 5))
                                    n += 1
                            last.then_inc(sem("su_full"), 1)
                        out = fill(pe, J_KV)
                        for c in range(NB * KC):
                            n = 0
                            for k in range(KT):
                                for l, r in PASSES:
                                    last = pe.matmul(out[:, c * KVC:(c + 1) * KVC],
                                                     ctxT[:, l, k, c * P:(c + 1) * P], wkvcS[:, r, k, :],
                                                     start=(n == 0), stop=(n == 5))
                                    n += 1
                        last.then_inc(sem("su_full"), 1)
                        pe.wait_ge(sem("su_read"), J_UK + 2)
                        for g in range(2):
                            out = fill(pe, J_A + g)
                            for i in range(8):
                                h = 8 * g + i
                                last = pe.matmul(out[0:QC, i * KVC:(i + 1) * KVC], uqT[:, h, :], ukT[:, h, :],
                                                 start=True, stop=True)
                            last.then_inc(sem("su_full"), 1)
                        pe.wait_ge(sem("in_wo"), 16)
                        pe.wait_ge(sem("su_read"), J_UV + 2)
                        for g in range(4):
                            out = fill(pe, J_M + g)
                            for i in range(4):
                                h = 4 * g + i
                                lo = (h % 2) * KVC
                                last = pe.matmul(out[lo:lo + KVC, (i // 2) * D:(i // 2 + 1) * D],
                                                 uvT[:, h, :], wo[:, h, :], start=True, stop=True)
                            last.then_inc(sem("su_full"), 1)
                        pe.wait_ge(sem("in_wkr"), 64)
                        pe.wait_ge(sem("wkr_zero"), 1)
                        pe.wait_ge(sem("su_read"), J_KVT + 2)
                        for b in range(NB):
                            for s in range(2):
                                out = fill(pe, J_K + 2 * b + s)
                                pe.matmul(out[:, :], wkr[:, s, :], kvcT[:, b, :], start=True, stop=True)\
                                  .then_inc(sem("su_full"), 1)
                        fill(pe, J_X)
                        ln_banks = [bank[(J_X + k) % 8] for k in range(KT)]
                        fill(pe, J_X + 1)
                        ln_tensor(pe, 0, ln_banks)
                        out = fill(pe, J_QC)
                        pe.wait_ge(sem("ln_lo"), KT)
                        n = 0
                        for k in range(KT):
                            for l, r in PASSES:
                                last = pe.matmul(out[0:QC, :], wdqS[:, l, k, :], xT[:, r, k, :],
                                                 start=(n == 0), stop=(n == 5))
                                n += 1
                        last.then_inc(sem("su_full2"), 1)

                    @block.scalar
                    def _(act):
                        def high(j, dst, src):
                            act.wait_ge(sem("su_full"), j + 1)
                            act.activation(dst, src, ACT.Copy).then_inc(sem("su_high"), 1)
                        for k in range(KT):
                            for b in range(NB):
                                high(J_CTX + 2 * k + b, ctxT[:, 0, k, b * SK:(b + 1) * SK],
                                     bank[(J_CTX + 2 * k + b) % 8][:])
                        high(J_KV, kv[:, 0].rearrange("p c n -> p (c n)"), bank[J_KV % 8][:])
                        for g in range(2):
                            high(J_A + g, Aq[:, 0, 8 * g:8 * g + 8, 0:KVC],
                                 bank[(J_A + g) % 8][0:QC, :].rearrange("p (h n) -> p h n", n=KVC))
                        for g in range(4):
                            high(J_M + g, M[:, 0, 2 * g:2 * g + 2, :],
                                 bank[(J_M + g) % 8][:].rearrange("p (h n) -> p h n", n=D))
                        for b in range(NB):
                            act.wait_ge(sem("k_roped"), b + 1)
                            act.activation(kF[:, 0, b * SK:(b + 1) * SK], rk[:, b, :], ACT.Copy)\
                               .then_inc(sem("k_high"), 1)
                        ln_scalar(act, 0, [bank[(J_X + k) % 8] for k in range(KT)])
                        act.wait_ge(sem("su_full2"), 1)
                        act.activation(qcT[:, 0, :], bank[J_QC % 8][0:QC, :], ACT.Copy)\
                           .then_inc(sem("qc_high"), 1)

                    @block.vector
                    def _(dve):
                        n_high = [0]

                        def low(dst, src, high):
                            n_high[0] += 1
                            dve.wait_ge(sem("su_high"), n_high[0])
                            dve.tensor_tensor(dst, src, high, ALU.subtract).then_inc(sem("su_read"), 1)

                        def plain(j, dst, src):
                            dve.wait_ge(sem("su_full"), j + 1)
                            dve.tensor_copy(dst, src).then_inc(sem("su_read"), 1)

                        dve.wait_ge(sem("in_x"), 16)
                        ln_vector(dve, 0)
                        for k in range(KT):
                            for b in range(NB):
                                s = slice(b * SK, (b + 1) * SK)
                                low(ctxT[:, 1, k, s], bank[(J_CTX + 2 * k + b) % 8][:], ctxT[:, 0, k, s])
                        for g in range(4):
                            plain(J_UQ + g, uqT[:, 4 * g:4 * g + 4, :],
                                  bank[(J_UQ + g) % 8][:, 0:4 * QC].rearrange("p (h n) -> p h n", n=QC))
                        for g in range(2):
                            plain(J_UK + g, ukT[:, 8 * g:8 * g + 8, :],
                                  bank[(J_UK + g) % 8][:].rearrange("p (h n) -> p h n", n=KVC))
                        for g in range(2):
                            plain(J_UV + g, uvT[:, 8 * g:8 * g + 8, :],
                                  bank[(J_UV + g) % 8][:].rearrange("p (h n) -> p h n", n=KVC))
                        for b in range(NB):
                            plain(J_KVT + b, kvcT[:, b, :], bank[(J_KVT + b) % 8][0:KVC, :])
                        low(kv[:, 1].rearrange("p c n -> p (c n)"), bank[J_KV % 8][:],
                            kv[:, 0].rearrange("p c n -> p (c n)"))
                        for g in range(2):
                            low(Aq[:, 1, 8 * g:8 * g + 8, 0:KVC],
                                bank[(J_A + g) % 8][0:QC, :].rearrange("p (h n) -> p h n", n=KVC),
                                Aq[:, 0, 8 * g:8 * g + 8, 0:KVC])
                        for g in range(4):
                            low(M[:, 1, 2 * g:2 * g + 2, :],
                                bank[(J_M + g) % 8][:].rearrange("p (h n) -> p h n", n=D),
                                M[:, 0, 2 * g:2 * g + 2, :])
                        dve.wait_ge(sem("in_tables"), 64)
                        for b in range(NB):
                            j = J_K + 2 * b
                            dve.wait_ge(sem("su_full"), j + 2)
                            dve.tensor_tensor(rc[:, b, :], bank[j % 8][:], cosT[:], ALU.mult)\
                               .then_inc(sem("su_read"), 1)
                            dve.tensor_tensor(rs[:, b, :], bank[(j + 1) % 8][:], sinT[:], ALU.mult)\
                               .then_inc(sem("su_read"), 1)
                            dve.wait_ge(sem("su_read"), j + 2)
                            dve.tensor_tensor(rk[:, b, :], rc[:, b, :], rs[:, b, :], ALU.add)\
                               .then_inc(sem("k_roped"), 1)
                        for b in range(NB):
                            s = slice(b * SK, (b + 1) * SK)
                            dve.wait_ge(sem("k_high"), b + 1)
                            dve.tensor_tensor(kF[:, 1, s], rk[:, b, :], kF[:, 0, s], ALU.subtract)\
                               .then_inc(sem("k_low"), 1)
                        dve.tensor_scalar(segf[:], segi[:], -1.0, LOOKBACK / 2, ALU.mult, ALU.add)\
                           .then_inc(sem("segf"), 1)
                        dve.wait_ge(sem("segf"), 1)
                        for t in range(TT):
                            if t:
                                dve.wait_ge(sem("mask"), t)
                            dve.tensor_scalar(mask[:, t, :], kidx[:], segf[:, t:t + 1], None, ALU.add)\
                               .then_inc(sem("mask_dist"), 1)
                            dve.wait_ge(sem("mask_dist"), 2 * t + 1)
                            dve.scalar_tensor_tensor(out=mtmp[:], in0=mask[:, t, :], scalar=-1.0,
                                                     in1=mask[:, t, :], op0=ALU.mult, op1=ALU.max)\
                               .then_inc(sem("mask_dist"), 1)
                            dve.wait_ge(sem("mask_dist"), 2 * t + 2)
                            dve.tensor_scalar(mask[:, t, :], mtmp[:], LOOKBACK / 2, NEG, ALU.is_gt, ALU.mult)\
                               .then_inc(sem("mask"), 1)
                        ln_vector_low(dve, 0, [bank[(J_X + k) % 8] for k in range(KT)])
                        dve.wait_ge(sem("qc_high"), 1)
                        dve.tensor_tensor(qcT[:, 1, :], bank[J_QC % 8][0:QC, :], qcT[:, 0, :], ALU.subtract)\
                           .then_inc(sem("qc_low"), 1)

            with ExitStack() as at:
                s_ = tensors(at, "l0head")
                tc = s_("tc", [P, 2, TOK])
                ts_ = s_("ts", [P, 2, TOK])
                tq = s_("tq", [P, 2, TOK])
                Q = s_("Q", [P, 2, 2, TOK], F16)
                X = s_("X", [P, TT, SK])
                PT = s_("PT", [P, 2, 2, SK], F16)
                mx = s_("mx", [P, TT])
                nm = s_("nm", [P, TT])
                den = s_("den", [P, 2 * TT])
                rden = s_("rden", [P, 2 * TT])
                O = s_("O", [P, TT, H * KVC])
                OT = s_("OT", [P, 2, 2, TOK], F16)
                SB, TB, QA, QS, OB = bank[0:2], bank[2:4], bank[4], bank[5], bank[6:8]
                ACC = bank[4:6]

                with nc.Block() as block:
                    @block.tensor
                    def _(pe):
                        def project(h):
                            pe.wait_ge(sem("a_qread"), 2 * h)
                            for out, w in ((QA, Aq), (QS, As)):
                                for n, (l, r) in enumerate(PASSES):
                                    last = pe.matmul(out[:], w[:, l, bass.ds(h, 1), :], qcT[:, r, :],
                                                     start=(n == 0), stop=(n == 2))
                            last.then_inc(sem("a_qfull"), 1)

                        def scores(h, t, par):
                            if t == 0:
                                pe.wait_ge(sem("a_qlow"), h + 1)
                            n = 4 * h + t
                            pe.wait_ge(sem("a_max"), n + 1)
                            b = t // 2
                            for i, (l, r) in enumerate(PASSES):
                                last = pe.matmul(SB[t % 2][:], Q[:, par, l, t * P:(t + 1) * P],
                                                 kF[:, r, b * SK:(b + 1) * SK], start=(i == 0), stop=(i == 2))
                            last.then_inc(sem("a_sfull"), 1)

                        def turn(h, t):
                            n = 4 * h + t
                            pe.wait_ge(sem("a_exp"), n + 1)
                            pe.wait_ge(sem("a_ptlow"), n + 1)
                            for c in range(KC):
                                last = pe.transpose(TB[t % 2][:, c * P:(c + 1) * P],
                                                    X[:, t, c * P:(c + 1) * P], ident[:])
                            last.then_inc(sem("a_tfull"), 1)

                        def attend(h, t):
                            n = 4 * h + t
                            pe.wait_ge(sem("a_ptlow"), n + 3)
                            pe.wait_ge(sem("a_oread"), n + 1)
                            b = t // 2
                            i = 0
                            for c in range(KC):
                                for l, r in PASSES:
                                    last = pe.matmul(OB[t % 2][:, 0:KVC], PT[:, t % 2, l, c * P:(c + 1) * P],
                                                     kv[:, r, b * KC + c, :], start=(i == 0),
                                                     stop=(i == 3 * KC - 1))
                                    i += 1
                            last.then_inc(sem("a_ofull"), 1)

                        def step(h, par, first=False, last=False, late=False):
                            for t in range(TT):
                                turn(h, t)
                                if not last:
                                    scores(h + 1, t, 1 - par)
                                if t:
                                    attend(h, t - 1)
                                elif not first:
                                    attend(h - 1, TT - 1)
                                if t == 1 and not late:
                                    project(h + 2)

                        project(0)
                        for t in range(TT):
                            scores(0, t, 0)
                        project(1)
                        step(0, 0, first=True)
                        step(1, 1)
                        with pe.Fori(1, H // 2 - 1) as g:
                            step(2 * g, 0)
                            step(2 * g + 1, 1)
                        step(H - 2, 0, late=True)
                        step(H - 1, 1, last=True, late=True)
                        attend(H - 1, TT - 1)

                        def turn_o(j):
                            if j >= 2:
                                pe.wait_ge(sem("a_otlow"), j - 1)
                            for t in range(TT):
                                last = pe.transpose(TB[j % 2][:, t * P:(t + 1) * P],
                                                    O[:, t, j * P:(j + 1) * P], ident[:])
                            last.then_inc(sem("a_otfull"), 1)
                        pe.wait_ge(sem("a_oread"), 4 * H + 2)
                        turn_o(0)
                        for j in range(H // 2):
                            if j + 1 < H // 2:
                                turn_o(j + 1)
                            pe.wait_ge(sem("a_otlow"), j + 1)
                            for t in range(TT):
                                for n, (l, r) in enumerate(PASSES):
                                    last = pe.matmul(ACC[t // 2][:, (t % 2) * D:(t % 2 + 1) * D],
                                                     OT[:, j % 2, l, t * P:(t + 1) * P], M[:, r, j, :],
                                                     start=(j == 0 and n == 0 and t % 2 == 0),
                                                     stop=(j == H // 2 - 1 and n == 2),
                                                     skip_group_check=True)
                            last.then_inc(sem("a_omm"), 1)

                    @block.scalar
                    def _(act):
                        def q_high(h, par):
                            act.wait_ge(sem("a_qsum"), h + 1)
                            act.activation(Q[:, par, 0, :], tq[:, par, :], ACT.Copy).then_inc(sem("a_qhigh"), 1)

                        def exp(h, t, par):
                            n = 4 * h + t
                            act.wait_ge(sem("a_nm"), n + 1)
                            act.activation(X[:, t, :], X[:, t, :], ACT.Exp, bias=nm[:, t:t + 1], scale=SCALE0,
                                           accum_out=den[:, par * TT + t:par * TT + t + 1])\
                               .then_inc(sem("a_exp"), 1)

                        def pt_high(h, t):
                            n = 4 * h + t
                            act.wait_ge(sem("a_tfull"), n + 1)
                            act.wait_ge(sem("a_ofull"), n + 1)
                            act.activation(PT[:, t % 2, 0, :], TB[t % 2][:], ACT.Copy)\
                               .then_inc(sem("a_pthigh"), 1)

                        def step(h, par, last=False, late=False):
                            for t in range(TT):
                                pt_high(h, t)
                                if t == 0:
                                    exp(h, 3, par)
                                elif not last:
                                    exp(h + 1, t - 1, 1 - par)
                                if t == 2 and not late:
                                    q_high(h + 2, par)

                        act.nop().then_inc(sem("a_ofull"), 2)
                        q_high(0, 0)
                        for t in range(3):
                            exp(0, t, 0)
                        q_high(1, 1)
                        step(0, 0)
                        step(1, 1)
                        with act.Fori(1, H // 2 - 1) as g:
                            step(2 * g, 0)
                            step(2 * g + 1, 1)
                        step(H - 2, 0, late=True)
                        step(H - 1, 1, last=True, late=True)
                        for j in range(H // 2):
                            act.wait_ge(sem("a_otfull"), j + 1)
                            if j >= 2:
                                act.wait_ge(sem("a_omm"), j - 1)
                            act.activation(OT[:, j % 2, 0, :], TB[j % 2][:], ACT.Copy)\
                               .then_inc(sem("a_othigh"), 1)

                    @block.gpsimd
                    def _(pool):
                        def q_sum(h, par):
                            pool.wait_ge(sem("a_qread"), 2 * h + 2)
                            pool.tensor_tensor(tq[:, par, :], tc[:, par, :], ts_[:, par, :], ALU.add)\
                                .then_inc(sem("a_qsum"), 1)
                            pool.wait_ge(sem("a_qhigh"), h + 1)
                            pool.tensor_tensor(Q[:, par, 1, :], tq[:, par, :], Q[:, par, 0, :], ALU.subtract)\
                                .then_inc(sem("a_qlow"), 1)
                        with pool.Fori(0, H // 2) as g:
                            q_sum(2 * g, 0)
                            q_sum(2 * g + 1, 1)

                    @block.vector
                    def _(dve):
                        def q_rope(h, par):
                            dve.wait_ge(sem("a_qfull"), h + 1)
                            dve.tensor_tensor(by_batch(tc[:, par, :]), by_batch(QA[:]), q_table(cosT),
                                              ALU.mult).then_inc(sem("a_qread"), 1)
                            dve.tensor_tensor(by_batch(ts_[:, par, :]), by_batch(QS[:]), q_table(sinT),
                                              ALU.mult).then_inc(sem("a_qread"), 1)

                        def top_score(h, t):
                            n = 4 * h + t
                            dve.tensor_tensor_reduce(X[:, t, :], SB[t % 2][:], mask[:, t, :], 1.0, LOWEST,
                                                     ALU.add, ALU.max, mx[:, t:t + 1])\
                               .then_inc(sem("a_max"), 1)
                            dve.wait_ge(sem("a_max"), n + 3)
                            dve.tensor_scalar(nm[:, t:t + 1], mx[:, t:t + 1], -SCALE0, None, ALU.mult)\
                               .then_inc(sem("a_nm"), 1)

                        def pt_low(h, t):
                            n = 4 * h + t
                            dve.wait_ge(sem("a_pthigh"), n + 1)
                            dve.tensor_tensor(PT[:, t % 2, 1, :], TB[t % 2][:], PT[:, t % 2, 0, :],
                                              ALU.subtract).then_inc(sem("a_ptlow"), 1)

                        def o_den(par, t):
                            i = par * TT + t
                            dve.reciprocal(rden[:, i:i + 1], den[:, i:i + 1]).then_inc(sem("a_rden"), 1)

                        def o_out(h, t, par):
                            n = 4 * h + t
                            i = par * TT + t
                            dve.wait_ge(sem("a_ofull"), n + 3)
                            dve.wait_ge(sem("a_rden"), n + 1)
                            dve.tensor_scalar(O[:, t, bass.ds(h * KVC, KVC)], OB[t % 2][:, 0:KVC],
                                              rden[:, i:i + 1], None, ALU.mult).then_inc(sem("a_oread"), 1)

                        def step(h, par, first=False, last=False, late=False):
                            for t in range(TT):
                                if not last:
                                    dve.wait_ge(sem("a_sfull"), 4 * (h + 1) + t + 1)
                                if t:
                                    o_den(par, t - 1)
                                elif not first:
                                    o_den(1 - par, TT - 1)
                                if not last:
                                    top_score(h + 1, t)
                                pt_low(h, t)
                                if t:
                                    o_out(h, t - 1, par)
                                elif not first:
                                    o_out(h - 1, TT - 1, 1 - par)
                                if t == 1 and not late:
                                    q_rope(h + 2, par)

                        for credit in ("a_max", "a_ptlow", "a_oread"):
                            dve.nop().then_inc(sem(credit), 2)
                        q_rope(0, 0)
                        for t in range(TT):
                            dve.wait_ge(sem("a_sfull"), t + 1)
                            top_score(0, t)
                        q_rope(1, 1)
                        step(0, 0, first=True)
                        step(1, 1)
                        with dve.Fori(1, H // 2 - 1) as g:
                            step(2 * g, 0)
                            step(2 * g + 1, 1)
                        step(H - 2, 0, late=True)
                        step(H - 1, 1, last=True, late=True)
                        o_den(1, TT - 1)
                        o_out(H - 1, TT - 1, 1)
                        for j in range(H // 2):
                            dve.wait_ge(sem("a_othigh"), j + 1)
                            dve.tensor_tensor(OT[:, j % 2, 1, :], TB[j % 2][:], OT[:, j % 2, 0, :],
                                              ALU.subtract).then_inc(sem("a_otlow"), 1)
                        dve.wait_ge(sem("a_omm"), H // 2)
                        for i in range(2):
                            xs = x[:, 2 * i:2 * i + 2, :].rearrange("p t d -> p (t d)")
                            dve.tensor_tensor(xs, ACC[i][:], xs, ALU.add).then_inc(sem("residual"), 1)

        with ExitStack() as ph:
            s_ = tensors(ph, "ffn")
            y1 = s_("y1", [P, PK], I32)
            y2 = s_("y2", [P, PK], I32)
            y3 = s_("y3", [P, PK], I32)
            codes = s_("codes", [P, 2, PK], I32)
            sc = s_("sc", [P, 2, BLK])
            W = s_("W", [P, 2, 2 * PK])
            WG = s_("WG", [P, 2, 2, 4, P], F16)
            WD = s_("WD", [P, 4, 2, D], F16)
            gl = s_("gl", [P, 2, TOK])
            it = s_("it", [P, 2, TOK])
            IN = s_("IN", [P, 4, 2, TOK], F16)
            zero = s_("zero", [P, P], F16)
            WB, WB2, ACC = bank[0], bank[1], bank[6:8]
            GB, UB = (bank[2], bank[4]), (bank[3], bank[5])
            LAST = FT - 1

            def over_blocks(ap):
                return ap.rearrange("p (b k f) -> p b k f", b=BLK, f=2)

            with nc.Block() as block:
                @block.gpsimd
                def _(pool):
                    def fetch_scales(i, u):
                        pool.tensor_copy(sc[:, u % 2, :], pscale[:, bass.ds(i, 1), :]
                                         .rearrange("p o b -> p (o b)")).then_inc(sem("f_sc"), 1)

                    def scaled(i, u):
                        pool.wait_ge(sem("f_w"), i + 2)
                        pool.wait_ge(sem("f_codes"), i + 1)
                        pool.wait_ge(sem("f_tr"), i + 1)
                        pool.wait_ge(sem("f_sc"), i + 1)
                        fetch_scales(i + 1, u + 1)
                        value = codes[:, u % 2, :].bitcast(F8)\
                            .rearrange("p (b k f) -> p b k f", b=BLK, f=4)[:, :, :, 0:2]
                        scale = sc[:, u % 2, :].rearrange("p (b o q) -> p b o q", o=1, q=1)\
                            .to_broadcast([P, BLK, 16, 2])
                        pool.tensor_tensor(over_blocks(W[:, u % 2, :]), value, scale, ALU.mult)\
                            .then_inc(sem("f_w"), 1)

                    def in_low(i, u):
                        pool.wait_ge(sem("f_ihigh"), i + 1)
                        pool.tensor_tensor(IN[:, u % 4, 1, :], it[:, u % 2, :], IN[:, u % 4, 0, :],
                                           ALU.subtract).then_inc(sem("f_ilow"), 1)

                    pool.memset(zero[:], 0.0).then_inc(sem("f_zero"), 1)
                    pool.nop().then_inc(sem("f_w"), 2)
                    pool.nop().then_inc(sem("f_ilow"), 2)
                    pool.wait_ge(sem("f_scale64"), 1)
                    fetch_scales(0, 0)
                    scaled(0, 0)
                    ln_pool(pool, 1)
                    scaled(1, 1)
                    scaled(2, 2)
                    in_low(0, 0)
                    scaled(3, 3)
                    in_low(1, 1)
                    with pool.Fori(0, 3) as g:
                        for u in range(1, 5):
                            scaled(4 * g + u + 3, u + 3)
                            in_low(4 * g + u + 1, u + 1)
                    for i in range(13, LAST):
                        in_low(i + 1, i + 1)

                @block.tensor
                def _(pe):
                    def turn(i, u):
                        pe.wait_ge(sem("f_w"), i + 3)
                        pe.wait_ge(sem("f_wlow"), 2 * i + 2)
                        for m in range(6):
                            out = WB[:, m * P:(m + 1) * P] if m < 4 else WB2[:, (m - 4) * P:(m - 3) * P]
                            last = pe.transpose(out, W[:, u % 2, m * P:(m + 1) * P], ident[:])
                        last.then_inc(sem("f_tr"), 1)

                    def gate_up(i, u):
                        pe.wait_ge(sem("f_wlow"), 2 * i + 4)
                        pe.wait_ge(sem("f_uread"), i + 1)
                        for m, out in enumerate((GB[u % 2], UB[u % 2])):
                            n = 0
                            for k in range(KT):
                                for l, r in PASSES:
                                    last = pe.matmul(out[:], WG[:, u % 2, l, 2 * m + k, :], xT[:, r, k, :],
                                                     start=(n == 0), stop=(n == 5))
                                    n += 1
                        last.then_inc(sem("f_gu"), 1)

                    def down(i, u):
                        pe.wait_ge(sem("f_ilow"), i + 3)
                        for t in range(TT):
                            for l, r in PASSES:
                                last = pe.matmul(ACC[t // 2][:, (t % 2) * D:(t % 2 + 1) * D],
                                                 IN[:, u % 4, l, t * P:(t + 1) * P], WD[:, u % 4, r, :],
                                                 start=False, stop=False, skip_group_check=True)
                        last.then_inc(sem("f_dn"), 1)

                    pe.wait_ge(sem("f_zero"), 1)
                    for acc in ACC:
                        pe.matmul(acc[:], zero[:], xT[:, 0, 0, :], start=True, stop=False,
                                  skip_group_check=True)
                    turn(0, 0)
                    turn(1, 1)
                    ln_tensor(pe, 1, bank[2:4])
                    pe.wait_ge(sem("ln_lo"), 2 * KT)
                    gate_up(0, 0)
                    turn(2, 2)
                    gate_up(1, 1)
                    with pe.Fori(0, 3) as g:
                        for u in range(1, 5):
                            turn(4 * g + u + 2, u + 2)
                            gate_up(4 * g + u + 1, u + 1)
                            down(4 * g + u - 1, u - 1)
                    for i in range(13, FT + 1):
                        if i + 2 < FT:
                            turn(i + 2, i + 2)
                        if i + 1 < FT:
                            gate_up(i + 1, i + 1)
                        down(i - 1, i - 1)

                @block.scalar
                def _(act):
                    def w_high(i, u):
                        act.wait_ge(sem("f_tr"), i + 3)
                        act.activation(WG[:, u % 2, 0].rearrange("p m n -> p (m n)"), WB[:], ACT.Copy)\
                           .then_inc(sem("f_whigh"), 1)
                        act.activation(WD[:, u % 4, 0, :], WB2[:, 0:D], ACT.Copy)\
                           .then_inc(sem("f_whigh"), 1)

                    def gelu(i, u):
                        act.wait_ge(sem("f_gu"), i + 1)
                        act.activation(gl[:, u % 2, :], GB[u % 2][:], ACT.Gelu_apprx_tanh)\
                           .then_inc(sem("f_gelu"), 1)

                    def in_high(i, u):
                        act.wait_ge(sem("f_uread"), i + 3)
                        act.activation(IN[:, u % 4, 0, :], it[:, u % 2, :], ACT.Copy)\
                           .then_inc(sem("f_ihigh"), 1)

                    act.nop().then_inc(sem("f_tr"), 2)
                    w_high(0, 0)
                    w_high(1, 1)
                    ln_scalar(act, 1, bank[2:4])
                    gelu(0, 0)
                    in_high(0, 0)
                    w_high(2, 2)
                    gelu(1, 1)
                    in_high(1, 1)
                    with act.Fori(0, 3) as g:
                        for u in range(1, 5):
                            w_high(4 * g + u + 2, u + 2)
                            gelu(4 * g + u + 1, u + 1)
                            in_high(4 * g + u + 1, u + 1)
                    for i in range(13, LAST):
                        if i + 2 < FT:
                            w_high(i + 2, i + 2)
                        gelu(i + 1, i + 1)
                        in_high(i + 1, i + 1)

                @block.vector
                def _(dve):
                    shl, band, bor = ALU.logical_shift_left, ALU.bitwise_and, ALU.bitwise_or

                    def decode(i, u):
                        src = packed[:, bass.ds(i, 1), :].rearrange("p o k -> p (o k)")
                        dve.wait_ge(sem("f_dec"), 5 * i + 1)
                        dve.tensor_scalar(y1[:], src, 4, 0xF00, shl, band).then_inc(sem("f_dec"), 1)
                        dve.tensor_scalar(y2[:], src, 0xF, None, band).then_inc(sem("f_dec"), 1)
                        dve.wait_ge(sem("f_dec"), 5 * i + 3)
                        dve.tensor_tensor(y3[:], y1[:], y2[:], bor).then_inc(sem("f_dec"), 1)
                        dve.wait_ge(sem("f_dec"), 5 * i + 4)
                        dve.tensor_scalar(y1[:], y3[:], 4, 0x8080, shl, band).then_inc(sem("f_dec"), 1)
                        dve.tensor_scalar(y2[:], y3[:], 2, 0x1C1C, shl, band).then_inc(sem("f_dec"), 1)
                        dve.wait_ge(sem("f_dec"), 5 * i + 6)
                        dve.wait_ge(sem("f_w"), i + 1)
                        dve.tensor_tensor(codes[:, u % 2, :], y1[:], y2[:], bor)\
                           .then_inc(sem("f_codes"), 1)
                        dve.wait_ge(sem("f_codes"), i + 1)

                    def w_low(i, u):
                        dve.wait_ge(sem("f_whigh"), 2 * i + 2)
                        wg = WG[:, u % 2, 0].rearrange("p m n -> p (m n)")
                        dve.tensor_tensor(WG[:, u % 2, 1].rearrange("p m n -> p (m n)"), WB[:], wg,
                                          ALU.subtract).then_inc(sem("f_wlow"), 1)
                        dve.tensor_tensor(WD[:, u % 4, 1, :], WB2[:, 0:D], WD[:, u % 4, 0, :],
                                          ALU.subtract).then_inc(sem("f_wlow"), 1)

                    def gated(i, u):
                        dve.wait_ge(sem("f_gelu"), i + 1)
                        dve.wait_ge(sem("f_ilow"), i + 1)
                        dve.tensor_tensor(it[:, u % 2, :], UB[u % 2][:], gl[:, u % 2, :], ALU.mult)\
                           .then_inc(sem("f_uread"), 1)

                    dve.nop().then_inc(sem("f_wlow"), 2)
                    dve.nop().then_inc(sem("f_uread"), 2)
                    dve.nop().then_inc(sem("f_dec"), 1)
                    dve.wait_ge(sem("in_packed"), 128)
                    sall = pscale[:].rearrange("p t b -> p (t b)")
                    dve.tensor_scalar(sall, sall, 64.0, None, ALU.mult).then_inc(sem("f_scale64"), 1)
                    decode(0, 0)
                    ln_vector(dve, 1)
                    decode(1, 1)
                    w_low(0, 0)
                    w_low(1, 1)
                    ln_vector_low(dve, 1, bank[2:4])
                    decode(2, 2)
                    gated(0, 0)
                    w_low(2, 2)
                    decode(3, 3)
                    gated(1, 1)
                    with dve.Fori(0, 3) as g:
                        for u in range(1, 5):
                            w_low(4 * g + u + 2, u + 2)
                            decode(4 * g + u + 3, u + 3)
                            gated(4 * g + u + 1, u + 1)
                    for i in range(13, LAST):
                        if i + 2 < FT:
                            w_low(i + 2, i + 2)
                        gated(i + 1, i + 1)
                    dve.wait_ge(sem("f_dn"), FT)
                    for i in range(2):
                        xs = x[:, 2 * i:2 * i + 2, :].rearrange("p t d -> p (t d)")
                        dve.tensor_tensor(xs, ACC[i][:], xs, ALU.add).then_inc(sem("residual"), 1)

        pk.close()

        with ExitStack() as ph:
            s_ = tensors(ph, "l1")
            KS = s_("KS", [P, 2, H, NB * SK], F16)
            QS_ = s_("QS_", [P, 2, H, TOK], F16)
            VW = s_("VW", [P, 2, 2, KT, INNER], F16)
            vec = s_("vec", [P, 8, H])
            vb = s_("vb", [P, H])
            ones = s_("ones", [P, P])
            obr = s_("obr", [1, 2 * D])
            rr = s_("rr", [P, NB * KC + TT])
            rq = s_("rq", [P, TT])
            nrq = s_("nrq", [P, TT])
            rK = s_("rK", [P, NB, SK])
            V_QB, V_KB, V_KIB, V_NQ, V_NKT, V_NKI, V_VB, V_VIB = range(8)

            with ExitStack() as pr:
                t_ = tensors(pr, "l1proj")
                HP = H // 2
                NST = 6
                stage = t_("stage", [P, NST, KT, 2 * HD])
                WS = t_("WS", [P, 2, 2, 2, KT, 2 * HD], F16)
                RAW = 4
                raw = t_("raw", [P, RAW, SK])
                sq = t_("sq", [P, RAW, SK])
                ssq = t_("ssq", [P, NB + 1, SK])
                vrow = t_("vrow", [P, P])
                dg = t_("dg", [P, 2, P])
                ms = t_("ms", [P, NB * KC + TT])
                KB = (bank[0:2], bank[2:4])
                pieces = []
                for p in range(HP):
                    for i, w in enumerate(("k_w", "ki_w", "v_w")):
                        pieces.append((w, p, (p % 2) * 3 + i)
                                      + (("p_vsplit", p + 1) if i == 2 else ("p_split", 2 * p + i + 1)))
                for p in range(HP):
                    pieces.append(("q_w", p, (p % 2) * 2, "p_split", 2 * HP + p + 1))
                    pieces.append(("vi_w", p, (p % 2) * 2 + 1, "p_vsplit", HP + p + 1))

                with nc.Block() as block:
                    @block.sync
                    def _(sync):
                        for n, name in enumerate(("q_b", "k_b", "ki_b", "nq_s", "nkt_s", "nki_s", "v_b",
                                                  "vi_b")):
                            sync.dma_start(vrow[n * H:(n + 1) * H, :],
                                           a["L1_xattn_" + name].rearrange("(h p) -> h p", p=P))\
                                .then_inc(sem("in_vec"), 16)
                        for i in range(2):
                            sync.dma_start(obr[:, i * D:(i + 1) * D],
                                           a["L1_xattn_o_b"].rearrange("(o n) -> o n", o=1))\
                                .then_inc(sem("in_vec"), 16)
                        read = {}
                        for w, p, slot, done, count in pieces:
                            if slot in read:
                                sync.wait_ge(*read[slot])
                            read[slot] = (sem(done), count)
                            sync.dma_start(stage[:, slot], a["L1_xattn_" + w]
                                           .rearrange("(k p) n -> p k n", p=P)[:, :, p * 256:p * 256 + 256])\
                                .then_inc(sem(f"in_stage{slot}"), 16)

                    @block.gpsimd
                    def _(pool):
                        def low_keys(p):
                            for i in range(2):
                                hi, lo = (WS[:, p % 2, s, i] for s in range(2))
                                pool.wait_ge(sem("p_hi"), 2 * p + i + 1)
                                pool.tensor_tensor(lo, stage[:, (p % 2) * 3 + i], hi, ALU.subtract)\
                                    .then_inc(sem("p_split"), 1)

                        def low_queries(p):
                            hi, lo = (WS[:, p % 2, s, 0] for s in range(2))
                            pool.wait_ge(sem("p_hi"), 2 * HP + p + 1)
                            pool.tensor_tensor(lo, stage[:, (p % 2) * 2], hi, ALU.subtract)\
                                .then_inc(sem("p_split"), 1)

                        def square_sum(u, part):
                            pool.wait_ge(sem("p_sq"), u + 1)
                            if part < NB and u >= NB:
                                pool.wait_ge(sem("p_ssq"), u - NB + 1 + RAW)
                            elif u > NB * H:
                                pool.wait_ge(sem("p_ssq"), u + RAW)
                            pool.tensor_tensor(ssq[:, part, :], ssq[:, part, :], sq[:, u % RAW, :], ALU.add)\
                                .then_inc(sem("p_ssq"), 1)

                        pool.memset(ones[:], 1.0).then_inc(sem("p_ones"), 1)
                        pool.memset(ssq[:], 0.0).then_inc(sem("p_ones"), 1)
                        low_keys(0)
                        low_keys(1)
                        ln_pool(pool, 2)
                        pool.wait_ge(sem("p_ones"), 2)
                        for p in range(HP):
                            if 2 <= p + 1 < HP:
                                low_keys(p + 1)
                            elif p + 1 == HP:
                                low_queries(0)
                            for u in range(4 * p, 4 * p + 4):
                                square_sum(u, u % NB)
                        for p in range(HP):
                            if p + 1 < HP:
                                low_queries(p + 1)
                            for h in range(2 * p, 2 * p + 2):
                                square_sum(NB * H + h, NB)
                        pool.wait_ge(sem("p_ms"), 1)
                        pool.tensor_tensor(rr[:], ms[:], mhalf[:, 0:NB * KC + TT], ALU.pow)\
                            .then_inc(sem("p_rr"), 1)

                    @block.tensor
                    def _(pe):
                        pe.wait_ge(sem("in_vec"), 160)
                        pe.transpose(bank[4][:, 0:P], vrow[:], ident[:]).then_inc(sem("p_vec"), 1)

                        def keys(h, u):
                            for b in range(NB):
                                pe.wait_ge(sem("p_raw"), 2 * h + b + 1)
                                for seg, (c0, w) in enumerate(SEG):
                                    n = 0
                                    for k in range(KT):
                                        for l, r in PASSES:
                                            last = pe.matmul(
                                                KB[u % 2][b][:, c0:c0 + w],
                                                WS[:, (u // 2) % 2, l, 1 - seg, k, (u % 2) * HD:(u % 2 + 1) * HD],
                                                ctxT[:, r, k, b * SK + c0:b * SK + c0 + w],
                                                start=(n == 0), stop=(n == 5))
                                            n += 1
                                last.then_inc(sem("p_kmm"), 1)

                        def queries(h, u):
                            pe.wait_ge(sem("p_raw"), 2 * H + h + 1)
                            n = 0
                            for k in range(KT):
                                for l, r in PASSES:
                                    last = pe.matmul(KB[(u // 2) % 2][u % 2][:],
                                                     WS[:, (u // 2) % 2, l, 0, k, (u % 2) * HD:(u % 2 + 1) * HD],
                                                     xT[:, r, k, :], start=(n == 0), stop=(n == 5))
                                    n += 1
                            last.then_inc(sem("p_kmm"), 1)

                        pe.wait_ge(sem("p_split"), 2)
                        for u in range(2):
                            keys(u, u)
                        pe.wait_ge(sem("p_split"), 4)
                        for u in range(2, 4):
                            keys(u, u)
                        ln_tensor(pe, 2, bank[6:8])
                        with pe.Fori(1, H // 4) as g:
                            for u in range(4):
                                if u % 2 == 0:
                                    pe.wait_ge(sem("p_split"), 4 * g + u + 2)
                                keys(4 * g + u, u)
                        pe.wait_ge(sem("ln_lo"), 3 * KT)
                        with pe.Fori(0, H // 4) as g:
                            for u in range(4):
                                if u % 2 == 0:
                                    pe.wait_ge(sem("p_split"), 2 * HP + 2 * g + u // 2 + 1)
                                queries(4 * g + u, u)
                        pe.wait_ge(sem("p_ssq"), 3 * H + RAW)
                        for c in range(NB * KC + TT):
                            last = pe.matmul(bank[4][:, c:c + 1],
                                             ssq[:, c // KC, (c % KC) * P:(c % KC + 1) * P],
                                             ones[:, 0:1], start=True, stop=True)
                        last.then_inc(sem("p_sum"), 1)
                        for c in range(NB * KC):
                            pe.wait_ge(sem("p_dg"), c + 1)
                            pe.matmul(bank[6 + c // KC][:, (c % KC) * P:(c % KC + 1) * P], ones[:],
                                      dg[:, c % 2, :], start=True, stop=True).then_inc(sem("p_rK"), 1)

                    @block.scalar
                    def _(act):
                        def square(n, u):
                            act.wait_ge(sem("p_raw"), n + 5)
                            act.wait_ge(sem("p_ssq"), n + 1)
                            act.activation(sq[:, u % RAW, :], raw[:, u % RAW, :], ACT.Square)\
                               .then_inc(sem("p_sq"), 1)

                        def raw_rows(bankv, u, segs, n, first=False):
                            act.wait_ge(sem("p_kmm"), n + 1)
                            act.wait_ge(sem("p_low"), n + 1)
                            if not first:
                                square(n - 1, u - 1)
                            for c0, w, bias in segs:
                                last = act.activation(raw[:, u % RAW, c0:c0 + w], bankv[:, c0:c0 + w],
                                                      ACT.Identity, bias=bias)
                            last.then_inc(sem("p_raw"), 1)

                        def head_of(v, h):
                            return vec[:, v, bass.ds(h, 1)]

                        def values_of(p, image):
                            return VW[:, 0, image, :, bass.ds(p * 2 * HD, 2 * HD)]

                        def high_keys(p, par, turn, late):
                            slot = par * 3
                            if late:
                                act.wait_ge(sem("p_kmm"), 4 * (p - 1))
                            act.wait_ge(sem(f"in_stage{slot}"), 16 * turn)
                            act.activation(WS[:, par, 0, 0], stage[:, slot], ACT.Copy).then_inc(sem("p_hi"), 1)
                            act.wait_ge(sem(f"in_stage{slot + 1}"), 16 * turn)
                            act.wait_ge(sem(f"in_stage{slot + 2}"), 16 * turn)
                            act.activation(WS[:, par, 0, 1], stage[:, slot + 1], ACT.Copy)\
                               .then_inc(sem("p_hi"), 1)
                            act.activation(values_of(p, 0), stage[:, slot + 2], ACT.Copy)\
                               .then_inc(sem("p_vhi"), 1)

                        def high_queries(p, par, turn):
                            slot = par * 2
                            act.wait_ge(sem("p_kmm"), 2 * H + 2 * (p - 1))
                            act.wait_ge(sem(f"in_stage{slot}"), 16 * turn)
                            act.wait_ge(sem(f"in_stage{slot + 1}"), 16 * turn)
                            act.activation(WS[:, par, 0, 0], stage[:, slot], ACT.Copy).then_inc(sem("p_hi"), 1)
                            act.activation(values_of(p, 1), stage[:, slot + 1], ACT.Copy)\
                               .then_inc(sem("p_vhi"), 1)

                        act.nop().then_inc(sem("p_raw"), 4)
                        high_keys(0, 0, 1, False)
                        high_keys(1, 1, 1, False)
                        act.wait_ge(sem("p_vec"), 1)
                        act.activation(vec[:].rearrange("p v h -> p (v h)"), bank[4][:, 0:P], ACT.Copy)\
                           .then_inc(sem("p_vec"), 1)
                        act.wait_ge(sem("p_vec"), 2)

                        def keys(h, u, fresh=False):
                            for b in range(NB):
                                raw_rows(KB[u % 2][b], 2 * u + b,
                                         ((0, NIMG, head_of(V_KIB, h)), (NIMG, NTXT, head_of(V_KB, h))),
                                         2 * h + b, first=(u == 0 and b == 0 and fresh))
                        for u in range(2):
                            keys(u, u, fresh=True)
                        for u in range(2, 4):
                            if u == 2:
                                high_keys(2, 0, 2, True)
                            keys(u, u, fresh=True)
                        ln_scalar(act, 2, bank[6:8])

                        def four_heads(g, last=False):
                            for u in range(4):
                                if u == 0:
                                    high_keys(2 * g + 1, 1, g + 1, True)
                                elif u == 2 and not last:
                                    high_keys(2 * g + 2, 0, g + 2, True)
                                elif u == 2:
                                    high_queries(0, 0, HP // 2 + 1)
                                keys(4 * g + u, u)
                        with act.Fori(1, H // 4 - 1) as g:
                            four_heads(g)
                        four_heads(H // 4 - 1, last=True)

                        def four_queries(g, last=False):
                            for u in range(4):
                                h = 4 * g + u
                                if u == 0:
                                    high_queries(2 * g + 1, 1, HP // 2 + g + 1)
                                elif u == 2 and not last:
                                    high_queries(2 * g + 2, 0, HP // 2 + g + 2)
                                raw_rows(KB[(u // 2) % 2][u % 2], u, ((0, TOK, head_of(V_QB, h)),), 2 * H + h)
                        with act.Fori(0, H // 4 - 1) as g:
                            four_queries(g)
                        four_queries(H // 4 - 1, last=True)
                        square(3 * H - 1, RAW - 1)
                        act.wait_ge(sem("p_rK"), NB * KC)
                        for b in range(NB):
                            act.activation(rK[:, b, :], bank[6 + b][:], ACT.Copy).then_inc(sem("p_end"), 1)

                    @block.vector
                    def _(dve):
                        def halves(dst, h, u, ahead, segs):
                            dve.wait_ge(sem("p_raw"), ahead + 5)
                            for c0, w, v in segs:
                                dve.tensor_scalar(dst(0, c0, w), raw[:, u % RAW, c0:c0 + w],
                                                  vec[:, v, bass.ds(h, 1)], None, ALU.mult)\
                                   .then_inc(sem(f"p_high{len(segs)}"), 1)
                            for i, (c0, w, v) in enumerate(segs):
                                dve.wait_ge(sem(f"p_high{len(segs)}"),
                                            (2 * ahead if len(segs) == 2 else h) + i + 1)
                                last = dve.scalar_tensor_tensor(
                                    out=dst(1, c0, w), in0=raw[:, u % RAW, c0:c0 + w],
                                    scalar=vec[:, v, bass.ds(h, 1)], in1=dst(0, c0, w),
                                    op0=ALU.mult, op1=ALU.subtract)
                            last.then_inc(sem("p_low"), 1)

                        def low_values(p, slot, image):
                            hi, lo = (VW[:, s, image, :, bass.ds(p * 2 * HD, 2 * HD)] for s in range(2))
                            dve.wait_ge(sem("p_vhi"), HP * image + p + 1)
                            dve.tensor_tensor(lo, stage[:, slot], hi, ALU.subtract)\
                               .then_inc(sem("p_vsplit"), 1)

                        def one(ap):
                            return ap.rearrange("p o n -> p (o n)")

                        def keys(h, u):
                            for b in range(NB):
                                halves(lambda s, c0, w, b=b: one(KS[:, s, bass.ds(h, 1),
                                                                   b * SK + c0:b * SK + c0 + w]),
                                       h, 2 * u + b, 2 * h + b, ((0, NIMG, V_NKI), (NIMG, NTXT, V_NKT)))

                        dve.nop().then_inc(sem("p_low"), RAW)
                        dve.nop().then_inc(sem("p_ssq"), RAW)
                        ln_vector(dve, 2)
                        dve.wait_ge(sem("p_vec"), 2)
                        dve.tensor_tensor(vb[:], vec[:, V_VB, :], vec[:, V_VIB, :], ALU.add)\
                           .then_inc(sem("p_end"), 1)
                        low_values(0, 2, 0)
                        for h in range(4):
                            keys(h, h)
                            if h == 1:
                                low_values(1, 5, 0)
                            elif h == 3:
                                low_values(2, 2, 0)
                        ln_vector_low(dve, 2, bank[6:8])

                        def four_heads(g, last=False):
                            for u in range(4):
                                keys(4 * g + u, u)
                                if u == 1:
                                    low_values(2 * g + 1, 5, 0)
                                elif u == 3 and not last:
                                    low_values(2 * g + 2, 2, 0)
                                elif u == 3:
                                    low_values(0, 1, 1)

                        def four_queries(g, last=False):
                            for u in range(4):
                                h = 4 * g + u
                                halves(lambda s, c0, w: one(QS_[:, s, bass.ds(h, 1), c0:c0 + w]),
                                       h, u, 2 * H + h, ((0, TOK, V_NQ),))
                                if u == 1:
                                    low_values(2 * g + 1, 3, 1)
                                elif u == 3 and not last:
                                    low_values(2 * g + 2, 1, 1)
                        with dve.Fori(1, H // 4 - 1) as g:
                            four_heads(g)
                        four_heads(H // 4 - 1, last=True)
                        with dve.Fori(0, H // 4 - 1) as g:
                            four_queries(g)
                        four_queries(H // 4 - 1, last=True)
                        dve.wait_ge(sem("p_sum"), 1)
                        dve.tensor_scalar(ms[:], bank[4][:, 0:NB * KC + TT], 1.0 / INNER, 1e-6, ALU.mult,
                                          ALU.add).then_inc(sem("p_ms"), 1)
                        dve.wait_ge(sem("p_rr"), 1)
                        qr = rr[:, NB * KC:NB * KC + TT]
                        dve.tensor_scalar(rq[:], qr, SCALE1, None, ALU.mult).then_inc(sem("p_end"), 1)
                        dve.tensor_scalar(nrq[:], qr, -SCALE1, None, ALU.mult).then_inc(sem("p_end"), 1)
                        for c in range(NB * KC):
                            if c >= 2:
                                dve.wait_ge(sem("p_rK"), c - 1)
                            dve.tensor_scalar(dg[:, c % 2, :], ident[:], rr[:, c:c + 1], None, ALU.mult)\
                               .then_inc(sem("p_dg"), 1)

            with ExitStack() as at:
                t_ = tensors(at, "l1head")
                OW = t_("OW", [P, 2, H, D], F16)
                ostage = t_("ostage", [P, 2, D])
                V = t_("V", [P, 2, 2, NB * KC, HD], F16)
                X = t_("X", [P, TT, SK])
                PT = t_("PT", [P, 2, 2, SK], F16)
                mx = t_("mx", [P, TT, 2])
                nm = t_("nm", [P, TT, 2])
                den = t_("den", [P, TT, 2])
                rden = t_("rden", [P, TT, 2])
                OT = t_("OT", [P, 2, 2, TOK], F16)
                SB, TB, OB, VB, ACC = bank[0], bank[1], bank[2:4], bank[4:6], bank[6:8]

                with nc.Block() as block:
                    @block.sync
                    def _(sync):
                        for g in range(H // 2):
                            if g:
                                sync.wait_ge(sem("o_split"), g)
                            sync.dma_start(ostage[:], a["L1_xattn_o_w"].rearrange(
                                "(h p) n -> p h n", p=P)[:, 2 * g:2 * g + 2, :]).then_inc(sem("in_ow0"), 16)

                    @block.gpsimd
                    def _(pool):
                        def normalise(h, t):
                            pool.wait_ge(sem("b_rden"), 4 * h + t + 1)
                            t = t % TT
                            for s, (c0, w) in enumerate(SEG):
                                last = pool.tensor_tensor(X[:, t, c0:c0 + w], X[:, t, c0:c0 + w],
                                                          rden[:, t, s:s + 1].to_broadcast([P, w]), ALU.mult)
                            last.then_inc(sem("b_norm"), 1)

                        def ow_low(g):
                            hi, lo = (OW[:, s, bass.ds(2 * g, 2), :] for s in range(2))
                            pool.wait_ge(sem("o_hi"), g + 1)
                            pool.tensor_tensor(lo, ostage[:], hi, ALU.subtract).then_inc(sem("o_split"), 1)

                        def step(h, par, last=False):
                            for t in range(TT):
                                if not (last and t):
                                    normalise(h, t + 3)

                        def two_heads(g, last=False):
                            step(2 * g, 0)
                            ow_low(g)
                            step(2 * g + 1, 1, last=last)
                        for t in range(3):
                            normalise(0, t)
                        two_heads(0)
                        with pool.Fori(1, H // 2 - 1) as g:
                            two_heads(g)
                        two_heads(H // 2 - 1, last=True)

                    @block.tensor
                    def _(pe):
                        def values(h, par, b, half):
                            if half == 0:
                                pe.wait_ge(sem("b_vlow"), 2 * h + b + 1)
                            for c in (2 * half, 2 * half + 1):
                                if c == NIMG // P:
                                    terms = [(ctxM[:, l, k, b, v, :], l, r, k, 1 - v)
                                             for v in range(2) for k in range(KT) for l, r in PASSES]
                                else:
                                    terms = [(ctxT[:, l, k, b * SK + c * P:b * SK + (c + 1) * P], l, r, k,
                                              int(c < NIMG // P)) for k in range(KT) for l, r in PASSES]
                                for n, (rows, l, r, k, w) in enumerate(terms):
                                    last = pe.matmul(VB[b][:, c * HD:(c + 1) * HD], rows,
                                                     VW[:, r, w, k, bass.ds(h * HD, HD)],
                                                     start=(n == 0), stop=(n == len(terms) - 1))
                            if half:
                                last.then_inc(sem("b_vfull"), 1)

                        def scores(h, t):
                            n = 4 * h + t
                            pe.wait_ge(sem("b_max"), 2 * n + 2)
                            b = t // 2
                            for i, (l, r) in enumerate(PASSES):
                                last = pe.matmul(SB[:], QS_[:, l, bass.ds(h, 1), t * P:(t + 1) * P],
                                                 KS[:, r, bass.ds(h, 1), b * SK:(b + 1) * SK],
                                                 start=(i == 0), stop=(i == 2))
                            last.then_inc(sem("b_sfull"), 1)

                        def turn(h, t):
                            n = 4 * h + t
                            pe.wait_ge(sem("b_norm"), n + 1)
                            pe.wait_ge(sem("b_ptlow"), n + 1)
                            for c in range(KC):
                                last = pe.transpose(TB[:, c * P:(c + 1) * P],
                                                    X[:, t, c * P:(c + 1) * P], ident[:])
                            last.then_inc(sem("b_tfull"), 1)

                        def attend(h, t, par):
                            n = 4 * h + t
                            b = t // 2
                            pe.wait_ge(sem("b_ptlow"), n + 2)
                            if t == 0:
                                pe.wait_ge(sem("b_vlow"), 2 * h + 4)
                                pe.wait_ge(sem("b_olow"), h + 1)
                            i = 0
                            for c in range(KC):
                                for l, r in PASSES:
                                    last = pe.matmul(OB[par][:, t * P:(t + 1) * P], V[:, par, l, b * KC + c, :],
                                                     PT[:, t % 2, r, c * P:(c + 1) * P], start=(i == 0),
                                                     stop=(i == 3 * KC - 1))
                                    i += 1
                            last.then_inc(sem("b_ofull"), 1)

                        def output(h, par, pair=None):
                            pe.wait_ge(sem("b_olow"), h + 3)
                            pe.wait_ge(sem("o_split"), h // 2 + 1 if isinstance(h, int) else pair + 1)
                            for t in range(TT):
                                for l, r in PASSES:
                                    last = pe.matmul(ACC[t // 2][:, (t % 2) * D:(t % 2 + 1) * D],
                                                     OT[:, par, l, t * P:(t + 1) * P],
                                                     OW[:, r, bass.ds(h, 1), :], start=False, stop=False,
                                                     skip_group_check=True)
                            last.then_inc(sem("b_omm"), 1)

                        def step(h, par, first=False, last=False, pair=None):
                            for t in range(TT):
                                turn(h, t)
                                if not last:
                                    scores(h + 1, t)
                                    values(h + 1, 1 - par, t // 2, t % 2)
                                if t:
                                    attend(h, t - 1, par)
                                elif not first:
                                    attend(h - 1, TT - 1, 1 - par)
                                if t == 2 and not first:
                                    output(h - 1, 1 - par, pair)

                        for acc in ACC:
                            pe.matmul(acc[:], ones[0:1, :], obr[:], start=True, stop=False,
                                      skip_group_check=True)
                        for t in range(TT):
                            scores(0, t)
                        for b in range(NB):
                            for half in range(2):
                                values(0, 0, b, half)
                        step(0, 0, first=True)
                        step(1, 1)
                        with pe.Fori(1, H // 2 - 1) as g:
                            step(2 * g, 0, pair=g - 1)
                            step(2 * g + 1, 1, pair=g)
                        step(H - 2, 0)
                        step(H - 1, 1, last=True)
                        attend(H - 1, TT - 1, 1)
                        output(H - 1, 1)

                    @block.scalar
                    def _(act):
                        def v_high(h, par, b):
                            act.wait_ge(sem("b_vfull"), 2 * h + b + 1)
                            act.wait_ge(sem("b_ofull"), 4 * h + 1)
                            act.activation(V[:, par, 0, b * KC:(b + 1) * KC, :].rearrange("p c n -> p (c n)"),
                                           VB[b][:], ACT.Copy).then_inc(sem("b_vhigh"), 1)

                        def exp(h, t):
                            n = 4 * h + t
                            act.wait_ge(sem("b_nm"), n + 1)
                            for s, (c0, w) in enumerate(SEG):
                                act.activation(X[:, t, c0:c0 + w], X[:, t, c0:c0 + w], ACT.Exp,
                                               bias=nm[:, t, s:s + 1], scale=rq[:, t:t + 1],
                                               accum_out=den[:, t, s:s + 1]).then_inc(sem("b_exp"), 1)

                        def pt_high(h, t):
                            n = 4 * h + t
                            act.wait_ge(sem("b_tfull"), n + 1)
                            act.wait_ge(sem("b_ofull"), n + 7)
                            act.activation(PT[:, t % 2, 0, :], TB[:], ACT.Copy)\
                               .then_inc(sem("b_pthigh"), 1)

                        def o_ready(h):
                            act.wait_ge(sem("b_ofull"), 4 * h + 12)
                            act.wait_ge(sem("b_omm"), h + 1)

                        def o_high(h, par):
                            act.activation(OT[:, par, 0, :], OB[par][:], ACT.Identity,
                                           bias=vb[:, bass.ds(h, 1)]).then_inc(sem("b_ohigh"), 1)

                        def step(h, par, first=False, last=False, pair=None):
                            for t in range(TT):
                                out = t == 1 and not first
                                if out:
                                    o_ready(h - 1)
                                if t == 2 and pair is not None:
                                    act.wait_ge(sem("in_ow0"), 16 * pair + 16)
                                pt_high(h, t)
                                if t == 2 and pair is not None:
                                    act.activation(OW[:, 0, bass.ds(2 * pair, 2), :], ostage[:], ACT.Copy)\
                                       .then_inc(sem("o_hi"), 1)
                                if out:
                                    o_high(h - 1, 1 - par)
                                if t == 0:
                                    exp(h, 3)
                                elif not last:
                                    exp(h + 1, t - 1)
                                if t % 2 and not last:
                                    v_high(h + 1, 1 - par, t // 2)

                        act.nop().then_inc(sem("b_ofull"), 8)
                        act.nop().then_inc(sem("b_omm"), 2)
                        for t in range(3):
                            exp(0, t)
                        for b in range(NB):
                            v_high(0, 0, b)
                        step(0, 0, first=True, pair=0)
                        step(1, 1)
                        with act.Fori(1, H // 2 - 1) as g:
                            step(2 * g, 0, pair=g)
                            step(2 * g + 1, 1)
                        step(H - 2, 0, pair=H // 2 - 1)
                        step(H - 1, 1, last=True)
                        o_ready(H - 1)
                        o_high(H - 1, 1)

                    @block.vector
                    def _(dve):
                        def top_score(h, t):
                            n = 4 * h + t
                            for s, (c0, w) in enumerate(SEG):
                                dve.tensor_tensor_reduce(X[:, t, c0:c0 + w], SB[:, c0:c0 + w],
                                                         rK[:, t // 2, c0:c0 + w], 1.0, LOWEST, ALU.mult,
                                                         ALU.max, mx[:, t, s:s + 1])\
                                   .then_inc(sem("b_max"), 1)
                            dve.wait_ge(sem("b_max"), 2 * n + 4)
                            dve.tensor_scalar(nm[:, t, :], mx[:, t, :], nrq[:, t:t + 1], None, ALU.mult)\
                               .then_inc(sem("b_nm"), 1)

                        def inverse(t):
                            dve.reciprocal(rden[:, t, :], den[:, t, :]).then_inc(sem("b_rden"), 1)

                        def pt_low(h, t):
                            n = 4 * h + t
                            dve.wait_ge(sem("b_pthigh"), n + 1)
                            dve.tensor_tensor(PT[:, t % 2, 1, :], TB[:], PT[:, t % 2, 0, :],
                                              ALU.subtract).then_inc(sem("b_ptlow"), 1)

                        def v_low(h, par, b):
                            dve.wait_ge(sem("b_vhigh"), 2 * h + b + 1)
                            hi, lo = (V[:, par, s, b * KC:(b + 1) * KC, :].rearrange("p c n -> p (c n)")
                                      for s in range(2))
                            dve.tensor_tensor(lo, VB[b][:], hi, ALU.subtract).then_inc(sem("b_vlow"), 1)

                        def o_low(h, par):
                            dve.wait_ge(sem("b_ohigh"), h + 1)
                            dve.scalar_tensor_tensor(out=OT[:, par, 1, :], in0=OB[par][:],
                                                     scalar=vb[:, bass.ds(h, 1)], in1=OT[:, par, 0, :],
                                                     op0=ALU.add, op1=ALU.subtract)\
                               .then_inc(sem("b_olow"), 1)

                        def step(h, par, first=False, last=False):
                            for t in range(TT):
                                if not last:
                                    dve.wait_ge(sem("b_sfull"), 4 * (h + 1) + t + 1)
                                pt_low(h, t)
                                if not last:
                                    top_score(h + 1, t)
                                if not (last and t):
                                    dve.wait_ge(sem("b_exp"), 2 * (4 * h + t + 3) + 2)
                                    inverse((t + 3) % 4)
                                if t == 1 and not first:
                                    o_low(h - 1, 1 - par)
                                if t % 2 and not last:
                                    v_low(h + 1, 1 - par, t // 2)

                        dve.nop().then_inc(sem("b_max"), 2)
                        for credit, n in (("b_ptlow", 1), ("b_vlow", 2), ("b_olow", 2)):
                            dve.nop().then_inc(sem(credit), n)
                        for t in range(TT):
                            dve.wait_ge(sem("b_sfull"), t + 1)
                            top_score(0, t)
                        for t in range(3):
                            dve.wait_ge(sem("b_exp"), 2 * t + 2)
                            inverse(t)
                        for b in range(NB):
                            v_low(0, 0, b)
                        step(0, 0, first=True)
                        step(1, 1)
                        with dve.Fori(1, H // 2 - 1) as g:
                            step(2 * g, 0)
                            step(2 * g + 1, 1)
                        step(H - 2, 0)
                        step(H - 1, 1, last=True)
                        o_low(H - 1, 1)
                        dve.wait_ge(sem("b_omm"), H + 2)
                        for i in range(2):
                            xs = x[:, 2 * i:2 * i + 2, :].rearrange("p t d -> p (t d)")
                            dve.tensor_tensor(xs, ACC[i][:], xs, ALU.add).then_inc(sem("residual"), 1)


        with ExitStack() as ph:
            s_ = tensors(ph, "moe")
            mG = s_("mG", [P, KT, MT * P])
            mU = s_("mU", [P, KT, MT * P])
            mD = s_("mD", [P, MT, D])
            WG = s_("WG", [P, 4, 2, 2, KT, P], F16)
            WD = s_("WD", [P, 4, 2, D], F16)
            si = s_("si", [P, 2, TOK])
            su_ = s_("su", [P, 2, TOK])
            it = s_("it", [P, 2, TOK])
            IN = s_("IN", [P, 4, 2, TOK], F16)
            zero = s_("zero", [P, P], F16)
            rrow = s_("rrow", [E, D])
            rT = s_("rT", [P, KT, EG])
            rTS = s_("rTS", [P, 2, KT, EG], F16)
            before = s_("before", [P, E * E])
            owner = s_("owner", [EG, MT * P], F16)
            lg = s_("lg", [P, TT, EG])
            ex = s_("ex", [P, TT, EG])
            pr_ = s_("pr", [P, TT, E])
            g1 = s_("g1", [P, TT, E * E])
            g2 = s_("g2", [P, TT, E * E])
            rank = s_("rank", [P, TT, E])
            comb = s_("comb", [P, TT, EG])
            v1 = s_("v1", [P, TT])
            v2 = s_("v2", [P, TT])
            combT = s_("combT", [EG, 2, TOK], F16)
            GB, UB, CB, ACC = (bank[0], bank[2]), (bank[1], bank[3]), bank[4:6], bank[6:8]
            RT, LB, CT, LNB = bank[4], bank[5], bank[4], bank[0:2]
            EPG = 4
            GCOL = EPG * IM
            NGRP = E // EPG + 1
            group_of = [min((j * P + P - 1) // GCOL, NGRP - 1) for j in range(MT)]

            with nc.Block() as block:
                @block.sync
                def _(sync):
                    sync.dma_start(rrow[:], a["L1_ffn_router_w"]).then_inc(sem("in_router"), 16)
                    for k in range(KT):
                        sync.dma_start(rT[:, k, E:EG], a["L1_ffn_sh_gate_w"][k * P:(k + 1) * P, :],
                                       allow_slow_non_contiguous=True).then_inc(sem("in_router"), 16)
                    sync.dma_start(before[:], a["before"]).then_inc(sem("in_before"), 16)
                    sync.dma_start(owner[:], a["owner"]).then_inc(sem("in_owner"), 16)
                    for g in range(NGRP):
                        arrived = sem(f"in_moe{g}")
                        for k in range(KT):
                            for dst, w in ((mG, "gate"), (mU, "up")):
                                rows = slice(k * P, (k + 1) * P)
                                if g < E // EPG:
                                    sync.dma_start(
                                        dst[:, k, g * GCOL:(g + 1) * GCOL].rearrange("p (e i) -> p e i", i=IM),
                                        a[f"L1_ffn_w_{w}"][g * EPG:(g + 1) * EPG, rows, :]
                                        .rearrange("e p i -> p e i")).then_inc(arrived, 16)
                                else:
                                    sync.dma_start(dst[:, k, E * IM:MROWS], a[f"L1_ffn_sh_{w}"][rows, :])\
                                        .then_inc(arrived, 16)
                        tiles = [j for j in range(MT) if group_of[j] == g]
                        j0, j1 = tiles[0], tiles[-1] + 1
                        if g < E // EPG:
                            sync.dma_start(mD[:, j0:j1, :], a["L1_ffn_w_down"].rearrange(
                                "e i d -> (e i) d").rearrange("(t p) d -> p t d", p=P)[:, j0:j1, :])\
                                .then_inc(arrived, 16)
                        else:
                            sync.dma_start(mD[:, j0:j1 - 1, :], a["L1_ffn_sh_down"][0:(j1 - 1 - j0) * P, :]
                                           .rearrange("(t p) d -> p t d", p=P)).then_inc(arrived, 16)
                            sync.dma_start(mD[0:MLAST, j1 - 1, :],
                                           a["L1_ffn_sh_down"][(j1 - 1 - j0) * P:ISH, :]).then_inc(arrived, 16)
                    for g in range(NGRP):
                        sync.wait_ge(sem(f"in_moe{g}"), 16 * (5 if g < E // EPG else 6))
                        sync.nop().then_inc(sem("m_arrived"), group_of.count(g))
                    sync.wait_ge(sem("residual"), 8)
                    sync.dma_start(a["out"].rearrange("b (t p) d -> p (b t) d", p=P), x[:])\
                        .then_inc(sem("out"), 16)
                    sync.wait_ge(sem("out"), 16)

                @block.gpsimd
                def _(pool):
                    pool.memset(zero[:], 0.0).then_inc(sem("m_zero"), 1)
                    for w in (mG, mU):
                        pool.memset(w[:, :, MROWS:MT * P], 0.0).then_inc(sem("m_zero"), 1)
                    pool.wait_ge(sem("m_zero"), 3)
                    pool.memset(mD[MLAST:P, MT - 1, :], 0.0).then_inc(sem("m_zero"), 1)
                    pool.nop().then_inc(sem("m_ilow"), 2)
                    pool.wait_ge(sem("m_zero"), 4)

                    def split(j):
                        cols = slice(j * P, (j + 1) * P)
                        srcs = [(WG[:, j % 4, :, m], w[:, :, cols]) for m, w in enumerate((mG, mU))]
                        for m, (dst, src) in enumerate(srcs):
                            pool.wait_ge(sem("m_whi"), 3 * j + m + 1)
                            pool.tensor_tensor(dst[:, 1], src, dst[:, 0], ALU.subtract)\
                                .then_inc(sem("m_wlo"), 1)
                        pool.wait_ge(sem("m_whi"), 3 * j + 3)
                        pool.tensor_tensor(WD[:, j % 4, 1, :], mD[:, j, :], WD[:, j % 4, 0, :],
                                           ALU.subtract).then_inc(sem("m_wlo"), 1)

                    def in_low(j):
                        pool.wait_ge(sem("m_ihigh"), j + 1)
                        pool.tensor_tensor(IN[:, j % 4, 1, :], it[:, j % 2, :], IN[:, j % 4, 0, :],
                                           ALU.subtract).then_inc(sem("m_ilow"), 1)

                    ln_pool(pool, 3)
                    pool.wait_ge(sem("m_rT"), 1)
                    pool.wait_ge(sem("in_router"), 48)
                    pool.tensor_copy(rTS[:, 0], rT[:]).then_inc(sem("m_router"), 1)
                    pool.wait_ge(sem("m_router"), 1)
                    pool.tensor_tensor(rTS[:, 1], rT[:], rTS[:, 0], ALU.subtract).then_inc(sem("m_router"), 1)
                    split(0)
                    split(1)
                    split(2)
                    for j in range(MT):
                        in_low(j)
                        if j + 3 < MT:
                            split(j + 3)

                @block.tensor
                def _(pe):
                    pe.wait_ge(sem("m_zero"), 1)
                    for acc in ACC:
                        pe.matmul(acc[:], zero[:], xT[:, 0, 0, :], start=True, stop=False,
                                  skip_group_check=True)
                    pe.wait_ge(sem("in_router"), 48)
                    for k in range(KT):
                        last = pe.transpose(RT[:, k * E:(k + 1) * E], rrow[:, k * P:(k + 1) * P],
                                            ident[0:E, 0:E])
                    last.then_inc(sem("m_rt"), 1)
                    ln_tensor(pe, 3, LNB)
                    pe.wait_ge(sem("m_router"), 2)
                    pe.wait_ge(sem("ln_lo"), 4 * KT)
                    for t in range(TT):
                        n = 0
                        for k in range(KT):
                            for l, r in PASSES:
                                last = pe.matmul(LB[:, t * EG:(t + 1) * EG], xT[:, l, k, t * P:(t + 1) * P],
                                                 rTS[:, r, k, :], start=(n == 0), stop=(n == 5))
                                n += 1
                    last.then_inc(sem("m_logits"), 1)

                    def gate_up(j, u):
                        pe.wait_ge(sem("m_wlo"), 3 * j + 3)
                        pe.wait_ge(sem("m_uread"), j + 1)
                        for m, out in enumerate((GB[u % 2], UB[u % 2])):
                            n = 0
                            for k in range(KT):
                                for l, r in PASSES:
                                    last = pe.matmul(out[:], WG[:, u % 4, l, m, k, :], xT[:, r, k, :],
                                                     start=(n == 0), stop=(n == 5))
                                    n += 1
                        last.then_inc(sem("m_gu"), 1)

                    def spread(j, u):
                        pe.wait_ge(sem("m_cread"), j + 1)
                        for r in range(2):
                            last = pe.matmul(CB[u % 2][:], owner[:, bass.ds(j * P, P)], combT[:, r, :],
                                             start=(r == 0), stop=(r == 1))
                        last.then_inc(sem("m_c"), 1)

                    def down(j, u):
                        pe.wait_ge(sem("m_ilow"), j + 3)
                        for t in range(TT):
                            for l, r in PASSES:
                                last = pe.matmul(ACC[t // 2][:, (t % 2) * D:(t % 2 + 1) * D],
                                                 IN[:, u % 4, l, t * P:(t + 1) * P], WD[:, u % 4, r, :],
                                                 start=False, stop=False, skip_group_check=True)
                        last.then_inc(sem("m_dn"), 1)

                    gate_up(0, 0)
                    gate_up(1, 1)
                    pe.wait_ge(sem("in_owner"), 16)
                    pe.wait_ge(sem("m_comb"), 1)
                    for t in range(TT):
                        last = pe.transpose(CT[0:EG, t * P:(t + 1) * P], comb[:, t, :], ident[:])
                    last.then_inc(sem("m_combT"), 1)
                    pe.wait_ge(sem("m_comblo"), 1)
                    spread(0, 0)
                    spread(1, 1)
                    with pe.Fori(0, 6) as g:
                        for u in range(1, 5):
                            gate_up(4 * g + u + 1, u + 1)
                            spread(4 * g + u + 1, u + 1)
                            down(4 * g + u - 1, u - 1)
                    for i in range(25, MT + 1):
                        if i + 1 < MT:
                            gate_up(i + 1, i + 1)
                            spread(i + 1, i + 1)
                        down(i - 1, i - 1)

                @block.scalar
                def _(act):
                    def w_high(j, u):
                        for m, w in enumerate((mG, mU)):
                            act.activation(WG[:, u % 4, 0, m], w[:, :, bass.ds(j * P, P)], ACT.Copy)\
                               .then_inc(sem("m_whi"), 1)
                        src = mD[:, j, :] if isinstance(j, int) else \
                            mD[:, bass.ds(j, 1), :].rearrange("p o d -> p (o d)")
                        act.activation(WD[:, u % 4, 0, :], src, ACT.Copy).then_inc(sem("m_whi"), 1)

                    ln_scalar(act, 3, LNB)
                    act.wait_ge(sem("m_zero"), 4)
                    act.wait_ge(sem("m_arrived"), 4)
                    w_high(0, 0)
                    w_high(1, 1)
                    act.wait_ge(sem("m_z"), 2)
                    act.activation(ex[:], lg[:], ACT.Exp).then_inc(sem("m_exp"), 1)
                    w_high(2, 2)
                    act.wait_ge(sem("m_combT"), 1)
                    act.activation(combT[:, 0, :], CT[0:EG, :], ACT.Copy).then_inc(sem("m_combhi"), 1)

                    def silu(j, u):
                        act.wait_ge(sem("m_gu"), j + 1)
                        act.activation(si[:, u % 2, :], GB[u % 2][:], ACT.Silu).then_inc(sem("m_silu"), 1)

                    def in_high(j, u, ahead=False):
                        act.wait_ge(sem("m_cread"), j + 3)
                        if ahead:
                            act.wait_ge(sem("m_dn"), j - 1)
                            act.wait_ge(sem("m_arrived"), j + 3)
                        act.activation(IN[:, u % 4, 0, :], it[:, u % 2, :], ACT.Copy)\
                           .then_inc(sem("m_ihigh"), 1)

                    silu(0, 0)
                    in_high(0, 0)
                    w_high(3, 3)
                    silu(1, 1)
                    in_high(1, 1)
                    with act.Fori(0, 6) as g:
                        for u in range(1, 5):
                            silu(4 * g + u + 1, u + 1)
                            in_high(4 * g + u + 1, u + 1, ahead=True)
                            w_high(4 * g + u + 3, u + 3)
                    for i in range(25, MT - 1):
                        silu(i + 1, i + 1)
                        in_high(i + 1, i + 1)

                @block.vector
                def _(dve):
                    dve.nop().then_inc(sem("m_uread"), 2)
                    dve.nop().then_inc(sem("m_cread"), 2)
                    ln_vector(dve, 3)
                    dve.wait_ge(sem("m_rt"), 1)
                    dve.tensor_copy(rT[:, :, 0:E], RT[:, 0:KT * E].rearrange("p (k e) -> p k e", e=E))\
                       .then_inc(sem("m_rT"), 1)
                    ln_vector_low(dve, 3, LNB)

                    links = [0]

                    def link(ins):
                        links[0] += 1
                        ins.then_inc(sem("m_link"), 1)
                        dve.wait_ge(sem("m_link"), links[0])

                    def of_row(ap, n):
                        return ap.rearrange("p (t o) -> p t o", o=1).to_broadcast([P, TT, n])

                    dve.wait_ge(sem("m_logits"), 1)
                    logits = LB[:, 0:TT * EG].rearrange("p (t e) -> p t e", e=EG)
                    link(dve.tensor_reduce(v1[:], logits[:, :, 0:E], AX, ALU.max))
                    dve.tensor_tensor(lg[:, :, 0:E], logits[:, :, 0:E], of_row(v1[:], E), ALU.subtract)\
                       .then_inc(sem("m_z"), 1)
                    dve.tensor_scalar(lg[:, :, E:EG], logits[:, :, E:EG], -1.0, None, ALU.mult)\
                       .then_inc(sem("m_z"), 1)
                    dve.wait_ge(sem("m_exp"), 1)
                    link(dve.tensor_reduce(v2[:], ex[:, :, 0:E], AX, ALU.add))
                    link(dve.reciprocal(v1[:], v2[:]))
                    link(dve.tensor_tensor(pr_[:], ex[:, :, 0:E], of_row(v1[:], E), ALU.mult))
                    shape = [P, E, E]
                    dve.wait_ge(sem("in_before"), 16)
                    for t in range(TT):
                        others = pr_[:, t, :].rearrange("p (o j) -> p o j", o=1).to_broadcast(shape)
                        own = pr_[:, t, :].rearrange("p (e o) -> p e o", o=1).to_broadcast(shape)
                        grid = [x_[:, t, :].rearrange("p (e j) -> p e j", j=E) for x_ in (g1, g2)]
                        dve.tensor_tensor(grid[0], others, own, ALU.is_gt).then_inc(sem("m_grid"), 1)
                        dve.tensor_tensor(grid[1], others, own, ALU.is_equal).then_inc(sem("m_grid"), 1)
                    for t in range(TT):
                        dve.wait_ge(sem("m_grid"), 2 * t + 2)
                        dve.tensor_tensor(g2[:, t, :], g2[:, t, :], before[:], ALU.mult)\
                           .then_inc(sem("m_tie"), 1)
                    dve.wait_ge(sem("m_tie"), TT)
                    link(dve.tensor_tensor(g1[:], g1[:], g2[:], ALU.add))
                    link(dve.tensor_reduce(rank[:], g1[:].rearrange("p t (e j) -> p (t e) j", j=E), AX,
                                           ALU.add))
                    link(dve.scalar_tensor_tensor(out=pr_[:], in0=rank[:], scalar=float(TOPK), in1=pr_[:],
                                                  op0=ALU.is_lt, op1=ALU.mult))
                    link(dve.tensor_reduce(v2[:], pr_[:], AX, ALU.add))
                    link(dve.tensor_scalar(v2[:], v2[:], 1e-9, None, ALU.max))
                    link(dve.reciprocal(v1[:], v2[:]))
                    link(dve.tensor_scalar(ex[:, :, E:EG], ex[:, :, E:EG], 1.0, None, ALU.add))
                    link(dve.reciprocal(comb[:, :, E:EG], ex[:, :, E:EG]))
                    dve.tensor_tensor(comb[:, :, 0:E], pr_[:], of_row(v1[:], E), ALU.mult)\
                       .then_inc(sem("m_comb"), 1)
                    dve.wait_ge(sem("m_combhi"), 1)
                    dve.tensor_tensor(combT[:, 1, :], CT[0:EG, :], combT[:, 0, :], ALU.subtract)\
                       .then_inc(sem("m_comblo"), 1)

                    def gated(j, u):
                        dve.wait_ge(sem("m_silu"), j + 1)
                        dve.tensor_tensor(su_[:, u % 2, :], UB[u % 2][:], si[:, u % 2, :], ALU.mult)\
                           .then_inc(sem("m_uread"), 1)
                        dve.wait_ge(sem("m_uread"), j + 3)
                        dve.wait_ge(sem("m_c"), j + 1)
                        dve.wait_ge(sem("m_ilow"), j + 1)
                        dve.tensor_tensor(it[:, u % 2, :], CB[u % 2][:], su_[:, u % 2, :], ALU.mult)\
                           .then_inc(sem("m_cread"), 1)

                    gated(0, 0)
                    gated(1, 1)
                    with dve.Fori(0, 6) as g:
                        for u in range(1, 5):
                            gated(4 * g + u + 1, u + 1)
                    for i in range(25, MT - 1):
                        gated(i + 1, i + 1)
                    dve.wait_ge(sem("m_dn"), MT)
                    for i in range(2):
                        xs = x[:, 2 * i:2 * i + 2, :].rearrange("p t d -> p (t d)")
                        dve.tensor_tensor(xs, ACC[i][:], xs, ALU.add).then_inc(sem("residual"), 1)



def constants():
    half = R // 2
    inv = (np.float32(1.0) / np.power(np.float32(10000.0),
                                      np.arange(half, dtype=np.float32) / np.float32(half))).astype(np.float32)
    ang = (np.arange(SK, dtype=np.float32)[:, None] * inv).astype(np.float32).T
    cos = np.ones((P, SK), np.float32)
    sin = np.zeros((P, SK), np.float32)
    cos[KVC:KVC + half] = cos[KVC + half:] = np.cos(ang)
    sin[KVC:KVC + half] = -np.sin(ang)
    sin[KVC + half:] = np.sin(ang)
    rows = np.minimum(np.arange(MT * P) // IM, E)
    return {
        "ident": np.eye(P, dtype=np.float32),
        "kidx": np.broadcast_to(np.arange(SK, dtype=np.float32), (P, SK)).copy(),
        "cos": cos, "sin": sin,
        "owner": (np.arange(EG)[:, None] == rows[None, :]).astype(np.float16),
        "before": np.broadcast_to((np.arange(E)[None, :] < np.arange(E)[:, None]).astype(np.float32)
                                  .reshape(1, E * E), (P, E * E)).copy(),
    }


def kernel(**inputs):
    import concourse.bacc as _bacc
    from concourse.bass_utils import run_bass_kernel_spmd as _run

    nc = _bacc.Bacc("TRN2", target_bir_lowering=False, num_devices=1)
    arrays, aps = {}, {}
    for name, v in [*inputs.items(), *constants().items()]:
        v = np.ascontiguousarray(v)
        arrays[f"in_{name}"] = v
        aps[name] = nc.dram_tensor(f"in_{name}", v.shape, mybir.dt.from_np(v.dtype), kind="ExternalInput").ap()
    aps["out"] = nc.dram_tensor("out_0", (NB, SQ, D), F32, kind="ExternalOutput").ap()
    build(nc, aps)
    r = _run(nc, [arrays], core_ids=[0])
    return r.results[0]["out_0"]
```

```python
from contextlib import ExitStack

import numpy as np

import concourse.bass as bass
from concourse import mybir

ALU = mybir.AluOpType
ACT = mybir.ActivationFunctionType
AX = mybir.AxisListType.X
F32 = mybir.dt.float32
F16 = mybir.dt.float16
F8 = mybir.dt.float8e4
I32 = mybir.dt.int32

P = 128
D = 256
KT = D // P
NB = 2
SQ = 256
SK = 512
TOK = NB * SQ
TT = TOK // P
KC = SK // P
H = 16
HD = 128
NEG = -1e30
LOWEST = -3.0e38

KVC, QC, R = 64, 96, 64
LOOKBACK = 8
SCALE0 = float(1.0 / np.sqrt(HD + R).astype(np.float32))

FT = 2048 // P
PK = 3 * P
BLK = 24

NIMG = 257
NTXT = SK - NIMG
SEG = ((0, NIMG), (NIMG, NTXT))
INNER = H * HD
SCALE1 = float(HD) ** -0.5

E, TOPK, IM, ISH = 16, 4, 176, 704
EG = E + 1
MROWS = E * IM + ISH
MT = (MROWS + P - 1) // P
MLAST = MROWS - (MT - 1) * P

PASSES = ((0, 0), (0, 1), (1, 0))


def build(nc, a):
    top = ExitStack()
    with top:
        sems = {}

        def sem(name):
            if name not in sems:
                sems[name] = top.enter_context(nc.semaphore(name))
            return sems[name]

        def tensors(stack, part="all"):
            return lambda name, shape, dt=F32: stack.enter_context(
                nc.sbuf_tensor(f"{part}_{name}", shape, dt))

        sb = tensors(top)
        bank = [top.enter_context(nc.psum_tensor(f"bank{i}", [P, 512], F32)) for i in range(8)]

        ident = sb("ident", [P, P])
        x = sb("x", [P, TT, D])
        xT = sb("xT", [P, 2, KT, TOK], F16)
        ctxT = sb("ctxT", [P, 2, KT, NB * SK], F16)
        ctxM = sb("ctxM", [P, 2, KT, NB, 2, P], F16)
        ln_st = sb("ln_st", [P, TT, 6])
        ln_mv = sb("ln_mv", [P, TT, 2])
        ln_ve = sb("ln_ve", [P, TT])
        ln_rs = sb("ln_rs", [P, TT])
        ln_x = sb("ln_x", [P, TT, D])
        mhalf = sb("mhalf", [P, 16])
        ahead = sb("ahead", [P, H * D])
        NST = 6
        stage = ahead[:, 0:NST * KT * 2 * HD].rearrange("p (s k n) -> p s k n", s=NST, k=KT)
        vrow = ahead[:, NST * KT * 2 * HD:NST * KT * 2 * HD + P]
        OW = ahead[:].bitcast(F16).rearrange("p (s h d) -> p s h d", s=2, h=H)
        HP = H // 2
        pieces = []
        for p in range(HP):
            for i, w in enumerate(("k_w", "ki_w", "v_w")):
                pieces.append((w, p, (p % 2) * 3 + i)
                              + (("p_vsplit", p + 1) if i == 2 else ("p_split", 2 * p + i + 1)))
        for p in range(HP):
            pieces.append(("q_w", p, (p % 2) * 2, "p_split", 2 * HP + p + 1))
            pieces.append(("vi_w", p, (p % 2) * 2 + 1, "p_vsplit", HP + p + 1))

        def load_piece(sync, n):
            w, p, slot, _, _ = pieces[n]
            sync.dma_start(stage[:, slot], a["L1_xattn_" + w]
                           .rearrange("(k p) n -> p k n", p=P)[:, :, p * 2 * HD:(p + 1) * 2 * HD])\
                .then_inc(sem(f"in_stage{slot}"), 16)

        pk = top.enter_context(ExitStack())
        packed = tensors(pk)("packed", [P, FT, PK], I32)
        pscale = tensors(pk)("pscale", [P, FT + 1, BLK])

        def ln_vector(dve, n):
            for t in range(TT):
                dve.bn_stats(ln_st[:, t, :], x[:, t, :]).then_inc(sem("ln_stats"), 1)
            for t in range(TT):
                dve.wait_ge(sem("ln_stats"), TT * n + t + 1)
                dve.bn_aggr(ln_mv[:, t, :], ln_st[:, t, :]).then_inc(sem("ln_aggr"), 1)
            dve.wait_ge(sem("ln_aggr"), TT * n + TT)
            dve.tensor_scalar(ln_ve[:], ln_mv[:, :, 1], 1e-5, None, ALU.add).then_inc(sem("ln_var"), 1)
            dve.wait_ge(sem("ln_rstd"), n + 1)
            for t in range(TT):
                dve.tensor_scalar(ln_x[:, t, :], x[:, t, :], ln_mv[:, t, 0:1], ln_rs[:, t:t + 1],
                                  ALU.subtract, ALU.mult).then_inc(sem("ln_x"), 1)

        def ln_pool(pool, n):
            pool.wait_ge(sem("ln_var"), n + 1)
            pool.tensor_tensor(ln_rs[:], ln_ve[:], mhalf[:, 0:TT], ALU.pow).then_inc(sem("ln_rstd"), 1)

        def ln_tensor(pe, n, banks):
            for t in range(TT):
                pe.wait_ge(sem("ln_x"), TT * n + t + 1)
                for k in range(KT):
                    last = pe.transpose(banks[k][:, t * P:(t + 1) * P], ln_x[:, t, k * P:(k + 1) * P], ident[:])
            last.then_inc(sem("ln_T"), 1)

        def ln_scalar(act, n, banks):
            act.wait_ge(sem("ln_T"), n + 1)
            for k in range(KT):
                act.activation(xT[:, 0, k, :], banks[k][:], ACT.Copy).then_inc(sem("ln_hi"), 1)

        def ln_vector_low(dve, n, banks):
            for k in range(KT):
                dve.wait_ge(sem("ln_hi"), KT * n + k + 1)
                dve.tensor_tensor(xT[:, 1, k, :], banks[k][:], xT[:, 0, k, :], ALU.subtract)\
                   .then_inc(sem("ln_lo"), 1)

        with ExitStack() as ph:
            sp = tensors(ph, "l0")
            Aq = sp("Aq", [QC, 2, H, P], F16)
            As = sp("As", [QC, 2, H, P], F16)
            qcT = sp("qcT", [QC, 2, TOK], F16)
            kF = sp("kF", [P, 2, NB * SK], F16)
            kv = sp("kv", [P, 2, NB * KC, KVC], F16)
            M = sp("M", [P, 2, H // 2, D], F16)
            mask = sp("mask", [P, TT, SK])
            cosT = sp("cosT", [P, SK])
            sinT = sp("sinT", [P, SK])

            def q_table(tab):
                return tab[:, 0:SQ].rearrange("p (b q) -> p b q", b=1).to_broadcast([P, NB, SQ])

            def by_batch(ap):
                return ap.rearrange("p (b q) -> p b q", b=NB)

            with ExitStack() as su:
                ss = tensors(su, "setup")
                ctx = ss("ctx", [P, NB * KC, D])
                wkvc = ss("wkvc", [P, KT, KVC])
                wdq = ss("wdq", [P, KT, QC])
                wkvcS = ss("wkvcS", [P, 2, KT, KVC], F16)
                wdqS = ss("wdqS", [P, 2, KT, QC], F16)
                wkr = ss("wkr", [KVC, 2, P])
                wuq = ss("wuq", [QC, H * HD])
                wqr = ss("wqr", [QC, H, R])
                wuk = ss("wuk", [KVC, H * HD])
                wuv = ss("wuv", [KVC, H * HD])
                wo = ss("wo", [P, H, D])
                uqT = ss("uqT", [P, H, QC])
                ukT = ss("ukT", [P, H, KVC])
                uvT = ss("uvT", [P, H, KVC])
                kvcT = ss("kvcT", [KVC, NB, SK])
                kidx = ss("kidx", [P, SK])
                segi = ss("segi", [P, TT], I32)
                segf = ss("segf", [P, TT])
                rc = ss("rc", [P, 2, SK])
                rs = ss("rs", [P, 2, SK])
                rk = ss("rk", [P, 2, SK])

                J_CTX, J_X, J_UQ, J_UK, J_UV, J_KVT, J_QC, J_KV, J_A, J_K, J_M, J_END = \
                    0, 4, 6, 10, 12, 14, 16, 17, 18, 20, 24, 28
                last_read = {J_X + k: ("ln_lo", k + 1) for k in range(KT)}
                last_read[J_QC] = ("qc_low", 1)
                for i, j in enumerate(range(J_UQ, J_KVT)):
                    last_read[j] = ("su_copied", i + 1)
                for i, j in enumerate([*range(J_CTX, J_X), *range(J_KVT, J_QC), *range(J_KV, J_END)]):
                    last_read[j] = ("su_read", i + 1)

                def is_read(eng, j):
                    name, count = last_read[j]
                    eng.wait_ge(sem(name), count)

                def is_full(eng, j):
                    eng.wait_ge(sem("su_full"), j + 1 - (KT if j > J_X else 0) - (j > J_QC))

                def fill(pe, j):
                    if j >= 8:
                        is_read(pe, j - 8)
                    return bank[j % 8]

                with nc.Block() as block:
                    @block.sync
                    def _(sync):
                        def load(name, dst, src):
                            sync.dma_start(dst, src).then_inc(sem("in_" + name), 16)
                        load("ident", ident[:], a["ident"])
                        load("x", x[:], a["x"].rearrange("b (t p) d -> p (b t) d", p=P))
                        for b in range(NB):
                            load(f"ctx{b}", ctx[:, b * KC:(b + 1) * KC, :],
                                 a["ctx_2048"][b].rearrange("(t p) d -> p t d", p=P))
                        load("proj", wkvc[:], a["L0_xattn_W_kvc"].rearrange("(k p) n -> p k n", p=P))
                        load("proj", wdq[:], a["L0_xattn_W_dq"].rearrange("(k p) n -> p k n", p=P))
                        load("wuq", wuq[:], a["L0_xattn_W_uq"])
                        load("wuk", wuk[:], a["L0_xattn_W_uk"])
                        load("wuv", wuv[:], a["L0_xattn_W_uv"])
                        load("wqr", wqr[:], a["L0_xattn_W_qr"].rearrange("c (h r) -> c h r", r=R))
                        sync.dma_start(segi[:], a["itok_BxS_0_1023"].rearrange("b (t p) -> p (b t)", p=P),
                                       allow_slow_non_contiguous=True).then_inc(sem("in_tables"), 16)
                        load("tables", kidx[:], a["kidx"])
                        load("wkr", wkr[:, 0, 0:KVC], a["ident"][0:KVC, 0:KVC])
                        load("wkr", wkr[:, 0, KVC:P], a["L0_xattn_W_kr"])
                        load("wkr", wkr[:, 1, KVC:KVC + R // 2], a["L0_xattn_W_kr"][:, R // 2:R])
                        load("wkr", wkr[:, 1, KVC + R // 2:P], a["L0_xattn_W_kr"][:, 0:R // 2])
                        load("tables", cosT[:], a["cos"])
                        load("tables", sinT[:], a["sin"])
                        load("wo", wo[:], a["L0_xattn_W_o"].rearrange("(h p) n -> p h n", p=P))
                        for n, w in enumerate(("gate", "up")):
                            load("packed", packed[:, :, n * P:(n + 1) * P],
                                 a[f"L0_ffn_{w}_W_packed"].rearrange("(t p) k -> p t k", p=P))
                            load("packed", pscale[:, 0:FT, n * 8:n * 8 + 8],
                                 a[f"L0_ffn_{w}_scales"].rearrange("(t p) k -> p t k", p=P))
                        for m in range(KT):
                            load("packed", packed[:, :, 2 * P + m * 64:2 * P + m * 64 + 64],
                                 a["L0_ffn_down_W_packed"][m * P:(m + 1) * P, :]
                                 .rearrange("p (t k) -> p t k", t=FT))
                            load("packed", pscale[:, 0:FT, 16 + 4 * m:20 + 4 * m],
                                 a["L0_ffn_down_scales"][m * P:(m + 1) * P, :]
                                 .rearrange("p (t k) -> p t k", t=FT))
                        for n, name in enumerate(("q_b", "k_b", "ki_b", "nq_s", "nkt_s", "nki_s", "v_b",
                                                  "vi_b")):
                            sync.dma_start(vrow[n * H:(n + 1) * H, :],
                                           a["L1_xattn_" + name].rearrange("(h p) -> h p", p=P))\
                                .then_inc(sem("in_vec"), 16)
                        for n in range(NST):
                            load_piece(sync, n)

                    @block.gpsimd
                    def _(pool):
                        pool.memset(mhalf[:], -0.5).then_inc(sem("half"), 1)
                        pool.memset(pscale[:, FT, :], 0.0).then_inc(sem("half"), 1)
                        pool.memset(As[:, :, :, 0:KVC], 0.0).then_inc(sem("half"), 1)
                        pool.memset(wkr[:, 1, 0:KVC], 0.0).then_inc(sem("wkr_zero"), 1)
                        pool.memset(ctxM[:], 0.0).then_inc(sem("ctxM_zero"), 1)
                        pool.wait_ge(sem("half"), 3)
                        ln_pool(pool, 0)
                        pool.wait_ge(sem("in_proj"), 32)
                        pool.tensor_copy(wkvcS[:, 0], wkvc[:]).then_inc(sem("wsplit"), 1)
                        pool.tensor_copy(wdqS[:, 0], wdq[:]).then_inc(sem("wsplit"), 1)
                        pool.wait_ge(sem("wsplit"), 2)
                        pool.tensor_tensor(wkvcS[:, 1], wkvc[:], wkvcS[:, 0], ALU.subtract)\
                            .then_inc(sem("wsplit"), 1)
                        pool.tensor_tensor(wdqS[:, 1], wdq[:], wdqS[:, 0], ALU.subtract)\
                            .then_inc(sem("wsplit"), 1)
                        pool.wait_ge(sem("ctxM_zero"), 1)
                        is_read(pool, J_CTX + 3)
                        for k in range(KT):
                            c = ctxT[:, :, k, :].rearrange("p s (b j) -> p s b j", b=NB)
                            c0 = NIMG - 1
                            for part in range(2):
                                pool.tensor_copy(ctxM[:, part, k, :, 0, 0:1], c[:, part, :, c0:c0 + 1])\
                                   .then_inc(sem("ctxM"), 1)
                                pool.tensor_copy(ctxM[:, part, k, :, 1, 1:P], c[:, part, :, c0 + 1:c0 + P])\
                                   .then_inc(sem("ctxM"), 1)
                        pool.wait_ge(sem("rope_hi"), 1)
                        pool.tensor_tensor(Aq[:, 1, :, KVC:P], wqr[:], Aq[:, 0, :, KVC:P], ALU.subtract)\
                            .then_inc(sem("rope_hi"), 1)
                        hR = R // 2
                        pool.wait_ge(sem("half"), 3)
                        pool.wait_ge(sem("rope_hi"), 2)
                        for part in range(2):
                            pool.tensor_copy(As[:, part, :, KVC:KVC + hR], Aq[:, part, :, KVC + hR:P])\
                               .then_inc(sem("rope_swap"), 1)
                            pool.tensor_copy(As[:, part, :, KVC + hR:P], Aq[:, part, :, KVC:KVC + hR])\
                               .then_inc(sem("rope_swap"), 1)
                        for t in range(TT):
                            pool.wait_ge(sem("mask_dist"), t + 1)
                            pool.tensor_scalar(mask[:, t, :], mask[:, t, :], (LOOKBACK / 2) ** 2, NEG,
                                               ALU.is_gt, ALU.mult).then_inc(sem("mask"), 1)

                    @block.tensor
                    def _(pe):
                        pe.wait_ge(sem("in_ident"), 16)
                        for b in range(NB):
                            pe.wait_ge(sem(f"in_ctx{b}"), 16)
                            for k in range(KT):
                                out = fill(pe, J_CTX + KT * b + k)
                                for c in range(KC):
                                    last = pe.transpose(out[:, c * P:(c + 1) * P],
                                                        ctx[:, b * KC + c, k * P:(k + 1) * P], ident[:])
                                last.then_inc(sem("su_full"), 1)
                        ln_banks = [fill(pe, J_X + k) for k in range(KT)]
                        ln_tensor(pe, 0, ln_banks)
                        pe.wait_ge(sem("in_wuq"), 16)
                        for g in range(4):
                            out = fill(pe, J_UQ + g)
                            for i in range(4):
                                h = 4 * g + i
                                last = pe.transpose(out[:, i * QC:(i + 1) * QC],
                                                    wuq[:, h * HD:(h + 1) * HD], ident[0:QC, 0:QC])
                            last.then_inc(sem("su_full"), 1)
                        for j, w, ready in ((J_UK, wuk, "in_wuk"), (J_UV, wuv, "in_wuv")):
                            pe.wait_ge(sem(ready), 16)
                            for g in range(2):
                                out = fill(pe, j + g)
                                for i in range(8):
                                    h = 8 * g + i
                                    last = pe.transpose(out[:, i * KVC:(i + 1) * KVC],
                                                        w[:, h * HD:(h + 1) * HD], ident[0:KVC, 0:KVC])
                                last.then_inc(sem("su_full"), 1)
                        pe.wait_ge(sem("wsplit"), 4)
                        for b in range(NB):
                            out = fill(pe, J_KVT + b)
                            if b == 0:
                                is_read(pe, J_CTX + 3)
                            n = 0
                            for k in range(KT):
                                for l, r in PASSES:
                                    last = pe.matmul(out[0:KVC, :], wkvcS[:, l, k, :],
                                                     ctxT[:, r, k, b * SK:(b + 1) * SK],
                                                     start=(n == 0), stop=(n == 5))
                                    n += 1
                            last.then_inc(sem("su_full"), 1)
                        out = fill(pe, J_QC)
                        pe.wait_ge(sem("ln_lo"), KT)
                        n = 0
                        for k in range(KT):
                            for l, r in PASSES:
                                last = pe.matmul(out[0:QC, :], wdqS[:, l, k, :], xT[:, r, k, :],
                                                 start=(n == 0), stop=(n == 5))
                                n += 1
                        last.then_inc(sem("su_full2"), 1)
                        out = fill(pe, J_KV)
                        for c in range(NB * KC):
                            n = 0
                            for k in range(KT):
                                for l, r in PASSES:
                                    last = pe.matmul(out[:, c * KVC:(c + 1) * KVC],
                                                     ctxT[:, l, k, c * P:(c + 1) * P], wkvcS[:, r, k, :],
                                                     start=(n == 0), stop=(n == 5))
                                    n += 1
                        last.then_inc(sem("su_full"), 1)
                        is_read(pe, J_UK + 1)
                        for g in range(2):
                            out = fill(pe, J_A + g)
                            for i in range(8):
                                h = 8 * g + i
                                last = pe.matmul(out[0:QC, i * KVC:(i + 1) * KVC], uqT[:, h, :], ukT[:, h, :],
                                                 start=True, stop=True)
                            last.then_inc(sem("su_full"), 1)
                        pe.wait_ge(sem("in_wkr"), 64)
                        pe.wait_ge(sem("wkr_zero"), 1)
                        is_read(pe, J_KVT + 1)
                        for b in range(NB):
                            for s in range(2):
                                out = fill(pe, J_K + 2 * b + s)
                                pe.matmul(out[:, :], wkr[:, s, :], kvcT[:, b, :], start=True, stop=True)\
                                  .then_inc(sem("su_full"), 1)
                        pe.wait_ge(sem("in_wo"), 16)
                        is_read(pe, J_UV + 1)
                        for g in range(4):
                            out = fill(pe, J_M + g)
                            for i in range(4):
                                h = 4 * g + i
                                lo = (h % 2) * KVC
                                last = pe.matmul(out[lo:lo + KVC, (i // 2) * D:(i // 2 + 1) * D],
                                                 uvT[:, h, :], wo[:, h, :], start=True, stop=True)
                            last.then_inc(sem("su_full"), 1)

                    @block.scalar
                    def _(act):
                        def high(j, dst, src):
                            is_full(act, j)
                            act.activation(dst, src, ACT.Copy).then_inc(sem("su_high"), 1)

                        def plain(j, dst, src):
                            is_full(act, j)
                            act.activation(dst, src, ACT.Copy).then_inc(sem("su_copied"), 1)
                        for b in range(NB):
                            for k in range(KT):
                                high(J_CTX + KT * b + k, ctxT[:, 0, k, b * SK:(b + 1) * SK],
                                     bank[(J_CTX + KT * b + k) % 8][:])
                        ln_scalar(act, 0, [bank[(J_X + k) % 8] for k in range(KT)])
                        for g in range(4):
                            plain(J_UQ + g, uqT[:, 4 * g:4 * g + 4, :],
                                  bank[(J_UQ + g) % 8][:, 0:4 * QC].rearrange("p (h n) -> p h n", n=QC))
                        for j, dst in ((J_UK, ukT), (J_UV, uvT)):
                            for g in range(2):
                                plain(j + g, dst[:, 8 * g:8 * g + 8, :],
                                      bank[(j + g) % 8][:].rearrange("p (h n) -> p h n", n=KVC))
                        act.wait_ge(sem("in_wqr"), 16)
                        act.activation(Aq[:, 0, :, KVC:P], wqr[:], ACT.Copy).then_inc(sem("rope_hi"), 1)
                        act.wait_ge(sem("su_full2"), 1)
                        act.activation(qcT[:, 0, :], bank[J_QC % 8][0:QC, :], ACT.Copy)\
                           .then_inc(sem("qc_high"), 1)
                        high(J_KV, kv[:, 0].rearrange("p c n -> p (c n)"), bank[J_KV % 8][:])
                        for g in range(2):
                            high(J_A + g, Aq[:, 0, 8 * g:8 * g + 8, 0:KVC],
                                 bank[(J_A + g) % 8][0:QC, :].rearrange("p (h n) -> p h n", n=KVC))
                        act.wait_ge(sem("segf"), 1)
                        for t in range(TT):
                            act.activation(mask[:, t, :], kidx[:], ACT.Square, bias=segf[:, t:t + 1])\
                               .then_inc(sem("mask_dist"), 1)
                        for b in range(NB):
                            act.wait_ge(sem("k_roped"), b + 1)
                            act.activation(kF[:, 0, b * SK:(b + 1) * SK], rk[:, b, :], ACT.Copy)\
                               .then_inc(sem("k_high"), 1)
                        for g in range(4):
                            high(J_M + g, M[:, 0, 2 * g:2 * g + 2, :],
                                 bank[(J_M + g) % 8][:].rearrange("p (h n) -> p h n", n=D))

                    @block.vector
                    def _(dve):
                        n_high = [0]

                        def low(dst, src, high):
                            n_high[0] += 1
                            dve.wait_ge(sem("su_high"), n_high[0])
                            dve.tensor_tensor(dst, src, high, ALU.subtract).then_inc(sem("su_read"), 1)

                        def plain(j, dst, src):
                            is_full(dve, j)
                            dve.tensor_copy(dst, src).then_inc(sem("su_read"), 1)

                        dve.wait_ge(sem("in_x"), 16)
                        ln_vector(dve, 0)
                        for b in range(NB):
                            for k in range(KT):
                                s = slice(b * SK, (b + 1) * SK)
                                low(ctxT[:, 1, k, s], bank[(J_CTX + KT * b + k) % 8][:], ctxT[:, 0, k, s])
                        ln_vector_low(dve, 0, [bank[(J_X + k) % 8] for k in range(KT)])
                        dve.wait_ge(sem("in_tables"), 64)
                        dve.tensor_scalar(segf[:], segi[:], -1.0, LOOKBACK / 2, ALU.mult, ALU.add)\
                           .then_inc(sem("segf"), 1)
                        for b in range(NB):
                            plain(J_KVT + b, kvcT[:, b, :], bank[(J_KVT + b) % 8][0:KVC, :])
                        dve.wait_ge(sem("qc_high"), 1)
                        dve.tensor_tensor(qcT[:, 1, :], bank[J_QC % 8][0:QC, :], qcT[:, 0, :], ALU.subtract)\
                           .then_inc(sem("qc_low"), 1)
                        low(kv[:, 1].rearrange("p c n -> p (c n)"), bank[J_KV % 8][:],
                            kv[:, 0].rearrange("p c n -> p (c n)"))
                        for g in range(2):
                            low(Aq[:, 1, 8 * g:8 * g + 8, 0:KVC],
                                bank[(J_A + g) % 8][0:QC, :].rearrange("p (h n) -> p h n", n=KVC),
                                Aq[:, 0, 8 * g:8 * g + 8, 0:KVC])
                        for b in range(NB):
                            j = J_K + 2 * b
                            is_full(dve, j + 1)
                            dve.tensor_tensor(rc[:, b, :], bank[j % 8][:], cosT[:], ALU.mult)\
                               .then_inc(sem("su_read"), 1)
                            dve.tensor_tensor(rs[:, b, :], bank[(j + 1) % 8][:], sinT[:], ALU.mult)\
                               .then_inc(sem("su_read"), 1)
                            is_read(dve, j + 1)
                            dve.tensor_tensor(rk[:, b, :], rc[:, b, :], rs[:, b, :], ALU.add)\
                               .then_inc(sem("k_roped"), 1)
                        for b in range(NB):
                            s = slice(b * SK, (b + 1) * SK)
                            dve.wait_ge(sem("k_high"), b + 1)
                            dve.tensor_tensor(kF[:, 1, s], rk[:, b, :], kF[:, 0, s], ALU.subtract)\
                               .then_inc(sem("k_low"), 1)
                        for g in range(4):
                            low(M[:, 1, 2 * g:2 * g + 2, :],
                                bank[(J_M + g) % 8][:].rearrange("p (h n) -> p h n", n=D),
                                M[:, 0, 2 * g:2 * g + 2, :])

            fe = tensors(ph, "ffn")
            y1 = fe("y1", [P, PK], I32)
            y2 = fe("y2", [P, PK], I32)
            y3 = fe("y3", [P, PK], I32)
            codes = fe("codes", [P, 2, PK], I32)
            sc = fe("sc", [P, 2, BLK])
            W = fe("W", [P, 4, 2 * PK])

            def over_blocks(ap):
                return ap.rearrange("p (b k f) -> p b k f", b=BLK, f=2)

            AHEAD = 4

            def fetch_scales(pool, i, u):
                pool.tensor_copy(sc[:, u % 2, :], pscale[:, bass.ds(i, 1), :]
                                 .rearrange("p o b -> p (o b)")).then_inc(sem("f_sc"), 1)

            def scaled(pool, i, u):
                pool.wait_ge(sem("f_w"), i + 2)
                pool.wait_ge(sem("f_codes"), i + 1)
                pool.wait_ge(sem("f_tr"), i + 1)
                pool.wait_ge(sem("f_sc"), i + 1)
                fetch_scales(pool, i + 1, u + 1)
                value = codes[:, u % 2, :].bitcast(F8)\
                    .rearrange("p (b k f) -> p b k f", b=BLK, f=4)[:, :, :, 0:2]
                scale = sc[:, u % 2, :].rearrange("p (b o q) -> p b o q", o=1, q=1)\
                    .to_broadcast([P, BLK, 16, 2])
                pool.tensor_tensor(over_blocks(W[:, u % 4, :]), value, scale, ALU.mult)\
                    .then_inc(sem("f_w"), 1)

            shl, band, bor = ALU.logical_shift_left, ALU.bitwise_and, ALU.bitwise_or

            def decode(dve, i, u, part=None):
                if part != 1:
                    src = packed[:, bass.ds(i, 1), :].rearrange("p o k -> p (o k)")
                    dve.wait_ge(sem("f_dec"), 5 * i + 1)
                    dve.tensor_scalar(y1[:], src, 4, 0xF00, shl, band).then_inc(sem("f_dec"), 1)
                    dve.tensor_scalar(y2[:], src, 0xF, None, band).then_inc(sem("f_dec"), 1)
                    dve.wait_ge(sem("f_dec"), 5 * i + 3)
                    dve.tensor_tensor(y3[:], y1[:], y2[:], bor).then_inc(sem("f_dec"), 1)
                if part != 0:
                    dve.wait_ge(sem("f_dec"), 5 * i + 4)
                    dve.tensor_scalar(y1[:], y3[:], 4, 0x8080, shl, band).then_inc(sem("f_dec"), 1)
                    dve.tensor_scalar(y2[:], y3[:], 2, 0x1C1C, shl, band).then_inc(sem("f_dec"), 1)
                    dve.wait_ge(sem("f_dec"), 5 * i + 6)
                    dve.wait_ge(sem("f_w"), i + 1)
                    dve.tensor_tensor(codes[:, u % 2, :], y1[:], y2[:], bor)\
                       .then_inc(sem("f_codes"), 1)
                    dve.wait_ge(sem("f_codes"), i + 1)

            with ExitStack() as at:
                s_ = tensors(at, "l0head")
                tc = s_("tc", [P, 2, TOK])
                ts_ = s_("ts", [P, 2, TOK])
                tq = s_("tq", [P, 2, TOK])
                Q = s_("Q", [P, 2, 2, TOK], F16)
                X = s_("X", [P, TT, SK])
                PT = s_("PT", [P, 2, 2, SK], F16)
                nm = s_("nm", [P, TT])
                den = s_("den", [P, 2 * TT])
                rden = s_("rden", [P, 2 * TT])
                O = s_("O", [P, TT, H * KVC])
                OT = s_("OT", [P, 2, 2, TOK], F16)
                SB, TB, QA, QS, OB = bank[0:2], bank[2:4], bank[4], bank[5], bank[6:8]
                ACC = bank[4:6]

                with nc.Block() as block:
                    @block.tensor
                    def _(pe):
                        def project(h):
                            pe.wait_ge(sem("a_qread"), 2 * h)
                            for out, w in ((QA, Aq), (QS, As)):
                                for n, (l, r) in enumerate(PASSES):
                                    last = pe.matmul(out[:], w[:, l, bass.ds(h, 1), :], qcT[:, r, :],
                                                     start=(n == 0), stop=(n == 2))
                            last.then_inc(sem("a_qfull"), 1)

                        def scores(h, t, par):
                            if t == 0:
                                pe.wait_ge(sem("a_qlow"), h + 1)
                            n = 4 * h + t
                            pe.wait_ge(sem("a_max"), n + 1)
                            b = t // 2
                            for i, (l, r) in enumerate(PASSES):
                                last = pe.matmul(SB[t % 2][:], Q[:, par, l, t * P:(t + 1) * P],
                                                 kF[:, r, b * SK:(b + 1) * SK], start=(i == 0), stop=(i == 2))
                            last.then_inc(sem("a_sfull"), 1)

                        def turn(h, t):
                            n = 4 * h + t
                            pe.wait_ge(sem("a_exp"), n + 1)
                            pe.wait_ge(sem("a_ptlow"), n + 1)
                            for c in range(KC):
                                last = pe.transpose(TB[t % 2][:, c * P:(c + 1) * P],
                                                    X[:, t, c * P:(c + 1) * P], ident[:])
                            last.then_inc(sem("a_tfull"), 1)

                        def attend(h, t):
                            n = 4 * h + t
                            pe.wait_ge(sem("a_ptlow"), n + 3)
                            pe.wait_ge(sem("a_oread"), n + 1)
                            b = t // 2
                            i = 0
                            for c in range(KC):
                                for l, r in PASSES:
                                    last = pe.matmul(OB[t % 2][:, 0:KVC], PT[:, t % 2, l, c * P:(c + 1) * P],
                                                     kv[:, r, b * KC + c, :], start=(i == 0),
                                                     stop=(i == 3 * KC - 1))
                                    i += 1
                            last.then_inc(sem("a_ofull"), 1)

                        def step(h, par, first=False, last=False, late=False):
                            for t in range(TT):
                                turn(h, t)
                                if not last:
                                    scores(h + 1, t, 1 - par)
                                if t:
                                    attend(h, t - 1)
                                elif not first:
                                    attend(h - 1, TT - 1)
                                if t == TT - 1 and not late:
                                    project(h + 3)

                        project(0)
                        project(1)
                        for t in range(TT):
                            scores(0, t, 0)
                        project(2)
                        step(0, 0, first=True)
                        step(1, 1)
                        with pe.Fori(1, H // 2 - 2) as g:
                            step(2 * g, 0)
                            step(2 * g + 1, 1)
                        step(H - 4, 0)
                        step(H - 3, 1, late=True)
                        step(H - 2, 0, late=True)
                        step(H - 1, 1, last=True, late=True)
                        attend(H - 1, TT - 1)

                        def turn_o(j):
                            if j >= 2:
                                pe.wait_ge(sem("a_otlow"), j - 1)
                            for t in range(TT):
                                last = pe.transpose(TB[j % 2][:, t * P:(t + 1) * P],
                                                    O[:, t, j * P:(j + 1) * P], ident[:])
                            last.then_inc(sem("a_otfull"), 1)
                        pe.wait_ge(sem("a_oread"), 4 * H + 2)
                        turn_o(0)
                        for j in range(H // 2):
                            if j + 1 < H // 2:
                                turn_o(j + 1)
                            pe.wait_ge(sem("a_otlow"), j + 1)
                            for t in range(TT):
                                for n, (l, r) in enumerate(PASSES):
                                    last = pe.matmul(ACC[t // 2][:, (t % 2) * D:(t % 2 + 1) * D],
                                                     OT[:, j % 2, l, t * P:(t + 1) * P], M[:, r, j, :],
                                                     start=(j == 0 and n == 0 and t % 2 == 0),
                                                     stop=(j == H // 2 - 1 and n == 2),
                                                     skip_group_check=True)
                            last.then_inc(sem("a_omm"), 1)

                    @block.scalar
                    def _(act):
                        def q_high(h, par):
                            act.wait_ge(sem("a_qsum"), h + 1)
                            act.activation(Q[:, par, 0, :], tq[:, par, :], ACT.Copy).then_inc(sem("a_qhigh"), 1)

                        def exp(h, t, par):
                            n = 4 * h + t
                            act.wait_ge(sem("a_max"), n + 3)
                            act.activation(X[:, t, :], X[:, t, :], ACT.Exp, bias=nm[:, t:t + 1], scale=-1.0,
                                           accum_out=den[:, par * TT + t:par * TT + t + 1])\
                               .then_inc(sem("a_exp"), 1)

                        def pt_high(h, t):
                            n = 4 * h + t
                            act.wait_ge(sem("a_tfull"), n + 1)
                            act.wait_ge(sem("a_ofull"), n + 1)
                            act.activation(PT[:, t % 2, 0, :], TB[t % 2][:], ACT.Copy)\
                               .then_inc(sem("a_pthigh"), 1)

                        def o_out(h, t, par):
                            i = par * TT + t
                            act.activation(O[:, t, bass.ds(h * KVC, KVC)], OB[t % 2][:, 0:KVC], ACT.Copy,
                                           scale=rden[:, i:i + 1]).then_inc(sem("a_oread"), 1)

                        def step(h, par, first=False, last=False, late=False):
                            for t in range(TT):
                                out = not first or t >= 2
                                if out:
                                    act.wait_ge(sem("a_rden"), 4 * h + t - 1)
                                pt_high(h, t)
                                if t >= 2:
                                    o_out(h, t - 2, par)
                                elif out:
                                    o_out(h - 1, t + 2, 1 - par)
                                if t == 0:
                                    exp(h, 3, par)
                                elif not last:
                                    exp(h + 1, t - 1, 1 - par)
                                if t == 2 and not late:
                                    q_high(h + 2, par)

                        act.nop().then_inc(sem("a_ofull"), 2)
                        act.nop().then_inc(sem("a_oread"), 2)
                        act.nop().then_inc(sem("f_tr"), 4)
                        q_high(0, 0)
                        for t in range(3):
                            exp(0, t, 0)
                        q_high(1, 1)
                        step(0, 0, first=True)
                        step(1, 1)
                        with act.Fori(1, H // 2 - 1) as g:
                            step(2 * g, 0)
                            step(2 * g + 1, 1)
                        step(H - 2, 0, late=True)
                        step(H - 1, 1, last=True, late=True)
                        for t in range(2, 4):
                            act.wait_ge(sem("a_rden"), 4 * (H - 1) + t + 1)
                            act.wait_ge(sem("a_ofull"), 4 * (H - 1) + t + 3)
                            o_out(H - 1, t, 1)
                        for j in range(H // 2):
                            act.wait_ge(sem("a_otfull"), j + 1)
                            if j >= 2:
                                act.wait_ge(sem("a_omm"), j - 1)
                            act.activation(OT[:, j % 2, 0, :], TB[j % 2][:], ACT.Copy)\
                               .then_inc(sem("a_othigh"), 1)

                    @block.gpsimd
                    def _(pool):
                        def q_sum(h, par):
                            pool.wait_ge(sem("a_qread"), 2 * h + 2)
                            pool.tensor_tensor(tq[:, par, :], tc[:, par, :], ts_[:, par, :], ALU.add)\
                                .then_inc(sem("a_qsum"), 1)
                            pool.wait_ge(sem("a_qhigh"), h + 1)
                            pool.tensor_tensor(Q[:, par, 1, :], tq[:, par, :], Q[:, par, 0, :], ALU.subtract)\
                                .then_inc(sem("a_qlow"), 1)
                        with pool.Fori(0, H // 2) as g:
                            q_sum(2 * g, 0)
                            q_sum(2 * g + 1, 1)
                        pool.nop().then_inc(sem("f_w"), 2)
                        pool.wait_ge(sem("f_scale64"), 1)
                        fetch_scales(pool, 0, 0)
                        for i in range(AHEAD):
                            scaled(pool, i, i)

                    @block.vector
                    def _(dve):
                        def q_cos(h, par):
                            dve.wait_ge(sem("a_qfull"), h + 1)
                            dve.tensor_tensor(by_batch(tc[:, par, :]), by_batch(QA[:]), q_table(cosT),
                                              ALU.mult).then_inc(sem("a_qread"), 1)

                        def q_sin(h, par):
                            dve.wait_ge(sem("a_qfull"), h + 1)
                            dve.tensor_tensor(by_batch(ts_[:, par, :]), by_batch(QS[:]), q_table(sinT),
                                              ALU.mult).then_inc(sem("a_qread"), 1)

                        def top_score(h, t):
                            dve.tensor_tensor_reduce(X[:, t, :], SB[t % 2][:], mask[:, t, :], -SCALE0,
                                                     -LOWEST, ALU.add, ALU.min, nm[:, t:t + 1])\
                               .then_inc(sem("a_max"), 1)

                        def pt_low(h, t):
                            n = 4 * h + t
                            dve.wait_ge(sem("a_pthigh"), n + 1)
                            dve.tensor_tensor(PT[:, t % 2, 1, :], TB[t % 2][:], PT[:, t % 2, 0, :],
                                              ALU.subtract).then_inc(sem("a_ptlow"), 1)

                        def o_den(par, t):
                            i = par * TT + t
                            dve.reciprocal(rden[:, i:i + 1], den[:, i:i + 1]).then_inc(sem("a_rden"), 1)

                        def step(h, par, first=False, last=False, late=False):
                            for t in range(TT):
                                if t < 2 and not late:
                                    (q_cos, q_sin)[t](h + 2, par)
                                if not last:
                                    dve.wait_ge(sem("a_sfull"), 4 * (h + 1) + t + 1)
                                if t:
                                    o_den(par, t - 1)
                                elif not first:
                                    o_den(1 - par, TT - 1)
                                if not last:
                                    top_score(h + 1, t)
                                pt_low(h, t)
                                if last:
                                    decode(dve, t // 2, t // 2, part=t % 2)

                        for credit in ("a_max", "a_ptlow"):
                            dve.nop().then_inc(sem(credit), 2)
                        for h in range(2):
                            q_cos(h, h)
                            q_sin(h, h)
                        for t in range(TT):
                            dve.wait_ge(sem("a_sfull"), t + 1)
                            top_score(0, t)
                        step(0, 0, first=True)
                        step(1, 1)
                        with dve.Fori(1, H // 2 - 1) as g:
                            step(2 * g, 0)
                            step(2 * g + 1, 1)
                        step(H - 2, 0, late=True)
                        dve.nop().then_inc(sem("f_dec"), 1)
                        dve.wait_ge(sem("in_packed"), 128)
                        sall = pscale[:].rearrange("p t b -> p (t b)")
                        dve.tensor_scalar(sall, sall, 64.0, None, ALU.mult).then_inc(sem("f_scale64"), 1)
                        step(H - 1, 1, last=True, late=True)
                        o_den(1, TT - 1)
                        for j in range(H // 2):
                            dve.wait_ge(sem("a_othigh"), j + 1)
                            dve.tensor_tensor(OT[:, j % 2, 1, :], TB[j % 2][:], OT[:, j % 2, 0, :],
                                              ALU.subtract).then_inc(sem("a_otlow"), 1)
                            if j in (1, 3, 5, 6):
                                i = 2 + j // 4
                                decode(dve, i, i, part=int(j in (3, 6)))
                        dve.wait_ge(sem("a_omm"), H // 2)
                        for i in range(2):
                            xs = x[:, 2 * i:2 * i + 2, :].rearrange("p t d -> p (t d)")
                            dve.tensor_tensor(xs, ACC[i][:], xs, ALU.add).then_inc(sem("residual"), 1)

            with ExitStack() as ff:
                s_ = tensors(ff, "ffn")
                WG = s_("WG", [P, 2, 2, 4, P], F16)
                WD = s_("WD", [P, 4, 2, D], F16)
                gl = s_("gl", [P, 2, TOK])
                it = s_("it", [P, 2, TOK])
                IN = s_("IN", [P, 4, 2, TOK], F16)
                zero = s_("zero", [P, P], F16)
                WB, WB2, ACC = bank[0], bank[1], bank[6:8]
                GB, UB = (bank[2], bank[4]), (bank[3], bank[5])
                LAST = FT - 1

                with nc.Block() as block:
                    @block.gpsimd
                    def _(pool):
                        def in_low(i, u):
                            pool.wait_ge(sem("f_ihigh"), i + 1)
                            pool.tensor_tensor(IN[:, u % 4, 1, :], it[:, u % 2, :], IN[:, u % 4, 0, :],
                                               ALU.subtract).then_inc(sem("f_ilow"), 1)

                        pool.memset(zero[:], 0.0).then_inc(sem("f_zero"), 1)
                        pool.nop().then_inc(sem("f_ilow"), 2)
                        ln_pool(pool, 1)
                        scaled(pool, AHEAD, AHEAD)
                        in_low(0, 0)
                        in_low(1, 1)
                        with pool.Fori(0, 2) as g:
                            for u in range(1, 5):
                                scaled(pool, 4 * g + u + 4, u + 4)
                                in_low(4 * g + u + 1, u + 1)
                        for i in range(9, LAST):
                            if i + 4 < FT:
                                scaled(pool, i + 4, i + 4)
                            in_low(i + 1, i + 1)

                    @block.tensor
                    def _(pe):
                        def turn(i, u):
                            pe.wait_ge(sem("f_w"), i + 3)
                            pe.wait_ge(sem("f_wlow"), 2 * i + 2)
                            for m in range(6):
                                out = WB[:, m * P:(m + 1) * P] if m < 4 else WB2[:, (m - 4) * P:(m - 3) * P]
                                last = pe.transpose(out, W[:, u % 4, m * P:(m + 1) * P], ident[:])
                            last.then_inc(sem("f_tr"), 1)

                        def gate_up(i, u):
                            pe.wait_ge(sem("f_wlow"), 2 * i + 4)
                            pe.wait_ge(sem("f_uread"), i + 1)
                            for m, out in enumerate((GB[u % 2], UB[u % 2])):
                                n = 0
                                for k in range(KT):
                                    for l, r in PASSES:
                                        last = pe.matmul(out[:], WG[:, u % 2, l, 2 * m + k, :], xT[:, r, k, :],
                                                         start=(n == 0), stop=(n == 5))
                                        n += 1
                            last.then_inc(sem("f_gu"), 1)

                        def down(i, u):
                            pe.wait_ge(sem("f_ilow"), i + 3)
                            for t in range(TT):
                                for l, r in PASSES:
                                    last = pe.matmul(ACC[t // 2][:, (t % 2) * D:(t % 2 + 1) * D],
                                                     IN[:, u % 4, l, t * P:(t + 1) * P], WD[:, u % 4, r, :],
                                                     start=False, stop=False, skip_group_check=True)
                            last.then_inc(sem("f_dn"), 1)

                        pe.wait_ge(sem("f_zero"), 1)
                        for acc in ACC:
                            pe.matmul(acc[:], zero[:], xT[:, 0, 0, :], start=True, stop=False,
                                      skip_group_check=True)
                        turn(0, 0)
                        ln_tensor(pe, 1, bank[2:4])
                        turn(1, 1)
                        pe.wait_ge(sem("ln_lo"), 2 * KT)
                        gate_up(0, 0)
                        turn(2, 2)
                        gate_up(1, 1)
                        with pe.Fori(0, 3) as g:
                            for u in range(1, 5):
                                turn(4 * g + u + 2, u + 2)
                                gate_up(4 * g + u + 1, u + 1)
                                down(4 * g + u - 1, u - 1)
                        for i in range(13, FT + 1):
                            if i + 2 < FT:
                                turn(i + 2, i + 2)
                            if i + 1 < FT:
                                gate_up(i + 1, i + 1)
                            down(i - 1, i - 1)

                    @block.scalar
                    def _(act):
                        def w_high(i, u):
                            act.wait_ge(sem("f_tr"), i + 5)
                            act.activation(WG[:, u % 2, 0].rearrange("p m n -> p (m n)"), WB[:], ACT.Copy)\
                               .then_inc(sem("f_whigh"), 1)
                            act.activation(WD[:, u % 4, 0, :], WB2[:, 0:D], ACT.Copy)\
                               .then_inc(sem("f_whigh"), 1)

                        def gelu(i, u):
                            act.wait_ge(sem("f_gu"), i + 1)
                            act.activation(gl[:, u % 2, :], GB[u % 2][:], ACT.Gelu_apprx_tanh)\
                               .then_inc(sem("f_gelu"), 1)

                        def in_high(i, u):
                            act.wait_ge(sem("f_uread"), i + 3)
                            act.activation(IN[:, u % 4, 0, :], it[:, u % 2, :], ACT.Copy)\
                               .then_inc(sem("f_ihigh"), 1)

                        w_high(0, 0)
                        ln_scalar(act, 1, bank[2:4])
                        w_high(1, 1)
                        gelu(0, 0)
                        w_high(2, 2)
                        in_high(0, 0)
                        gelu(1, 1)
                        with act.Fori(0, 3) as g:
                            for u in range(1, 5):
                                w_high(4 * g + u + 2, u + 2)
                                in_high(4 * g + u, u)
                                gelu(4 * g + u + 1, u + 1)
                        for i in range(13, LAST):
                            if i + 2 < FT:
                                w_high(i + 2, i + 2)
                            in_high(i, i)
                            gelu(i + 1, i + 1)
                        in_high(LAST, LAST)

                    @block.vector
                    def _(dve):
                        def w_low(i, u):
                            dve.wait_ge(sem("f_whigh"), 2 * i + 2)
                            wg = WG[:, u % 2, 0].rearrange("p m n -> p (m n)")
                            dve.tensor_tensor(WG[:, u % 2, 1].rearrange("p m n -> p (m n)"), WB[:], wg,
                                              ALU.subtract).then_inc(sem("f_wlow"), 1)
                            dve.tensor_tensor(WD[:, u % 4, 1, :], WB2[:, 0:D], WD[:, u % 4, 0, :],
                                              ALU.subtract).then_inc(sem("f_wlow"), 1)

                        def gated(i, u):
                            dve.wait_ge(sem("f_gelu"), i + 1)
                            dve.wait_ge(sem("f_ilow"), i + 1)
                            dve.tensor_tensor(it[:, u % 2, :], UB[u % 2][:], gl[:, u % 2, :], ALU.mult)\
                               .then_inc(sem("f_uread"), 1)

                        dve.nop().then_inc(sem("f_wlow"), 2)
                        dve.nop().then_inc(sem("f_uread"), 2)
                        ln_vector(dve, 1)
                        w_low(0, 0)
                        ln_vector_low(dve, 1, bank[2:4])
                        w_low(1, 1)
                        decode(dve, AHEAD, AHEAD)
                        gated(0, 0)
                        w_low(2, 2)
                        decode(dve, AHEAD + 1, AHEAD + 1)
                        gated(1, 1)
                        with dve.Fori(0, 2) as g:
                            for u in range(1, 5):
                                w_low(4 * g + u + 2, u + 2)
                                decode(dve, 4 * g + u + 5, u + 5)
                                gated(4 * g + u + 1, u + 1)
                        for i in range(9, LAST):
                            if i + 2 < FT:
                                w_low(i + 2, i + 2)
                            if i + 5 < FT:
                                decode(dve, i + 5, i + 5)
                            gated(i + 1, i + 1)
                        dve.wait_ge(sem("f_dn"), FT)
                        for i in range(2):
                            xs = x[:, 2 * i:2 * i + 2, :].rearrange("p t d -> p (t d)")
                            dve.tensor_tensor(xs, ACC[i][:], xs, ALU.add).then_inc(sem("residual"), 1)

        pk.close()
        wide = [sb("wide", [P, H * NB * SK]), sb("wide_values", [P, 2 * KT * INNER])]
        KS = wide[0][:].bitcast(F16).rearrange("p (s h k) -> p s h k", s=2, h=H)
        VW = wide[1][:].bitcast(F16).rearrange("p (s w k n) -> p s w k n", s=2, w=2, k=KT)
        mG, mU = (wide[0][:, i * KT * MT * P:(i + 1) * KT * MT * P].rearrange("p (k n) -> p k n", k=KT)
                  for i in range(2))
        mD = wide[1][:, 0:MT * D].rearrange("p (t d) -> p t d", t=MT)
        EPG = 4
        GCOL = EPG * IM
        NGRP = E // EPG + 1
        group_of = [min((j * P + P - 1) // GCOL, NGRP - 1) for j in range(MT)]

        def load_group(sync, g):
            arrived = sem(f"in_moe{g}")
            for k in range(KT):
                for dst, w in ((mG, "gate"), (mU, "up")):
                    rows = slice(k * P, (k + 1) * P)
                    if g < E // EPG:
                        sync.dma_start(
                            dst[:, k, g * GCOL:(g + 1) * GCOL].rearrange("p (e i) -> p e i", i=IM),
                            a[f"L1_ffn_w_{w}"][g * EPG:(g + 1) * EPG, rows, :]
                            .rearrange("e p i -> p e i")).then_inc(arrived, 16)
                    else:
                        sync.dma_start(dst[:, k, E * IM:MROWS], a[f"L1_ffn_sh_{w}"][rows, :])\
                            .then_inc(arrived, 16)
            tiles = [j for j in range(MT) if group_of[j] == g]
            j0, j1 = tiles[0], tiles[-1] + 1
            if g < E // EPG:
                sync.dma_start(mD[:, j0:j1, :], a["L1_ffn_w_down"].rearrange(
                    "e i d -> (e i) d").rearrange("(t p) d -> p t d", p=P)[:, j0:j1, :])\
                    .then_inc(arrived, 16)
            else:
                sync.dma_start(mD[:, j0:j1 - 1, :], a["L1_ffn_sh_down"][0:(j1 - 1 - j0) * P, :]
                               .rearrange("(t p) d -> p t d", p=P)).then_inc(arrived, 16)
                sync.dma_start(mD[0:MLAST, j1 - 1, :],
                               a["L1_ffn_sh_down"][(j1 - 1 - j0) * P:ISH, :]).then_inc(arrived, 16)

        with ExitStack() as ph:
            s_ = tensors(ph, "l1")
            QS_ = s_("QS_", [P, 2, H, TOK], F16)
            vec = s_("vec", [P, 8, H])
            vb = s_("vb", [P, H])
            ones = s_("ones", [P, P])
            obr = s_("obr", [1, 2 * D])
            rr = s_("rr", [P, NB * KC + TT])
            rq = s_("rq", [P, TT])
            nrq = s_("nrq", [P, TT])
            rK = s_("rK", [P, NB, SK])
            V_QB, V_KB, V_KIB, V_NQ, V_NKT, V_NKI, V_VB, V_VIB = range(8)

            with ExitStack() as pr:
                t_ = tensors(pr, "l1proj")
                WS = t_("WS", [P, 2, 2, 2, KT, 2 * HD], F16)
                RAW = 4
                raw = t_("raw", [P, RAW, SK])
                sq = t_("sq", [P, RAW, SK])
                ssq = t_("ssq", [P, NB + 1, SK])
                dg = ln_x[:].rearrange("p t (k n) -> p (t k) n", k=KT)
                ms = t_("ms", [P, NB * KC + TT])
                KB = (bank[0:2], bank[2:4])

                with nc.Block() as block:
                    @block.sync
                    def _(sync):
                        for i in range(2):
                            sync.dma_start(obr[:, i * D:(i + 1) * D],
                                           a["L1_xattn_o_b"].rearrange("(o n) -> o n", o=1))\
                                .then_inc(sem("in_ob"), 16)
                        read = {slot: (done, count) for _, _, slot, done, count in pieces[:NST]}
                        for n in range(NST, len(pieces)):
                            _, _, slot, done, count = pieces[n]
                            sync.wait_ge(sem(read[slot][0]), read[slot][1])
                            read[slot] = (done, count)
                            load_piece(sync, n)

                    @block.gpsimd
                    def _(pool):
                        def low_keys(p):
                            for i in range(2):
                                hi, lo = (WS[:, p % 2, s, i] for s in range(2))
                                pool.wait_ge(sem("p_hi"), 2 * p + i + 1)
                                pool.tensor_tensor(lo, stage[:, (p % 2) * 3 + i], hi, ALU.subtract)\
                                    .then_inc(sem("p_split"), 1)

                        def low_queries(p):
                            hi, lo = (WS[:, 0, s, p % 2] for s in range(2))
                            pool.wait_ge(sem("p_hi"), 2 * HP + p + 1)
                            pool.tensor_tensor(lo, stage[:, (p % 2) * 2], hi, ALU.subtract)\
                                .then_inc(sem("p_split"), 1)

                        def inverse_rms(n, c0, c1):
                            pool.wait_ge(sem("p_ms"), n + 1)
                            pool.tensor_tensor(rr[:, c0:c1], ms[:, c0:c1], mhalf[:, c0:c1], ALU.pow)\
                                .then_inc(sem("p_rr"), 1)

                        def square_sum(u, part):
                            pool.wait_ge(sem("p_sq"), u + 1)
                            if part < NB and u >= NB:
                                pool.wait_ge(sem("p_ssq"), u - NB + 1 + RAW)
                            elif u > NB * H:
                                pool.wait_ge(sem("p_ssq"), u + RAW)
                            pool.tensor_tensor(ssq[:, part, :], ssq[:, part, :], sq[:, u % RAW, :], ALU.add)\
                                .then_inc(sem("p_ssq"), 1)

                        low_keys(0)
                        pool.memset(ones[:], 1.0).then_inc(sem("p_ones"), 1)
                        low_keys(1)
                        ln_pool(pool, 2)
                        pool.memset(ssq[:], 0.0).then_inc(sem("p_ones"), 1)
                        pool.wait_ge(sem("p_ones"), 2)
                        for p in range(HP):
                            if 2 <= p + 1 < HP:
                                low_keys(p + 1)
                            elif p + 1 == HP:
                                low_queries(0)
                                low_queries(1)
                            for u in range(4 * p, 4 * p + 4):
                                square_sum(u, u % NB)
                        for p in range(HP):
                            square_sum(NB * H + 2 * p, NB)
                            if p + 2 < HP:
                                low_queries(p + 2)
                            square_sum(NB * H + 2 * p + 1, NB)
                            if p == HP // 2:
                                inverse_rms(0, 0, NB * KC)
                        inverse_rms(1, NB * KC, NB * KC + TT)

                    @block.tensor
                    def _(pe):
                        pe.wait_ge(sem("in_vec"), 128)
                        pe.transpose(bank[4][:, 0:P], vrow, ident[:]).then_inc(sem("p_vec"), 1)

                        def keys(h, u):
                            for b in range(NB):
                                pe.wait_ge(sem("p_raw"), 2 * h + b + 1)
                                for seg, (c0, w) in enumerate(SEG):
                                    n = 0
                                    for k in range(KT):
                                        for l, r in PASSES:
                                            last = pe.matmul(
                                                KB[u % 2][b][:, c0:c0 + w],
                                                WS[:, (u // 2) % 2, l, 1 - seg, k, (u % 2) * HD:(u % 2 + 1) * HD],
                                                ctxT[:, r, k, b * SK + c0:b * SK + c0 + w],
                                                start=(n == 0), stop=(n == 5))
                                            n += 1
                                last.then_inc(sem("p_kmm"), 1)

                        def queries(h, u):
                            pe.wait_ge(sem("p_raw"), 2 * H + h + 1)
                            n = 0
                            for k in range(KT):
                                for l, r in PASSES:
                                    last = pe.matmul(KB[(u // 2) % 2][u % 2][:],
                                                     WS[:, 0, l, (u // 2) % 2, k, (u % 2) * HD:(u % 2 + 1) * HD],
                                                     xT[:, r, k, :], start=(n == 0), stop=(n == 5))
                                    n += 1
                            last.then_inc(sem("p_kmm"), 1)

                        pe.wait_ge(sem("p_split"), 2)
                        for u in range(2):
                            keys(u, u)
                        pe.wait_ge(sem("p_split"), 4)
                        for u in range(2, 4):
                            keys(u, u)
                        ln_tensor(pe, 2, bank[6:8])
                        with pe.Fori(1, H // 4) as g:
                            for u in range(4):
                                if u % 2 == 0:
                                    pe.wait_ge(sem("p_split"), 4 * g + u + 2)
                                keys(4 * g + u, u)

                        def four_queries(g):
                            for u in range(4):
                                if u % 2 == 0:
                                    pe.wait_ge(sem("p_split"), 2 * HP + 2 * g + u // 2 + 1)
                                queries(4 * g + u, u)

                        def sums(c0, c1):
                            for c in range(c0, c1):
                                last = pe.matmul(bank[4][:, c:c + 1],
                                                 ssq[:, c // KC, (c % KC) * P:(c % KC + 1) * P],
                                                 ones[:, 0:1], start=True, stop=True)
                            last.then_inc(sem("p_sum"), 1)

                        pe.wait_ge(sem("ln_lo"), 3 * KT)
                        with pe.Fori(0, H // 4 - 2) as g:
                            four_queries(g)
                        pe.wait_ge(sem("p_ssq"), NB * H + RAW)
                        sums(0, NB * KC)
                        four_queries(H // 4 - 2)
                        four_queries(H // 4 - 1)
                        for c in range(NB * KC):
                            pe.wait_ge(sem("p_dg"), c + 1)
                            pe.matmul(bank[6 + c // KC][:, (c % KC) * P:(c % KC + 1) * P], ones[:],
                                      dg[:, c, :], start=True, stop=True).then_inc(sem("p_rK"), 1)
                        pe.wait_ge(sem("p_ssq"), 3 * H + RAW)
                        pe.wait_ge(sem("p_ms"), 1)
                        sums(NB * KC, NB * KC + TT)

                    @block.scalar
                    def _(act):
                        def square(n, u):
                            act.wait_ge(sem("p_raw"), n + 5)
                            act.wait_ge(sem("p_ssq"), n + 1)
                            act.activation(sq[:, u % RAW, :], raw[:, u % RAW, :], ACT.Square)\
                               .then_inc(sem("p_sq"), 1)

                        def raw_rows(bankv, u, segs, n, first=False):
                            act.wait_ge(sem("p_kmm"), n + 1)
                            act.wait_ge(sem("p_low"), n + 1)
                            if not first:
                                square(n - 1, u - 1)
                            for c0, w, bias in segs:
                                last = act.activation(raw[:, u % RAW, c0:c0 + w], bankv[:, c0:c0 + w],
                                                      ACT.Identity, bias=bias)
                            last.then_inc(sem("p_raw"), 1)

                        def head_of(v, h):
                            return vec[:, v, bass.ds(h, 1)]

                        def values_of(p, image):
                            return VW[:, 0, image, :, bass.ds(p * 2 * HD, 2 * HD)]

                        def high_keys(p, par, turn, late):
                            slot = par * 3
                            if late:
                                act.wait_ge(sem("p_kmm"), 4 * (p - 1))
                            act.wait_ge(sem(f"in_stage{slot}"), 16 * turn)
                            act.activation(WS[:, par, 0, 0], stage[:, slot], ACT.Copy).then_inc(sem("p_hi"), 1)
                            act.wait_ge(sem(f"in_stage{slot + 1}"), 16 * turn)
                            act.wait_ge(sem(f"in_stage{slot + 2}"), 16 * turn)
                            act.activation(WS[:, par, 0, 1], stage[:, slot + 1], ACT.Copy)\
                               .then_inc(sem("p_hi"), 1)
                            act.activation(values_of(p, 0), stage[:, slot + 2], ACT.Copy)\
                               .then_inc(sem("p_vhi"), 1)

                        def high_queries(p, par, turn):
                            slot = par * 2
                            first = isinstance(p, int) and p < 2
                            act.wait_ge(sem("p_kmm"), 4 * (HP - 1) if first else 2 * H + 2 * (p - 1))
                            act.wait_ge(sem(f"in_stage{slot}"), 16 * turn)
                            act.activation(WS[:, 0, 0, par], stage[:, slot], ACT.Copy).then_inc(sem("p_hi"), 1)

                        def image_values_here(par, turn):
                            act.wait_ge(sem(f"in_stage{par * 2 + 1}"), 16 * turn)

                        def high_image_values(p, par):
                            act.activation(values_of(p, 1), stage[:, par * 2 + 1], ACT.Copy)\
                               .then_inc(sem("p_vhi"), 1)

                        act.nop().then_inc(sem("p_raw"), 4)
                        high_keys(0, 0, 1, False)
                        high_keys(1, 1, 1, False)
                        act.wait_ge(sem("p_vec"), 1)
                        act.activation(vec[:].rearrange("p v h -> p (v h)"), bank[4][:, 0:P], ACT.Copy)\
                           .then_inc(sem("p_vec"), 1)
                        act.wait_ge(sem("p_vec"), 2)

                        def keys(h, u, fresh=False):
                            for b in range(NB):
                                raw_rows(KB[u % 2][b], 2 * u + b,
                                         ((0, NIMG, head_of(V_KIB, h)), (NIMG, NTXT, head_of(V_KB, h))),
                                         2 * h + b, first=(u == 0 and b == 0 and fresh))
                        for u in range(2):
                            keys(u, u, fresh=True)
                        for u in range(2, 4):
                            if u == 2:
                                high_keys(2, 0, 2, True)
                            keys(u, u, fresh=True)
                        ln_scalar(act, 2, bank[6:8])

                        def four_heads(g, last=False):
                            for u in range(4):
                                if u == 0:
                                    high_keys(2 * g + 1, 1, g + 1, True)
                                elif u == 2 and not last:
                                    high_keys(2 * g + 2, 0, g + 2, True)
                                elif u == 2:
                                    high_queries(0, 0, HP // 2 + 1)
                                elif u == 3 and last:
                                    high_queries(1, 1, HP // 2 + 1)
                                    image_values_here(0, HP // 2 + 1)
                                keys(4 * g + u, u)
                            if last:
                                high_image_values(0, 0)
                        with act.Fori(1, H // 4 - 1) as g:
                            four_heads(g)
                        four_heads(H // 4 - 1, last=True)

                        def four_queries(g, last=False):
                            for u in range(4):
                                h = 4 * g + u
                                if u == 1 and not last:
                                    high_queries(2 * g + 2, 0, HP // 2 + g + 2)
                                elif u == 3 and not last:
                                    high_queries(2 * g + 3, 1, HP // 2 + g + 2)
                                if u == 1:
                                    image_values_here(1, HP // 2 + g + 1)
                                elif u == 3 and not last:
                                    image_values_here(0, HP // 2 + g + 2)
                                raw_rows(KB[(u // 2) % 2][u % 2], u, ((0, TOK, head_of(V_QB, h)),), 2 * H + h)
                                if u == 1:
                                    high_image_values(2 * g + 1, 1)
                                elif u == 3 and not last:
                                    high_image_values(2 * g + 2, 0)
                        with act.Fori(0, H // 4 - 1) as g:
                            four_queries(g)
                        four_queries(H // 4 - 1, last=True)
                        square(3 * H - 1, RAW - 1)
                        act.wait_ge(sem("p_rK"), NB * KC)
                        for b in range(NB):
                            act.activation(rK[:, b, :], bank[6 + b][:], ACT.Copy).then_inc(sem("p_end"), 1)

                    @block.vector
                    def _(dve):
                        def halves(dst, h, u, ahead, segs):
                            dve.wait_ge(sem("p_raw"), ahead + 5)
                            for c0, w, v in segs:
                                dve.tensor_scalar(dst(0, c0, w), raw[:, u % RAW, c0:c0 + w],
                                                  vec[:, v, bass.ds(h, 1)], None, ALU.mult)\
                                   .then_inc(sem(f"p_high{len(segs)}"), 1)
                            for i, (c0, w, v) in enumerate(segs):
                                dve.wait_ge(sem(f"p_high{len(segs)}"),
                                            (2 * ahead if len(segs) == 2 else h) + i + 1)
                                last = dve.scalar_tensor_tensor(
                                    out=dst(1, c0, w), in0=raw[:, u % RAW, c0:c0 + w],
                                    scalar=vec[:, v, bass.ds(h, 1)], in1=dst(0, c0, w),
                                    op0=ALU.mult, op1=ALU.subtract)
                            last.then_inc(sem("p_low"), 1)

                        def low_values(p, slot, image):
                            hi, lo = (VW[:, s, image, :, bass.ds(p * 2 * HD, 2 * HD)] for s in range(2))
                            dve.wait_ge(sem("p_vhi"), HP * image + p + 1)
                            dve.tensor_tensor(lo, stage[:, slot], hi, ALU.subtract)\
                               .then_inc(sem("p_vsplit"), 1)

                        def one(ap):
                            return ap.rearrange("p o n -> p (o n)")

                        def keys(h, u):
                            for b in range(NB):
                                halves(lambda s, c0, w, b=b: one(KS[:, s, bass.ds(h, 1),
                                                                   b * SK + c0:b * SK + c0 + w]),
                                       h, 2 * u + b, 2 * h + b, ((0, NIMG, V_NKI), (NIMG, NTXT, V_NKT)))

                        dve.nop().then_inc(sem("p_low"), RAW)
                        dve.nop().then_inc(sem("p_ssq"), RAW)
                        ln_vector(dve, 2)
                        dve.wait_ge(sem("p_vec"), 2)
                        dve.tensor_tensor(vb[:], vec[:, V_VB, :], vec[:, V_VIB, :], ALU.add)\
                           .then_inc(sem("p_end"), 1)
                        low_values(0, 2, 0)
                        for h in range(4):
                            keys(h, h)
                            if h == 1:
                                low_values(1, 5, 0)
                            elif h == 3:
                                low_values(2, 2, 0)
                        ln_vector_low(dve, 2, bank[6:8])

                        def four_heads(g, last=False):
                            for u in range(4):
                                keys(4 * g + u, u)
                                if u == 1:
                                    low_values(2 * g + 1, 5, 0)
                                elif u == 3 and not last:
                                    low_values(2 * g + 2, 2, 0)
                                elif u == 3:
                                    low_values(0, 1, 1)

                        def four_queries(g, last=False):
                            for u in range(4):
                                h = 4 * g + u
                                halves(lambda s, c0, w: one(QS_[:, s, bass.ds(h, 1), c0:c0 + w]),
                                       h, u, 2 * H + h, ((0, TOK, V_NQ),))
                                if u == 1:
                                    low_values(2 * g + 1, 3, 1)
                                elif u == 3 and not last:
                                    low_values(2 * g + 2, 1, 1)
                        with dve.Fori(1, H // 4 - 1) as g:
                            four_heads(g)
                        four_heads(H // 4 - 1, last=True)
                        def mean_squares(n, c0, c1):
                            dve.wait_ge(sem("p_sum"), n + 1)
                            dve.tensor_scalar(ms[:, c0:c1], bank[4][:, c0:c1], 1.0 / INNER, 1e-6, ALU.mult,
                                              ALU.add).then_inc(sem("p_ms"), 1)
                        with dve.Fori(0, H // 4 - 2) as g:
                            four_queries(g)
                        mean_squares(0, 0, NB * KC)
                        four_queries(H // 4 - 2)
                        dve.wait_ge(sem("p_rr"), 1)
                        for c in range(NB * KC):
                            dve.tensor_scalar(dg[:, c, :], ident[:], rr[:, c:c + 1], None, ALU.mult)\
                               .then_inc(sem("p_dg"), 1)
                        four_queries(H // 4 - 1, last=True)
                        mean_squares(1, NB * KC, NB * KC + TT)
                        dve.wait_ge(sem("p_rr"), 2)
                        qr = rr[:, NB * KC:NB * KC + TT]
                        dve.tensor_scalar(rq[:], qr, SCALE1, None, ALU.mult).then_inc(sem("p_end"), 1)
                        dve.tensor_scalar(nrq[:], qr, -SCALE1, None, ALU.mult).then_inc(sem("p_end"), 1)

            with ExitStack() as at:
                t_ = tensors(at, "l1head")
                ostage = t_("ostage", [P, 2, D])
                V = t_("V", [P, 2, 2, NB * KC, HD], F16)
                X = t_("X", [P, TT, SK])
                PT = t_("PT", [P, 2, 2, SK], F16)
                mx = t_("mx", [P, TT, 2])
                nm = t_("nm", [P, TT, 2])
                den = t_("den", [P, TT, 2])
                rden = t_("rden", [P, TT, 2])
                OT = t_("OT", [P, 2, 2, TOK], F16)
                SB, TB, OB, VB, ACC = bank[0], bank[1], bank[2:4], bank[4:6], bank[6:8]

                with nc.Block() as block:
                    @block.sync
                    def _(sync):
                        for g in range(H // 2):
                            if g:
                                sync.wait_ge(sem("o_split"), g)
                            sync.dma_start(ostage[:], a["L1_xattn_o_w"].rearrange(
                                "(h p) n -> p h n", p=P)[:, 2 * g:2 * g + 2, :]).then_inc(sem("in_ow0"), 16)
                        sync.wait_ge(sem("b_sfull"), 4 * H)
                        sync.wait_ge(sem("b_vfull"), NB * H)
                        load_group(sync, 0)

                    @block.gpsimd
                    def _(pool):
                        def normalise(h, t):
                            pool.wait_ge(sem("b_rden"), 4 * h + t + 1)
                            t = t % TT
                            for s, (c0, w) in enumerate(SEG):
                                last = pool.tensor_tensor(X[:, t, c0:c0 + w], X[:, t, c0:c0 + w],
                                                          rden[:, t, s:s + 1].to_broadcast([P, w]), ALU.mult)
                            last.then_inc(sem("b_norm"), 1)

                        def ow_low(g):
                            hi, lo = (OW[:, s, bass.ds(2 * g, 2), :] for s in range(2))
                            pool.wait_ge(sem("o_hi"), g + 1)
                            pool.tensor_tensor(lo, ostage[:], hi, ALU.subtract).then_inc(sem("o_split"), 1)

                        def step(h, par, last=False):
                            for t in range(TT):
                                if not (last and t):
                                    normalise(h, t + 3)

                        def two_heads(g, last=False):
                            step(2 * g, 0)
                            ow_low(g)
                            step(2 * g + 1, 1, last=last)
                        for t in range(3):
                            normalise(0, t)
                        two_heads(0)
                        with pool.Fori(1, H // 2 - 1) as g:
                            two_heads(g)
                        two_heads(H // 2 - 1, last=True)

                    @block.tensor
                    def _(pe):
                        def values(h, par, b, half):
                            if half == 0:
                                pe.wait_ge(sem("b_vlow"), 2 * h + b + 1)
                            for c in (2 * half, 2 * half + 1):
                                if c == NIMG // P:
                                    terms = [(ctxM[:, l, k, b, v, :], l, r, k, 1 - v)
                                             for v in range(2) for k in range(KT) for l, r in PASSES]
                                else:
                                    terms = [(ctxT[:, l, k, b * SK + c * P:b * SK + (c + 1) * P], l, r, k,
                                              int(c < NIMG // P)) for k in range(KT) for l, r in PASSES]
                                for n, (rows, l, r, k, w) in enumerate(terms):
                                    last = pe.matmul(VB[b][:, c * HD:(c + 1) * HD], rows,
                                                     VW[:, r, w, k, bass.ds(h * HD, HD)],
                                                     start=(n == 0), stop=(n == len(terms) - 1))
                            if half:
                                last.then_inc(sem("b_vfull"), 1)

                        def scores(h, t):
                            n = 4 * h + t
                            pe.wait_ge(sem("b_max"), 2 * n + 2)
                            b = t // 2
                            for i, (l, r) in enumerate(PASSES):
                                last = pe.matmul(SB[:], QS_[:, l, bass.ds(h, 1), t * P:(t + 1) * P],
                                                 KS[:, r, bass.ds(h, 1), b * SK:(b + 1) * SK],
                                                 start=(i == 0), stop=(i == 2))
                            last.then_inc(sem("b_sfull"), 1)

                        def turn(h, t):
                            n = 4 * h + t
                            pe.wait_ge(sem("b_norm"), n + 1)
                            pe.wait_ge(sem("b_ptlow"), n + 1)
                            for c in range(KC):
                                last = pe.transpose(TB[:, c * P:(c + 1) * P],
                                                    X[:, t, c * P:(c + 1) * P], ident[:])
                            last.then_inc(sem("b_tfull"), 1)

                        def attend(h, t, par):
                            n = 4 * h + t
                            b = t // 2
                            pe.wait_ge(sem("b_ptlow"), n + 2)
                            if t == 0:
                                pe.wait_ge(sem("b_vlow"), 2 * h + 4)
                                pe.wait_ge(sem("b_olow"), h + 1)
                            i = 0
                            for c in range(KC):
                                for l, r in PASSES:
                                    last = pe.matmul(OB[par][:, t * P:(t + 1) * P], V[:, par, l, b * KC + c, :],
                                                     PT[:, t % 2, r, c * P:(c + 1) * P], start=(i == 0),
                                                     stop=(i == 3 * KC - 1))
                                    i += 1
                            last.then_inc(sem("b_ofull"), 1)

                        def output(h, par, pair=None):
                            pe.wait_ge(sem("b_olow"), h + 3)
                            pe.wait_ge(sem("o_split"), h // 2 + 1 if isinstance(h, int) else pair + 1)
                            for t in range(TT):
                                for l, r in PASSES:
                                    last = pe.matmul(ACC[t // 2][:, (t % 2) * D:(t % 2 + 1) * D],
                                                     OT[:, par, l, t * P:(t + 1) * P],
                                                     OW[:, r, bass.ds(h, 1), :], start=False, stop=False,
                                                     skip_group_check=True)
                            last.then_inc(sem("b_omm"), 1)

                        def step(h, par, first=False, last=False, pair=None):
                            for t in range(TT):
                                turn(h, t)
                                if not last:
                                    scores(h + 1, t)
                                    values(h + 1, 1 - par, t // 2, t % 2)
                                if t:
                                    attend(h, t - 1, par)
                                elif not first:
                                    attend(h - 1, TT - 1, 1 - par)
                                if t == 2 and not first:
                                    output(h - 1, 1 - par, pair)

                        pe.wait_ge(sem("in_ob"), 32)
                        for t in range(TT):
                            scores(0, t)
                            values(0, 0, t // 2, t % 2)
                            if t < 2:
                                pe.matmul(ACC[t][:], ones[0:1, :], obr[:], start=True, stop=False,
                                          skip_group_check=True)
                        step(0, 0, first=True)
                        step(1, 1)
                        with pe.Fori(1, H // 2 - 1) as g:
                            step(2 * g, 0, pair=g - 1)
                            step(2 * g + 1, 1, pair=g)
                        step(H - 2, 0)
                        step(H - 1, 1, last=True)
                        attend(H - 1, TT - 1, 1)
                        output(H - 1, 1)

                    @block.scalar
                    def _(act):
                        def v_high(h, par, b):
                            act.wait_ge(sem("b_vfull"), 2 * h + b + 1)
                            act.wait_ge(sem("b_ofull"), 4 * h + 1)
                            act.activation(V[:, par, 0, b * KC:(b + 1) * KC, :].rearrange("p c n -> p (c n)"),
                                           VB[b][:], ACT.Copy).then_inc(sem("b_vhigh"), 1)

                        def exp(h, t):
                            n = 4 * h + t
                            act.wait_ge(sem("b_nm"), n + 1)
                            for s, (c0, w) in enumerate(SEG):
                                act.activation(X[:, t, c0:c0 + w], X[:, t, c0:c0 + w], ACT.Exp,
                                               bias=nm[:, t, s:s + 1], scale=rq[:, t:t + 1],
                                               accum_out=den[:, t, s:s + 1]).then_inc(sem("b_exp"), 1)

                        def pt_high(h, t):
                            n = 4 * h + t
                            act.wait_ge(sem("b_tfull"), n + 1)
                            act.wait_ge(sem("b_ofull"), n + 7)
                            act.activation(PT[:, t % 2, 0, :], TB[:], ACT.Copy)\
                               .then_inc(sem("b_pthigh"), 1)

                        def o_ready(h):
                            act.wait_ge(sem("b_ofull"), 4 * h + 12)
                            act.wait_ge(sem("b_omm"), h + 1)

                        def o_high(h, par):
                            act.activation(OT[:, par, 0, :], OB[par][:], ACT.Identity,
                                           bias=vb[:, bass.ds(h, 1)]).then_inc(sem("b_ohigh"), 1)

                        def step(h, par, first=False, last=False, pair=None):
                            for t in range(TT):
                                out = t == 1 and not first
                                if out:
                                    o_ready(h - 1)
                                if t == 2 and pair is not None:
                                    act.wait_ge(sem("in_ow0"), 16 * pair + 16)
                                pt_high(h, t)
                                if t == 2 and pair is not None:
                                    act.activation(OW[:, 0, bass.ds(2 * pair, 2), :], ostage[:], ACT.Copy)\
                                       .then_inc(sem("o_hi"), 1)
                                if out:
                                    o_high(h - 1, 1 - par)
                                if t == 0:
                                    exp(h, 3)
                                elif not last:
                                    exp(h + 1, t - 1)
                                if t % 2 and not last:
                                    v_high(h + 1, 1 - par, t // 2)

                        act.nop().then_inc(sem("b_ofull"), 8)
                        act.nop().then_inc(sem("b_omm"), 2)
                        for t in range(3):
                            exp(0, t)
                        for b in range(NB):
                            v_high(0, 0, b)
                        step(0, 0, first=True, pair=0)
                        step(1, 1)
                        with act.Fori(1, H // 2 - 1) as g:
                            step(2 * g, 0, pair=g)
                            step(2 * g + 1, 1)
                        step(H - 2, 0, pair=H // 2 - 1)
                        step(H - 1, 1, last=True)
                        o_ready(H - 1)
                        o_high(H - 1, 1)

                    @block.vector
                    def _(dve):
                        def top_score(h, t):
                            n = 4 * h + t
                            for s, (c0, w) in enumerate(SEG):
                                dve.tensor_tensor_reduce(X[:, t, c0:c0 + w], SB[:, c0:c0 + w],
                                                         rK[:, t // 2, c0:c0 + w], 1.0, LOWEST, ALU.mult,
                                                         ALU.max, mx[:, t, s:s + 1])\
                                   .then_inc(sem("b_max"), 1)
                            dve.wait_ge(sem("b_max"), 2 * n + 4)
                            dve.tensor_scalar(nm[:, t, :], mx[:, t, :], nrq[:, t:t + 1], None, ALU.mult)\
                               .then_inc(sem("b_nm"), 1)

                        def inverse(t):
                            dve.reciprocal(rden[:, t, :], den[:, t, :]).then_inc(sem("b_rden"), 1)

                        def pt_low(h, t):
                            n = 4 * h + t
                            dve.wait_ge(sem("b_pthigh"), n + 1)
                            dve.tensor_tensor(PT[:, t % 2, 1, :], TB[:], PT[:, t % 2, 0, :],
                                              ALU.subtract).then_inc(sem("b_ptlow"), 1)

                        def v_low(h, par, b):
                            dve.wait_ge(sem("b_vhigh"), 2 * h + b + 1)
                            hi, lo = (V[:, par, s, b * KC:(b + 1) * KC, :].rearrange("p c n -> p (c n)")
                                      for s in range(2))
                            dve.tensor_tensor(lo, VB[b][:], hi, ALU.subtract).then_inc(sem("b_vlow"), 1)

                        def o_low(h, par):
                            dve.wait_ge(sem("b_ohigh"), h + 1)
                            dve.scalar_tensor_tensor(out=OT[:, par, 1, :], in0=OB[par][:],
                                                     scalar=vb[:, bass.ds(h, 1)], in1=OT[:, par, 0, :],
                                                     op0=ALU.add, op1=ALU.subtract)\
                               .then_inc(sem("b_olow"), 1)

                        def step(h, par, first=False, last=False):
                            for t in range(TT):
                                if not last:
                                    dve.wait_ge(sem("b_sfull"), 4 * (h + 1) + t + 1)
                                pt_low(h, t)
                                if not last:
                                    top_score(h + 1, t)
                                if not (last and t):
                                    dve.wait_ge(sem("b_exp"), 2 * (4 * h + t + 3) + 2)
                                    inverse((t + 3) % 4)
                                if t == 1 and not first:
                                    o_low(h - 1, 1 - par)
                                if t % 2 and not last:
                                    v_low(h + 1, 1 - par, t // 2)

                        dve.nop().then_inc(sem("b_max"), 2)
                        for credit, n in (("b_ptlow", 1), ("b_vlow", 2), ("b_olow", 2)):
                            dve.nop().then_inc(sem(credit), n)
                        for t in range(TT):
                            dve.wait_ge(sem("b_sfull"), t + 1)
                            top_score(0, t)
                        for t in range(3):
                            dve.wait_ge(sem("b_exp"), 2 * t + 2)
                            inverse(t)
                        for b in range(NB):
                            v_low(0, 0, b)
                        step(0, 0, first=True)
                        step(1, 1)
                        with dve.Fori(1, H // 2 - 1) as g:
                            step(2 * g, 0)
                            step(2 * g + 1, 1)
                        step(H - 2, 0)
                        step(H - 1, 1, last=True)
                        o_low(H - 1, 1)
                        dve.wait_ge(sem("b_omm"), H + 2)
                        for i in range(2):
                            xs = x[:, 2 * i:2 * i + 2, :].rearrange("p t d -> p (t d)")
                            dve.tensor_tensor(xs, ACC[i][:], xs, ALU.add).then_inc(sem("residual"), 1)

        with ExitStack() as ph:
            s_ = tensors(ph, "moe")
            WG = s_("WG", [P, 4, 2, 2, KT, P], F16)
            WD = s_("WD", [P, 4, 2, D], F16)
            si = s_("si", [P, 2, TOK])
            su_ = s_("su", [P, 2, TOK])
            it = s_("it", [P, 2, TOK])
            IN = s_("IN", [P, 4, 2, TOK], F16)
            zero = s_("zero", [P, P], F16)
            rrow = s_("rrow", [E, D])
            rT = s_("rT", [P, KT, EG])
            rTS = s_("rTS", [P, 2, KT, EG], F16)
            before = s_("before", [P, E * E])
            owner = s_("owner", [EG, MT * P], F16)
            lg = s_("lg", [P, TT, EG])
            ex = s_("ex", [P, TT, EG])
            pr_ = s_("pr", [P, TT, E])
            g1 = s_("g1", [P, TT, E * E])
            g2 = s_("g2", [P, TT, E * E])
            rank = s_("rank", [P, TT, E])
            comb = s_("comb", [P, TT, EG])
            v1 = s_("v1", [P, TT])
            v2 = s_("v2", [P, TT])
            combT = s_("combT", [EG, 2, TOK], F16)
            GB, UB, CB, ACC = (bank[0], bank[2]), (bank[1], bank[3]), bank[4:6], bank[6:8]
            RT, LB, CT, LNB = bank[4], bank[5], bank[4], bank[0:2]
            with nc.Block() as block:
                @block.sync
                def _(sync):
                    def arrived(g):
                        sync.wait_ge(sem(f"in_moe{g}"), 16 * (5 if g < E // EPG else 6))
                        sync.nop().then_inc(sem("m_arrived"), group_of.count(g))

                    arrived(0)
                    sync.dma_start(rrow[:], a["L1_ffn_router_w"]).then_inc(sem("in_router"), 16)
                    for k in range(KT):
                        sync.dma_start(rT[:, k, E:EG], a["L1_ffn_sh_gate_w"][k * P:(k + 1) * P, :],
                                       allow_slow_non_contiguous=True).then_inc(sem("in_router"), 16)
                    sync.dma_start(before[:], a["before"]).then_inc(sem("in_before"), 16)
                    sync.dma_start(owner[:], a["owner"]).then_inc(sem("in_owner"), 16)
                    for g in range(1, NGRP):
                        load_group(sync, g)
                    for g in range(1, NGRP):
                        arrived(g)
                    sync.wait_ge(sem("residual"), 8)
                    sync.dma_start(a["out"].rearrange("b (t p) d -> p (b t) d", p=P), x[:])\
                        .then_inc(sem("out"), 16)
                    sync.wait_ge(sem("out"), 16)

                @block.gpsimd
                def _(pool):
                    pool.memset(zero[:], 0.0).then_inc(sem("m_zero"), 1)
                    for w in (mG, mU):
                        pool.memset(w[:, :, MROWS:MT * P], 0.0).then_inc(sem("m_zero"), 1)
                    pool.wait_ge(sem("m_zero"), 3)
                    pool.memset(mD[MLAST:P, MT - 1, :], 0.0).then_inc(sem("m_zero"), 1)
                    pool.nop().then_inc(sem("m_ilow"), 2)
                    pool.wait_ge(sem("m_zero"), 4)

                    def split(j):
                        cols = slice(j * P, (j + 1) * P)
                        srcs = [(WG[:, j % 4, :, m], w[:, :, cols]) for m, w in enumerate((mG, mU))]
                        for m, (dst, src) in enumerate(srcs):
                            pool.wait_ge(sem("m_whi"), 3 * j + m + 1)
                            pool.tensor_tensor(dst[:, 1], src, dst[:, 0], ALU.subtract)\
                                .then_inc(sem("m_wlo"), 1)
                        pool.wait_ge(sem("m_whi"), 3 * j + 3)
                        pool.tensor_tensor(WD[:, j % 4, 1, :], mD[:, j, :], WD[:, j % 4, 0, :],
                                           ALU.subtract).then_inc(sem("m_wlo"), 1)

                    def in_low(j):
                        pool.wait_ge(sem("m_ihigh"), j + 1)
                        pool.tensor_tensor(IN[:, j % 4, 1, :], it[:, j % 2, :], IN[:, j % 4, 0, :],
                                           ALU.subtract).then_inc(sem("m_ilow"), 1)

                    ln_pool(pool, 3)
                    pool.wait_ge(sem("m_rT"), 1)
                    pool.wait_ge(sem("in_router"), 48)
                    pool.tensor_copy(rTS[:, 0], rT[:]).then_inc(sem("m_router"), 1)
                    pool.wait_ge(sem("m_router"), 1)
                    pool.tensor_tensor(rTS[:, 1], rT[:], rTS[:, 0], ALU.subtract).then_inc(sem("m_router"), 1)
                    split(0)
                    split(1)
                    split(2)
                    for j in range(MT):
                        in_low(j)
                        if j + 3 < MT:
                            split(j + 3)

                @block.tensor
                def _(pe):
                    pe.wait_ge(sem("m_zero"), 1)
                    for acc in ACC:
                        pe.matmul(acc[:], zero[:], xT[:, 0, 0, :], start=True, stop=False,
                                  skip_group_check=True)
                    pe.wait_ge(sem("in_router"), 48)
                    for k in range(KT):
                        last = pe.transpose(RT[:, k * E:(k + 1) * E], rrow[:, k * P:(k + 1) * P],
                                            ident[0:E, 0:E])
                    last.then_inc(sem("m_rt"), 1)
                    ln_tensor(pe, 3, LNB)
                    pe.wait_ge(sem("m_router"), 2)
                    pe.wait_ge(sem("ln_lo"), 4 * KT)
                    for t in range(TT):
                        n = 0
                        for k in range(KT):
                            for l, r in PASSES:
                                last = pe.matmul(LB[:, t * EG:(t + 1) * EG], xT[:, l, k, t * P:(t + 1) * P],
                                                 rTS[:, r, k, :], start=(n == 0), stop=(n == 5))
                                n += 1
                    last.then_inc(sem("m_logits"), 1)

                    def gate_up(j, u):
                        pe.wait_ge(sem("m_wlo"), 3 * j + 3)
                        pe.wait_ge(sem("m_uread"), j + 1)
                        for m, out in enumerate((GB[u % 2], UB[u % 2])):
                            n = 0
                            for k in range(KT):
                                for l, r in PASSES:
                                    last = pe.matmul(out[:], WG[:, u % 4, l, m, k, :], xT[:, r, k, :],
                                                     start=(n == 0), stop=(n == 5))
                                    n += 1
                        last.then_inc(sem("m_gu"), 1)

                    def spread(j, u):
                        pe.wait_ge(sem("m_cread"), j + 1)
                        for r in range(2):
                            last = pe.matmul(CB[u % 2][:], owner[:, bass.ds(j * P, P)], combT[:, r, :],
                                             start=(r == 0), stop=(r == 1))
                        last.then_inc(sem("m_c"), 1)

                    def down(j, u):
                        pe.wait_ge(sem("m_ilow"), j + 3)
                        for t in range(TT):
                            for l, r in PASSES:
                                last = pe.matmul(ACC[t // 2][:, (t % 2) * D:(t % 2 + 1) * D],
                                                 IN[:, u % 4, l, t * P:(t + 1) * P], WD[:, u % 4, r, :],
                                                 start=False, stop=False, skip_group_check=True)
                        last.then_inc(sem("m_dn"), 1)

                    gate_up(0, 0)
                    gate_up(1, 1)
                    pe.wait_ge(sem("in_owner"), 16)
                    pe.wait_ge(sem("m_comb"), 1)
                    for t in range(TT):
                        last = pe.transpose(CT[0:EG, t * P:(t + 1) * P], comb[:, t, :], ident[:])
                    last.then_inc(sem("m_combT"), 1)
                    pe.wait_ge(sem("m_comblo"), 1)
                    spread(0, 0)
                    spread(1, 1)
                    with pe.Fori(0, 6) as g:
                        for u in range(1, 5):
                            gate_up(4 * g + u + 1, u + 1)
                            spread(4 * g + u + 1, u + 1)
                            down(4 * g + u - 1, u - 1)
                    for i in range(25, MT + 1):
                        if i + 1 < MT:
                            gate_up(i + 1, i + 1)
                            spread(i + 1, i + 1)
                        down(i - 1, i - 1)

                @block.scalar
                def _(act):
                    def w_high(j, u):
                        for m, w in enumerate((mG, mU)):
                            act.activation(WG[:, u % 4, 0, m], w[:, :, bass.ds(j * P, P)], ACT.Copy)\
                               .then_inc(sem("m_whi"), 1)
                        src = mD[:, j, :] if isinstance(j, int) else \
                            mD[:, bass.ds(j, 1), :].rearrange("p o d -> p (o d)")
                        act.activation(WD[:, u % 4, 0, :], src, ACT.Copy).then_inc(sem("m_whi"), 1)

                    act.wait_ge(sem("m_arrived"), 4)
                    for j in range(3):
                        w_high(j, j)
                    ln_scalar(act, 3, LNB)
                    act.wait_ge(sem("m_z"), 2)
                    act.activation(ex[:], lg[:], ACT.Exp).then_inc(sem("m_exp"), 1)
                    def silu(j, u):
                        act.wait_ge(sem("m_gu"), j + 1)
                        act.activation(si[:, u % 2, :], GB[u % 2][:], ACT.Silu).then_inc(sem("m_silu"), 1)

                    def in_high(j, u, ahead=False):
                        act.wait_ge(sem("m_cread"), j + 3)
                        if ahead:
                            act.wait_ge(sem("m_dn"), j - 1)
                            act.wait_ge(sem("m_arrived"), j + 3)
                        act.activation(IN[:, u % 4, 0, :], it[:, u % 2, :], ACT.Copy)\
                           .then_inc(sem("m_ihigh"), 1)

                    silu(0, 0)
                    silu(1, 1)
                    act.wait_ge(sem("m_combT"), 1)
                    act.activation(combT[:, 0, :], CT[0:EG, :], ACT.Copy).then_inc(sem("m_combhi"), 1)
                    in_high(0, 0)
                    w_high(3, 3)
                    in_high(1, 1)
                    with act.Fori(0, 6) as g:
                        for u in range(1, 5):
                            silu(4 * g + u + 1, u + 1)
                            in_high(4 * g + u + 1, u + 1, ahead=True)
                            w_high(4 * g + u + 3, u + 3)
                    for i in range(25, MT - 1):
                        silu(i + 1, i + 1)
                        in_high(i + 1, i + 1)

                @block.vector
                def _(dve):
                    dve.nop().then_inc(sem("m_uread"), 2)
                    dve.nop().then_inc(sem("m_cread"), 2)
                    ln_vector(dve, 3)
                    dve.wait_ge(sem("m_rt"), 1)
                    dve.tensor_copy(rT[:, :, 0:E], RT[:, 0:KT * E].rearrange("p (k e) -> p k e", e=E))\
                       .then_inc(sem("m_rT"), 1)
                    ln_vector_low(dve, 3, LNB)

                    links = [0]

                    def link(ins):
                        links[0] += 1
                        ins.then_inc(sem("m_link"), 1)
                        dve.wait_ge(sem("m_link"), links[0])

                    def of_row(ap, n):
                        return ap.rearrange("p (t o) -> p t o", o=1).to_broadcast([P, TT, n])

                    dve.wait_ge(sem("m_logits"), 1)
                    logits = LB[:, 0:TT * EG].rearrange("p (t e) -> p t e", e=EG)
                    link(dve.tensor_reduce(v1[:], logits[:, :, 0:E], AX, ALU.max))
                    dve.tensor_tensor(lg[:, :, 0:E], logits[:, :, 0:E], of_row(v1[:], E), ALU.subtract)\
                       .then_inc(sem("m_z"), 1)
                    dve.tensor_scalar(lg[:, :, E:EG], logits[:, :, E:EG], -1.0, None, ALU.mult)\
                       .then_inc(sem("m_z"), 1)
                    dve.wait_ge(sem("m_exp"), 1)
                    link(dve.tensor_reduce(v2[:], ex[:, :, 0:E], AX, ALU.add))
                    link(dve.reciprocal(v1[:], v2[:]))
                    link(dve.tensor_tensor(pr_[:], ex[:, :, 0:E], of_row(v1[:], E), ALU.mult))
                    shape = [P, TT, E, E]
                    others = pr_[:].rearrange("p t (o j) -> p t o j", o=1).to_broadcast(shape)
                    own = pr_[:].rearrange("p t (e o) -> p t e o", o=1).to_broadcast(shape)
                    likelier, equal = (x_[:].rearrange("p t (e j) -> p t e j", j=E) for x_ in (g1, g2))
                    dve.wait_ge(sem("in_before"), 16)
                    dve.tensor_tensor(likelier, others, own, ALU.is_gt)
                    link(dve.tensor_tensor(equal, others, own, ALU.is_equal))
                    lower = before[:].rearrange("p (t n) -> p t n", t=1).to_broadcast([P, TT, E * E])
                    link(dve.tensor_tensor(g2[:], g2[:], lower, ALU.mult))
                    link(dve.tensor_tensor(g1[:], g1[:], g2[:], ALU.add))
                    link(dve.tensor_reduce(rank[:], g1[:].rearrange("p t (e j) -> p (t e) j", j=E), AX,
                                           ALU.add))
                    link(dve.scalar_tensor_tensor(out=pr_[:], in0=rank[:], scalar=float(TOPK), in1=pr_[:],
                                                  op0=ALU.is_lt, op1=ALU.mult))
                    link(dve.tensor_reduce(v2[:], pr_[:], AX, ALU.add))
                    link(dve.tensor_scalar(v2[:], v2[:], 1e-9, None, ALU.max))
                    link(dve.reciprocal(v1[:], v2[:]))
                    link(dve.tensor_scalar(ex[:, :, E:EG], ex[:, :, E:EG], 1.0, None, ALU.add))
                    link(dve.reciprocal(comb[:, :, E:EG], ex[:, :, E:EG]))
                    dve.tensor_tensor(comb[:, :, 0:E], pr_[:], of_row(v1[:], E), ALU.mult)\
                       .then_inc(sem("m_comb"), 1)
                    dve.wait_ge(sem("m_combhi"), 1)
                    dve.tensor_tensor(combT[:, 1, :], CT[0:EG, :], combT[:, 0, :], ALU.subtract)\
                       .then_inc(sem("m_comblo"), 1)

                    def gated(j, u):
                        dve.wait_ge(sem("m_silu"), j + 1)
                        dve.tensor_tensor(su_[:, u % 2, :], UB[u % 2][:], si[:, u % 2, :], ALU.mult)\
                           .then_inc(sem("m_uread"), 1)
                        dve.wait_ge(sem("m_uread"), j + 3)
                        dve.wait_ge(sem("m_c"), j + 1)
                        dve.wait_ge(sem("m_ilow"), j + 1)
                        dve.tensor_tensor(it[:, u % 2, :], CB[u % 2][:], su_[:, u % 2, :], ALU.mult)\
                           .then_inc(sem("m_cread"), 1)

                    gated(0, 0)
                    gated(1, 1)
                    with dve.Fori(0, 6) as g:
                        for u in range(1, 5):
                            gated(4 * g + u + 1, u + 1)
                    for i in range(25, MT - 1):
                        gated(i + 1, i + 1)
                    dve.wait_ge(sem("m_dn"), MT)
                    for i in range(2):
                        xs = x[:, 2 * i:2 * i + 2, :].rearrange("p t d -> p (t d)")
                        dve.tensor_tensor(xs, ACC[i][:], xs, ALU.add).then_inc(sem("residual"), 1)



def constants():
    half = R // 2
    inv = (np.float32(1.0) / np.power(np.float32(10000.0),
                                      np.arange(half, dtype=np.float32) / np.float32(half))).astype(np.float32)
    ang = (np.arange(SK, dtype=np.float32)[:, None] * inv).astype(np.float32).T
    cos = np.ones((P, SK), np.float32)
    sin = np.zeros((P, SK), np.float32)
    cos[KVC:KVC + half] = cos[KVC + half:] = np.cos(ang)
    sin[KVC:KVC + half] = -np.sin(ang)
    sin[KVC + half:] = np.sin(ang)
    rows = np.minimum(np.arange(MT * P) // IM, E)
    return {
        "ident": np.eye(P, dtype=np.float32),
        "kidx": np.broadcast_to(np.arange(SK, dtype=np.float32), (P, SK)).copy(),
        "cos": cos, "sin": sin,
        "owner": (np.arange(EG)[:, None] == rows[None, :]).astype(np.float16),
        "before": np.broadcast_to((np.arange(E)[None, :] < np.arange(E)[:, None]).astype(np.float32)
                                  .reshape(1, E * E), (P, E * E)).copy(),
    }


def kernel(**inputs):
    import concourse.bacc as _bacc
    from concourse.bass_utils import run_bass_kernel_spmd as _run

    nc = _bacc.Bacc("TRN2", target_bir_lowering=False, num_devices=1)
    arrays, aps = {}, {}
    for name, v in [*inputs.items(), *constants().items()]:
        v = np.ascontiguousarray(v)
        arrays[f"in_{name}"] = v
        aps[name] = nc.dram_tensor(f"in_{name}", v.shape, mybir.dt.from_np(v.dtype), kind="ExternalInput").ap()
    aps["out"] = nc.dram_tensor("out_0", (NB, SQ, D), F32, kind="ExternalOutput").ap()
    build(nc, aps)
    r = _run(nc, [arrays], core_ids=[0])
    return r.results[0]["out_0"]
```
